# Optimizing a Trainium2 kernel written in Bass

```python
import numpy as np
import jax
import jax.numpy as jnp

def _softmax(x, axis=-1):
    return jax.nn.softmax(x, axis=axis)
def _gelu(x):
    return jax.nn.gelu(x, approximate=True)
def _silu(x):
    return jax.nn.silu(x)
def _sigmoid(x):
    return jax.nn.sigmoid(x)
def _layernorm(x, axis=-1, eps=1e-5):
    m = jnp.mean(x, axis=axis, keepdims=True)
    v = jnp.var(x, axis=axis, keepdims=True)
    return (x - m) / jnp.sqrt(v + eps)
def _scatter_add(tgt, idx, src, axis=0):
    return tgt.at[idx].add(src)
def _segment_sum(src, seg, n):
    return jax.ops.segment_sum(src, seg, n)

kernel_name = 'mk_adj_preln_d4_adj_64_f27973'

def setup_inputs(seed: int = 0):
    np.random.seed(seed)
    _w = jnp.asarray
    def _rec_inputs():
        import jax
        import jax.numpy as jnp
        _gk = jax.random.key(seed)
        x = -0.000929 + 1 * jax.random.normal(jax.random.fold_in(_gk, 1), (4096, 64), jnp.float32)
        _a = jax.random.bernoulli(jax.random.fold_in(_gk, 2), 0.00195312, (4096, 4096))
        _a = jnp.logical_or(_a, jnp.swapaxes(_a, -1, -2))
        _a = jnp.logical_or(_a, jnp.eye(4096, dtype=bool))
        _af = _a.astype(jnp.float32)
        _af = _af * jax.random.uniform(jax.random.fold_in(_gk, 3), (4096, 4096), jnp.float32, 0.05, 1)
        adj = _af
        return x, adj
    x, adj = _rec_inputs()
    def _L0_gnn_setup():
        import jax, jax.numpy as jnp
        import numpy as np
        N = 16384
        IN_DIM = 64
        OUT_DIM = 64
        key = jax.random.key(seed)
        k1, k2, k3, k4 = jax.random.split(key, 4)
        x = jax.random.normal(k1, (N, IN_DIM), dtype=jnp.float32)
        adj = jax.random.uniform(k2, (N, N), dtype=jnp.float32)
        bound = 1.0 / np.sqrt(IN_DIM)
        W = jax.random.uniform(k3, (OUT_DIM, IN_DIM), dtype=jnp.float32, minval=-bound, maxval=bound)
        b = jax.random.uniform(k4, (OUT_DIM,), dtype=jnp.float32, minval=-bound, maxval=bound)
        return {'x': x, 'adj': adj, 'W': W, 'b': b}
    _L0_gnn_all = _L0_gnn_setup()
    _L0_gnn_in = {k: v for k, v in _L0_gnn_all.items() if k in ('W', 'b', )}
    del _L0_gnn_all

    def _L1_gnn_setup():
        import jax, jax.numpy as jnp
        import numpy as np
        import math
        N = 12288
        D = 64
        SCALE0 = math.log(10.0)

        def lorentz_linear(x, W, b, scale):
            h = x @ W.T + b
            time = jax.nn.sigmoid(h[:, :1]) * jnp.exp(scale) + 1.1
            xn = h[:, 1:]
            sq = jnp.clip(jnp.sum(xn * xn, axis=-1, keepdims=True), 1e-08, None)
            s = (time * time - 1.0) / sq
            return jnp.concatenate([time, xn * jnp.sqrt(s)], axis=-1)
        key = jax.random.key(seed)
        ks = jax.random.split(key, 8)
        stdv = 1.0 / math.sqrt(D)
        x = jax.random.normal(ks[0], (N, D), dtype=jnp.float32)
        adj = (jax.random.uniform(ks[1], (N, N)) < 0.002).astype(jnp.float32)
        W = jax.random.uniform(ks[2], (D, D), minval=-stdv, maxval=stdv, dtype=jnp.float32)
        Wq = jax.random.uniform(ks[3], (D, D), minval=-stdv, maxval=stdv, dtype=jnp.float32)
        Wk = jax.random.uniform(ks[4], (D, D), minval=-stdv, maxval=stdv, dtype=jnp.float32)
        z = jnp.zeros((D,), dtype=jnp.float32)
        sc = jnp.asarray(SCALE0, dtype=jnp.float32)
        return {'x': x, 'adj': adj, 'W': W, 'b': z, 'scale': sc, 'Wq': Wq, 'bq': z, 'scale_q': sc, 'Wk': Wk, 'bk': z, 'scale_k': sc, 'att_bias': jnp.asarray(20.0, dtype=jnp.float32), 'att_scale': jnp.asarray(math.sqrt(D), dtype=jnp.float32)}
    _L1_gnn_all = _L1_gnn_setup()
    _L1_gnn_in = {k: v for k, v in _L1_gnn_all.items() if k in ('W', 'b', 'scale', 'Wq', 'bq', 'scale_q', 'Wk', 'bk', 'scale_k', 'att_bias', 'att_scale', )}
    del _L1_gnn_all

    def _L2_gnn_setup():
        import jax, jax.numpy as jnp
        import numpy as np
        CURV = 1.0
        MIN_NORM = 1e-15
        TANH_CLIP = 1.0 - 1e-05

        def _mobius_add(x, y, c):
            x2 = jnp.sum(x * x, axis=-1, keepdims=True)
            y2 = jnp.sum(y * y, axis=-1, keepdims=True)
            xy = jnp.sum(x * y, axis=-1, keepdims=True)
            num = (1.0 + 2.0 * c * xy + c * y2) * x + (1.0 - c * x2) * y
            den = 1.0 + 2.0 * c * xy + c ** 2 * x2 * y2
            return num / jnp.maximum(den, MIN_NORM)

        def _logmap(x, y, c):
            sub = _mobius_add(-x, y, c)
            sub_norm = jnp.maximum(jnp.linalg.norm(sub, axis=-1, keepdims=True), MIN_NORM)
            x2 = jnp.sum(x * x, axis=-1, keepdims=True)
            lam_x = 2.0 / jnp.maximum(1.0 - c * x2, MIN_NORM)
            sqrt_c = jnp.sqrt(c)
            arg = jnp.clip(sqrt_c * sub_norm, 0.0, TANH_CLIP)
            return 2.0 / (sqrt_c * lam_x) * jnp.arctanh(arg) * sub / sub_norm

        def _expmap(x, v, c):
            v_norm = jnp.maximum(jnp.linalg.norm(v, axis=-1, keepdims=True), MIN_NORM)
            x2 = jnp.sum(x * x, axis=-1, keepdims=True)
            lam_x = 2.0 / jnp.maximum(1.0 - c * x2, MIN_NORM)
            sqrt_c = jnp.sqrt(c)
            second = jnp.tanh(sqrt_c * lam_x * v_norm / 2.0) * v / (sqrt_c * v_norm)
            return _mobius_add(x, second, c)
        key = jax.random.key(seed)
        k1, k2, k3 = jax.random.split(key, 3)
        N, C_IN, C_OUT = (1536, 64, 64)
        x = jax.random.normal(k1, (N, C_IN), dtype=jnp.float32) * 0.03
        adj = (jax.random.uniform(k2, (N, N)) < 0.02).astype(jnp.float32)
        bound = 1.0 / np.sqrt(C_IN)
        weight = jax.random.uniform(k3, (C_IN, C_OUT), dtype=jnp.float32, minval=-bound, maxval=bound)
        bias = jnp.zeros((C_OUT,), dtype=jnp.float32)
        return {'x': x, 'adj': adj, 'weight': weight, 'bias': bias}
    _L2_gnn_all = _L2_gnn_setup()
    _L2_gnn_in = {k: v for k, v in _L2_gnn_all.items() if k in ('weight', 'bias', )}
    del _L2_gnn_all

    def _L3_gnn_setup():
        import jax, jax.numpy as jnp
        import numpy as np
        N, D_IN, D_OUT = (8192, 64, 64)
        MAX_NEIGH = 100
        DECAY = 0.5
        key = jax.random.key(seed)
        k1, k2, k3, k4 = jax.random.split(key, 4)
        stdv = 1.0 / np.sqrt(D_OUT)
        inputs = {'input': jax.random.normal(k1, (N, D_IN), dtype=jnp.float32), 'adj': jax.random.randint(k2, (N, N), 0, 2).astype(jnp.float32), 'weight': jax.random.uniform(k3, (D_IN, D_OUT), minval=-stdv, maxval=stdv, dtype=jnp.float32), 'bias': jax.random.uniform(k4, (D_OUT,), minval=-stdv, maxval=stdv, dtype=jnp.float32)}
        return inputs
    _L3_gnn_all = _L3_gnn_setup()
    _L3_gnn_in = {k: v for k, v in _L3_gnn_all.items() if k in ('weight', 'bias', )}
    del _L3_gnn_all

    return {
        "x": x,
        "adj": adj,
        "L0_gnn_W": _L0_gnn_in["W"],
        "L0_gnn_b": _L0_gnn_in["b"],
        "L1_gnn_W": _L1_gnn_in["W"],
        "L1_gnn_b": _L1_gnn_in["b"],
        "L1_gnn_scale": _L1_gnn_in["scale"],
        "L1_gnn_Wq": _L1_gnn_in["Wq"],
        "L1_gnn_bq": _L1_gnn_in["bq"],
        "L1_gnn_scale_q": _L1_gnn_in["scale_q"],
        "L1_gnn_Wk": _L1_gnn_in["Wk"],
        "L1_gnn_bk": _L1_gnn_in["bk"],
        "L1_gnn_scale_k": _L1_gnn_in["scale_k"],
        "L1_gnn_att_bias": _L1_gnn_in["att_bias"],
        "L1_gnn_att_scale": _L1_gnn_in["att_scale"],
        "L2_gnn_weight": _L2_gnn_in["weight"],
        "L2_gnn_bias": _L2_gnn_in["bias"],
        "L3_gnn_weight": _L3_gnn_in["weight"],
        "L3_gnn_bias": _L3_gnn_in["bias"],
    }

def reference(x, adj, L0_gnn_W, L0_gnn_b, L1_gnn_W, L1_gnn_b, L1_gnn_scale, L1_gnn_Wq, L1_gnn_bq, L1_gnn_scale_q, L1_gnn_Wk, L1_gnn_bk, L1_gnn_scale_k, L1_gnn_att_bias, L1_gnn_att_scale, L2_gnn_weight, L2_gnn_bias, L3_gnn_weight, L3_gnn_bias):
    import jax
    import jax.numpy as jnp
    def _L0_gnn_ref(x, adj, W, b):
        import jax, jax.numpy as jnp
        import numpy as np
        N = 16384
        IN_DIM = 64
        OUT_DIM = 64
        h = adj @ x
        h = h @ W.T + b
        return jax.nn.relu(h)

    def _L1_gnn_ref(x, adj, W, b, scale, Wq, bq, scale_q, Wk, bk, scale_k, att_bias, att_scale):
        import jax, jax.numpy as jnp
        import numpy as np
        import math
        N = 12288
        D = 64
        SCALE0 = math.log(10.0)

        def lorentz_linear(x, W, b, scale):
            h = x @ W.T + b
            time = jax.nn.sigmoid(h[:, :1]) * jnp.exp(scale) + 1.1
            xn = h[:, 1:]
            sq = jnp.clip(jnp.sum(xn * xn, axis=-1, keepdims=True), 1e-08, None)
            s = (time * time - 1.0) / sq
            return jnp.concatenate([time, xn * jnp.sqrt(s)], axis=-1)
        h = lorentz_linear(x, W, b, scale)
        q = lorentz_linear(h, Wq, bq, scale_q)
        k = lorentz_linear(h, Wk, bk, scale_k)
        qm = jnp.concatenate([-q[:, :1], q[:, 1:]], axis=-1)
        att = 2.0 + 2.0 * (qm @ k.T)
        att = jax.nn.sigmoid(att / att_scale + att_bias)
        att = adj * att
        support = att @ h
        inner = -support[:, :1] ** 2 + jnp.sum(support[:, 1:] ** 2, axis=-1, keepdims=True)
        denorm = jnp.sqrt(jnp.clip(jnp.abs(-inner), 1e-08, None))
        return support / denorm

    def _L2_gnn_ref(x, adj, weight, bias):
        import jax, jax.numpy as jnp
        import numpy as np
        CURV = 1.0
        MIN_NORM = 1e-15
        TANH_CLIP = 1.0 - 1e-05

        def _mobius_add(x, y, c):
            x2 = jnp.sum(x * x, axis=-1, keepdims=True)
            y2 = jnp.sum(y * y, axis=-1, keepdims=True)
            xy = jnp.sum(x * y, axis=-1, keepdims=True)
            num = (1.0 + 2.0 * c * xy + c * y2) * x + (1.0 - c * x2) * y
            den = 1.0 + 2.0 * c * xy + c ** 2 * x2 * y2
            return num / jnp.maximum(den, MIN_NORM)

        def _logmap(x, y, c):
            sub = _mobius_add(-x, y, c)
            sub_norm = jnp.maximum(jnp.linalg.norm(sub, axis=-1, keepdims=True), MIN_NORM)
            x2 = jnp.sum(x * x, axis=-1, keepdims=True)
            lam_x = 2.0 / jnp.maximum(1.0 - c * x2, MIN_NORM)
            sqrt_c = jnp.sqrt(c)
            arg = jnp.clip(sqrt_c * sub_norm, 0.0, TANH_CLIP)
            return 2.0 / (sqrt_c * lam_x) * jnp.arctanh(arg) * sub / sub_norm

        def _expmap(x, v, c):
            v_norm = jnp.maximum(jnp.linalg.norm(v, axis=-1, keepdims=True), MIN_NORM)
            x2 = jnp.sum(x * x, axis=-1, keepdims=True)
            lam_x = 2.0 / jnp.maximum(1.0 - c * x2, MIN_NORM)
            sqrt_c = jnp.sqrt(c)
            second = jnp.tanh(sqrt_c * lam_x * v_norm / 2.0) * v / (sqrt_c * v_norm)
            return _mobius_add(x, second, c)
        c = CURV
        deg = jnp.maximum(adj.sum(axis=1, keepdims=True), 1e-08)
        w = adj / deg
        log_ij = _logmap(x[:, None, :], x[None, :, :], c)
        agg = jnp.einsum('ij,ijc->ic', w, log_ij)
        transformed = agg @ weight + bias
        origin = jnp.zeros_like(transformed)
        return _expmap(origin, transformed, c)

    def _L3_gnn_ref(input, adj, weight, bias):
        import jax, jax.numpy as jnp
        import numpy as np
        N, D_IN, D_OUT = (8192, 64, 64)
        MAX_NEIGH = 100
        DECAY = 0.5
        support = input @ weight
        mask = (adj != 0).astype(support.dtype)
        rank = jnp.cumsum(mask, axis=1)
        deg = rank[:, -1:]
        k = jnp.minimum(deg, float(MAX_NEIGH))
        pos = rank - (deg - k)
        w = mask * jnp.where(pos > 0, DECAY ** (k - pos), 0.0)
        out = w @ support + bias
        return out

    h = jnp.maximum(_layernorm(x, axis=-1), 0.0)
    x = x + _L0_gnn_ref(h, adj, L0_gnn_W, L0_gnn_b)
    h = jnp.maximum(_layernorm(x, axis=-1), 0.0)
    x = x + _L1_gnn_ref(h, adj, L1_gnn_W, L1_gnn_b, L1_gnn_scale, L1_gnn_Wq, L1_gnn_bq, L1_gnn_scale_q, L1_gnn_Wk, L1_gnn_bk, L1_gnn_scale_k, L1_gnn_att_bias, L1_gnn_att_scale)
    h = jnp.maximum(_layernorm(x, axis=-1), 0.0)
    x = x + _L2_gnn_ref(h, adj, L2_gnn_weight, L2_gnn_bias)
    h = jnp.maximum(_layernorm(x, axis=-1), 0.0)
    x = x + _L3_gnn_ref(h, adj, L3_gnn_weight, L3_gnn_bias)
    return x


_drawn_inputs = setup_inputs


def setup_inputs(seed=0):
    import zlib

    import numpy as np

    out = dict(_drawn_inputs(seed))
    spreads = {'L1_gnn_b': (0.0, 0.33),
     'L1_gnn_bq': (0.0, 0.8),
     'L1_gnn_bk': (0.0, 0.8),
     'L2_gnn_bias': (0.0, 0.1)}
    factors = {'L1_gnn_Wq': 8.0, 'L1_gnn_Wk': 8.0}
    for name, (base, spread) in spreads.items():
        noise = np.random.default_rng([zlib.crc32(name.encode()), seed]).standard_normal(out[name].shape)
        drawn = base * np.exp(spread * noise) if base else spread * noise
        out[name] = jnp.asarray(drawn.astype(out[name].dtype))
    for name, factor in factors.items():
        out[name] = (out[name] * factor).astype(out[name].dtype)
    return out
```

```python
import concourse.bass as bass
from concourse import mybir
from contextlib import ExitStack

F32 = mybir.dt.float32
BF16 = mybir.dt.bfloat16
F16 = mybir.dt.float16
I16 = mybir.dt.int16
ALU = mybir.AluOpType
ACT = mybir.ActivationFunctionType
AX = mybir.AxisListType

N = 4096
D = 64
P = 128
T = N // P
BANK = 512
EPS = 1e-5
UNIT = 2 * BANK
HALF = N // 2
RING = 4
SLOT = 2048

CLIP = 1.0 - 1e-5
TAU_MAX = 12.206062
MIN_NORM = 1e-15
BALL_FLOOR = 1e-6
KAPPA = 2.0 ** 39
ROWS = D + 3
QUART = N // 4
ROT = 3
RING2 = 6

HALVES_TOP = 1024.0

MAX_NEIGH = 100
BF_STEP = 128.0
BF_BASE = MAX_NEIGH * BF_STEP
W_SCALE = 2.0 ** (127 - MAX_NEIGH)


def graph_layers(nc, x, adj_t, w0_t, b0, w1_t, b1, wq_t, bq, wk_t, bk, scalars, w2, b2, w3, b3, out):
    ctx = ExitStack()
    with ctx:
        def sb(name, shape, dt=F32):
            return ctx.enter_context(nc.sbuf_tensor(name, shape, dt))

        named = {}

        def sem(name):
            if name not in named:
                named[name] = ctx.enter_context(nc.semaphore(name))
            return named[name]

        ring = sb("ring", [P, RING, HALF])
        ring2 = ring[:, :, :].rearrange("p r (u n) -> p (r u) n", u=2)
        X = sb("X", [P, T, D])
        H = sb("H", [P, T, D])
        Y = sb("Y", [P, T, ROWS])
        TA = sb("TA", [P, N])
        TB = sb("TB", [P, N])
        work = sb("work", [P, 12 * SLOT])
        PS = ctx.enter_context(nc.psum_tensor("PS", [P, 8 * BANK], F32))

        def slot(k, n=1):
            return work[:, k * SLOT:(k + n) * SLOT]

        def nodes(ap):
            return ap.rearrange("p (t c) -> p t c", t=T)

        ident = sb("ident", [P, P])
        identh = sb("identh", [P, P], F16)
        wbd = {k: sb(f"wbd_{k}", [P, P]) for k in ("l0", "l1", "q", "k", "w2", "w3")}
        bias = {k: sb(f"bias_{k}", [P, D]) for k in ("l0", "l1", "q", "k", "w2", "w3")}
        scal = sb("scal", [P, 5])
        esc = sb("esc", [P, 3])
        att_sc = sb("att_sc", [P, 3])
        top, inv_top = sb("top", [P, 3]), sb("inv_top", [P, 3])
        deg = sb("deg", [P, T])
        zeros = sb("zeros", [P, BANK], BF16)
        ones = sb("ones", [P, 1])
        st = [sb(f"st{k}", [P, T]) for k in range(10)]
        ystage = sb("ystage", [P, 4, D + 1])
        zstage = sb("zstage", [P, ROT, P])
        sstage = sb("sstage", [P, 4, 3 * D], BF16)
        kmask = sb("kmask", [P, 1])
        tri_above = sb("tri_above", [P, P], BF16)
        tri_rest = sb("tri_rest", [P, P], BF16)

        cen = nodes(slot(10))
        sqr = nodes(slot(11))

        def bcast_t(v):
            return v.unsqueeze(2).broadcast_to([P, T, D])

        def bcast_c(v):
            return v.unsqueeze(1).broadcast_to([P, T, D])

        def banks(a, b):
            return PS[:, a * BANK:b * BANK]

        q_hh, q_ll, k_hl = (slot(k).bitcast(F16) for k in range(3))
        HL = nodes(slot(5))
        HBq, HBk = nodes(slot(6)), nodes(slot(7))
        Q4 = slot(8, 2).bitcast(F16).rearrange("p (t s c) -> p t s c", t=T, s=4)
        K2 = slot(10).bitcast(F16).rearrange("p (t s c) -> p t s c", t=T, s=2)
        att = slot(6).rearrange("p (k n) -> p k n", k=2)
        prob = slot(7, 2).rearrange("p (k n) -> p k n", k=4)
        def trio(first):
            return work[:, first * UNIT:(first + ROT) * UNIT].rearrange("p (k n) -> p k n", k=ROT)
        sqz, rin, sum_, rad, wgt = (trio(ROT * k) for k in range(5))
        kap_l = work[:, 15 * UNIT:17 * UNIT].bitcast(BF16)
        kap_r = work[:, 17 * UNIT:19 * UNIT].bitcast(BF16)
        zi = work[:, 0:T * ROWS].rearrange("p (t c) -> p t c", t=T)
        mask = slot(0, 2).bitcast(BF16).rearrange("p (k n) -> p k n", k=4)
        pw = slot(2, 2).bitcast(BF16).rearrange("p (k n) -> p k n", k=4)
        S3 = work[:, 4 * SLOT:4 * SLOT + 3 * SLOT // 2].bitcast(BF16).rearrange("p (t s c) -> p t s c", t=T, s=3)

        adj_tiles = adj_t.rearrange("(t p) n -> t p n", p=P)
        x_nodes = x.rearrange("(t p) c -> p t c", p=P)
        out_nodes = out.rearrange("(t p) c -> p t c", p=P)

        def unit(Q, j, back):
            if isinstance(j, tuple):
                it, k = j
                n0 = Q * T + k - back
                return (Q, it * RING2 + (k - back), n0 % RING2, it + n0 // RING2)
            n = Q * T + j - back
            return (n // T, n % T, n % RING2, n // RING2) if 0 <= n < 4 * T else None

        def walk2(eng, step):
            for Q in range(4):
                for j in range(RING2):
                    step(Q, j)
                with eng.Fori(1, T // RING2) as it:
                    for k in range(RING2):
                        step(Q, (it, k))
                for j in range(T // RING2 * RING2, T):
                    step(Q, j)
            for j in range(DRAIN):
                step(4, j)

        DRAIN = 6

        def count(u):
            return u[0] * T + u[1] + 1

        def prior(u, rot):
            return None if isinstance(u[1], int) and count(u) <= rot else count(u) - rot

        def loads2(u):
            return u[3] * 16 + 16

        def agg2_col(t):
            return (t // 7) * BANK + (t % 7) * (D + 1)

        def u1(u):
            return slice(u[1], u[1] + 1) if isinstance(u[1], int) else bass.ts(u[1], 1)

        block = ctx.enter_context(nc.Block())

        @block.sync
        def _(sp):
            sp.dma_start(X[:, :, :], x_nodes).then_inc(sem("x_loaded"), 16)

            def tile(g):
                if isinstance(g, int):
                    return adj_tiles[g // 2, :, (g % 2) * HALF:(g % 2 + 1) * HALF]
                it, k = g
                return adj_tiles[it * (RING // 2) + k // 2, :, (k % 2) * HALF:(k % 2 + 1) * HALF]

            def load(layer, k, src):
                sp.dma_start(ring[:, k, :], src).then_inc(sem(f"adj{layer}_loaded{k}"), 16)

            for k in range(RING):
                load(0, k, tile(k))
            for wname, wsrc in (("l0", w0_t), ("l1", w1_t), ("q", wq_t), ("k", wk_t), ("w2", w2), ("w3", w3)):
                sp.wait_ge(sem("wbd_zeroed"), 6)
                for r in range(2):
                    sp.dma_start(wbd[wname][r * D:(r + 1) * D, r * D:(r + 1) * D], wsrc).then_inc(sem("weights_loaded"), 16)
            for bname, bsrc in (("l0", b0), ("l1", b1), ("q", bq), ("k", bk), ("w2", b2), ("w3", b3)):
                sp.dma_start(bias[bname][:, :], bsrc.partition_broadcast(P)).then_inc(sem("biases_loaded"), 16)
            sp.dma_start(scal[:, :], scalars.partition_broadcast(P)).then_inc(sem("biases_loaded"), 16)
            with sp.Fori(1, 2 * T // RING) as it:
                for k in range(RING):
                    sp.wait_ge(sem("agg0_done"), it * RING + (k - RING + 1))
                    sp.wait_ge(sem("deg_added"), it * RING + (k - RING + 1))
                    load(0, k, tile((it, k)))
            for k in range(RING):
                sp.wait_ge(sem("agg0_done"), 2 * T - RING + k + 1)
                sp.wait_ge(sem("deg_added"), 2 * T - RING + k + 1)
                load(1, k, tile(k))
            with sp.Fori(1, 2 * T // RING) as it:
                for k in range(RING):
                    sp.wait_ge(sem("prob_ready"), (it * RING + (k - RING + 1)) * 2)
                    load(1, k, tile((it, k)))
            sp.wait_ge(sem("prob_ready"), 4 * T)

            def load2(Q, j):
                u = unit(Q, j, 0)
                if u is None:
                    return
                if prior(u, RING2) is not None:
                    sp.wait_ge(sem("rad_ready"), prior(u, RING2))
                sp.dma_start(ring2[:, u[2], :], adj_tiles[u[1], :, Q * QUART:(Q + 1) * QUART])\
                  .then_inc(sem(f"adj2_loaded{u[2]}"), 16)
            walk2(sp, load2)
            sp.wait_ge(sem("rad_ready"), 4 * T)

            def load3(h, jt, k):
                sp.dma_start(ring[:, k, :], adj_tiles[jt, :, h * HALF:(h + 1) * HALF])\
                  .then_inc(sem(f"adj3_loaded{k}"), 16)
            for h in range(2):
                for k in range(RING):
                    if h:
                        sp.wait_ge(sem("mask_ready"), h * T + k - RING + 1)
                    load3(h, T - 1 - k, k)
                with sp.Fori(1, T // RING) as it:
                    for k in range(RING):
                        jt = it * (-RING) + (T - 1 - k)
                        sp.wait_ge(sem("mask_ready"), it * RING + (h * T + k - RING + 1))
                        load3(h, jt, k)
            sp.wait_ge(sem("result_ready"), 1)
            sp.dma_start(out_nodes, X[:, :, :]).then_inc(sem("stored"), 16)
            sp.wait_ge(sem("stored"), 16)

        @block.gpsimd
        def _(pool):
            chain = [0]

            def link(ins):
                chain[0] += 1
                ins.then_inc(sem("pool_chain"), 1)
                pool.wait_ge(sem("pool_chain"), chain[0])

            for w in wbd.values():
                nc.gpsimd.memset(w[:, :], 0.0).then_inc(sem("wbd_zeroed"), 1)
            nc.gpsimd.memset(zeros[:, :], 0.0).then_inc(sem("consts_ready"), 1)
            nc.gpsimd.memset(ones[:, :], 1.0).then_inc(sem("consts_ready"), 1)
            link(nc.gpsimd.memset(ident[:, :], 0.0))
            link(nc.gpsimd.affine_select(out=ident[:, :], in_=ident[:, :], compare_op=ALU.not_equal, fill=1.0,
                                         base=0, pattern=[[-1, P]], channel_multiplier=1))
            nc.gpsimd.tensor_copy(identh[:, :], ident[:, :]).then_inc(sem("consts_ready"), 1)
            link(nc.gpsimd.memset(kmask[:, :], 0.0))
            link(nc.gpsimd.affine_select(out=kmask[:, :], in_=kmask[:, :], compare_op=ALU.not_equal, fill=KAPPA,
                                         base=-(D + 1), pattern=[[0, 1]], channel_multiplier=1))
            nc.gpsimd.affine_select(out=kmask[:, :], in_=kmask[:, :], compare_op=ALU.not_equal, fill=-KAPPA,
                                    base=-(D + 2), pattern=[[0, 1]], channel_multiplier=1)\
              .then_inc(sem("consts_ready"), 1)
            link(nc.gpsimd.memset(tri_above[:, :], -BF_STEP))
            link(nc.gpsimd.affine_select(out=tri_above[:, :], in_=tri_above[:, :], compare_op=ALU.is_ge, fill=0.0,
                                         base=0, pattern=[[-1, P]], channel_multiplier=1))
            nc.gpsimd.affine_select(out=tri_above[:, :], in_=tri_above[:, :], compare_op=ALU.not_equal, fill=BF_BASE,
                                    base=0, pattern=[[-1, P]], channel_multiplier=1).then_inc(sem("consts_ready"), 1)
            link(nc.gpsimd.memset(tri_rest[:, :], -BF_STEP))
            link(nc.gpsimd.affine_select(out=tri_rest[:, :], in_=tri_rest[:, :], compare_op=ALU.is_ge, fill=0.0,
                                         base=0, pattern=[[1, P]], channel_multiplier=-1))
            nc.gpsimd.affine_select(out=tri_rest[:, :], in_=tri_rest[:, :], compare_op=ALU.not_equal,
                                    fill=-BF_STEP - BF_BASE, base=0, pattern=[[-1, P]], channel_multiplier=1)\
              .then_inc(sem("consts_ready"), 1)

            for layer, feats in ((0, H), (1, HL)):
                pool.wait_ge(sem(f"feats{layer}_ready"), 1)
                if layer:
                    pool.wait_ge(sem("agg0_done"), 2 * T)
                for k in range(2):
                    nc.gpsimd.tensor_copy(ystage[:, k, 0:D], feats[:, k, 0:D]).then_inc(sem(f"staged{layer}"), 1)
                with pool.Fori(1, T // 2) as it:
                    for k in range(2):
                        if layer == 0:
                            pool.wait_ge(sem("agg0_done"), it * 4 + (2 * k - 2))
                        else:
                            pool.wait_ge(sem("agg1_done"), it * 8 + (4 * k - 4))
                        nc.gpsimd.tensor_copy(ystage[:, k, 0:D], feats[:, it * 2 + k, 0:D])\
                          .then_inc(sem(f"staged{layer}"), 1)

            pool.wait_ge(sem("zl_out_a"), 1)
            pool.wait_ge(sem("zl_out_v"), 1)
            pool.wait_ge(sem("agg1_done"), 4 * T)

            def step2(Q, j):
                for u in ([unit(0, 0, 0)] if (Q, j) == (0, 0) else []) + [unit(Q, j, -1)]:
                    if u is None:
                        continue
                    if prior(u, ROT) is not None:
                        pool.wait_ge(sem("z_ready"), prior(u, ROT))
                    nc.gpsimd.tensor_copy(zstage[0:ROWS, u[2] % ROT, :], TA[0:ROWS, bass.ts(u[1], P)])\
                      .then_inc(sem("zstaged"), 1)
                u = unit(Q, j, 2)
                if u:
                    k = u[2] % ROT
                    pool.wait_ge(sem("rin_ready"), count(u))
                    pool.wait_ge(sem(f"adj2_loaded{u[2]}"), loads2(u))
                    if prior(u, ROT) is not None:
                        pool.wait_ge(sem("wgt_ready"), prior(u, ROT))
                    nc.gpsimd.tensor_tensor(rad[:, k, :], rin[:, k, :], ring2[:, u[2], :], ALU.mult)\
                      .then_inc(sem("rad_ready"), 1)
                    if prior(u, ROT) is not None:
                        pool.wait_ge(sem("agg2_done"), prior(u, ROT))
                    nc.gpsimd.tensor_copy(ystage[:, k, :], Y[:, u[1], 0:D + 1]).then_inc(sem("ystaged"), 1)
            walk2(pool, step2)

            pool.wait_ge(sem("parts3_ready"), 1)
            for h in range(2):
                for k in range(4):
                    if h:
                        pool.wait_ge(sem("agg3_done"), 2 * (h * T + k - 4 + 1))
                    nc.gpsimd.tensor_copy(sstage[:, k, :].rearrange("p (s c) -> p s c", s=3), S3[:, T - 1 - k, :, :])\
                      .then_inc(sem("staged3"), 1)
                with pool.Fori(1, T // 4) as it:
                    for k in range(4):
                        jt = it * (-4) + (T - 1 - k)
                        pool.wait_ge(sem("agg3_done"), it * 8 + 2 * (h * T + k - 4 + 1))
                        nc.gpsimd.tensor_copy(sstage[:, k, :].rearrange("p (s c) -> p s c", s=3), S3[:, jt, :, :]).then_inc(sem("staged3"), 1)

        @block.tensor
        def _(pe):
            mm = nc.tensor.matmul

            def clear(first, last, signal=None):
                for b in range(first, last):
                    ins = mm(PS[:, b * BANK:(b + 1) * BANK], zeros[:, 0:P], zeros[:, :], start=True, stop=True)
                return ins

            def add(out_ap, lhsT, rhs):
                return mm(out_ap, lhsT, rhs, start=False, stop=True, skip_group_check=True)

            def to_nodes(rhs, src, dst):
                for a in range(4):
                    for b in range(4):
                        o = PS[:, dst + a * BANK:dst + (a + 1) * BANK].rearrange("p (r b c) -> p b r c", r=2, b=4)
                        ins = mm(o[:, b, :, :], src[:, a * BANK + b * P:a * BANK + (b + 1) * P], rhs,
                                 start=True, stop=True)
                return ins

            def flip(src, dst):
                for u in range(T // 2):
                    ins = nc.tensor.transpose(PS[:, dst + u * P:dst + (u + 1) * P], src[:, 2 * u:2 * u + 2, :], ident[:, :])
                return ins

            def linear(w, dst):
                for u in range(T // 2):
                    ins = mm(PS[:, dst + u * P:dst + (u + 1) * P], TA[:, u * P:(u + 1) * P], w, start=True, stop=True)
                return ins

            def copied_out(name, n=1):
                pe.wait_ge(sem(f"{name}_a"), n)
                pe.wait_ge(sem(f"{name}_v"), n)

            pe.wait_ge(sem("consts_ready"), 6)
            clear(0, 4)

            def tile0(k, loaded, staged):
                pe.wait_ge(sem("staged0"), staged)
                for half in range(2):
                    s = 2 * k + half
                    pe.wait_ge(sem(f"adj0_loaded{s}"), loaded)
                    for c in range(4):
                        cc = 4 * half + c
                        ins = add(PS[D * (cc % 2):D * (cc % 2) + D, (cc // 2) * BANK:(cc // 2 + 1) * BANK],
                                  ystage[:, k, 0:D], ring[:, s, c * BANK:(c + 1) * BANK])
                    ins.then_inc(sem("agg0_done"), 1)
            with pe.Fori(0, T // 2) as it:
                for k in range(2):
                    tile0(k, it * 16 + 16, it * 2 + (k + 1))
            copied_out("sums_out0")
            pe.wait_ge(sem("weights_loaded"), 16 * 12)
            to_nodes(wbd["l0"][:, :], TA, 4 * BANK).then_inc(sem("z0_ready"), 1)

            pe.wait_ge(sem("deg_added"), 2 * T)
            for t in range(T):
                ins = mm(PS[:, t:t + 1], TB[:, t * P:(t + 1) * P], ones[:, :], start=True, stop=True)
            ins.then_inc(sem("deg_summed"), 1)

            pe.wait_ge(sem("feats_ready_l1"), 1)
            pe.wait_ge(sem("deg_out"), 1)
            flip(H, 0).then_inc(sem("hT_ready"), 1)
            copied_out("hT_out")
            linear(wbd["l1"][:, :], 4 * BANK).then_inc(sem("lin_h"), 1)
            pe.wait_ge(sem("feats1_ready"), 1)
            flip(HL, 0).then_inc(sem("hlT_ready"), 1)
            copied_out("hlT_out")
            linear(wbd["q"][:, :], 4 * BANK).then_inc(sem("lin_q"), 1)
            linear(wbd["k"][:, :], 0).then_inc(sem("lin_k"), 1)

            pairs = [(Q4, 0, 4), (Q4, 2, 0), (K2, 0, 4)]
            for n, (src, part, b) in enumerate(pairs):
                pe.wait_ge(sem("halves_ready"), 1 + n // 2)
                if n >= 2:
                    copied_out("pair_out", n - 1)
                o = banks(b, b + 4).bitcast(F16)
                for t in range(T):
                    ins = nc.tensor.transpose(o[:, t * P:(t + 1) * P],
                                              src[:, t, part:part + 2, :], identh[:, :])
                ins.then_inc(sem("pair_ready"), 1)
            copied_out("pair_out", 3)
            clear(0, 4)

            def scores(k, u, n, first, jt):
                b = 4 + 2 * (u % 2)
                if not first:
                    pe.wait_ge(sem("att_ready"), n - 1)
                for c in range(2):
                    i0 = u * UNIT + c * BANK
                    o = PS[:, (b + c) * BANK:(b + c + 1) * BANK]
                    mm(o, k_hl[:, bass.ts(jt, P)], q_hh[:, i0:i0 + BANK], start=True, stop=False)
                    ins = mm(o, k_hl[:, bass.ts(jt, P)], q_ll[:, i0:i0 + BANK], start=False, stop=True)
                ins.then_inc(sem("scores_ready"), 1)

            def gather1(k, u, n):
                pe.wait_ge(sem("prob_ready"), n + 1)
                for c in range(2):
                    ins = add(PS[D * c:D * c + D, u * BANK:(u + 1) * BANK], ystage[:, k, 0:D],
                              prob[:, u, c * BANK:(c + 1) * BANK])
                ins.then_inc(sem("agg1_done"), 1)

            def turn1(it, peeled):
                for k in range(2):
                    jt = it * 2 + k
                    pe.wait_ge(sem("staged1"), it * 2 + (k + 1))
                    for u in range(4):
                        n = it * 8 + (4 * k + u)
                        scores(k, u, n, peeled and k == 0 and u < 2, jt)
                        if not (peeled and k == 0 and u < 2):
                            back = 4 * k + u - 2
                            gather1((back // 4) % 2, back % 4, it * 8 + back)
            turn1(0, True)
            with pe.Fori(1, T // 2) as it:
                turn1(it, False)
            for u in (2, 3):
                gather1(1, u, 4 * (T - 1) + u)
            copied_out("sums_out1")
            to_nodes(ident[:, :], TA, 4 * BANK).then_inc(sem("support_ready"), 1)

            pe.wait_ge(sem("zl_nodes_ready"), 1)
            for t in range(T):
                ins = nc.tensor.transpose(PS[0:ROWS, t * P:(t + 1) * P], Y[:, t, :], ident[:, :])
                if t == T // 2 - 1 or t == T - 1:
                    ins.then_inc(sem("zl_flipped"), 1)
            pe.wait_ge(sem("zr_nodes_ready"), 1)
            for t in range(T):
                if t == 0:
                    pe.wait_ge(sem("zl_out_a"), 1)
                if t == T // 2:
                    pe.wait_ge(sem("zl_out_v"), 1)
                ins = nc.tensor.transpose(PS[0:ROWS, t * P:(t + 1) * P], zi[:, t, :], ident[:, :])
                if t == T // 2 - 1 or t == T - 1:
                    ins.then_inc(sem("zr_flipped"), 1)
            copied_out("zr_out")
            pe.wait_ge(sem("kap_rows_ready"), 2)

            def z_bank(k, c):
                return PS[:, (2 + 2 * k + c) * BANK:(3 + 2 * k + c) * BANK]

            def step2(Q, j):
                u = unit(Q, j, 0)
                if u:
                    k = u[2] % ROT
                    pe.wait_ge(sem("zstaged"), count(u))
                    if prior(u, ROT) is not None:
                        pe.wait_ge(sem("sum_ready"), prior(u, ROT))
                    for c in range(2):
                        ins = mm(z_bank(k, c), zstage[0:ROWS, k, :], TB[0:ROWS, Q * QUART + c * BANK:Q * QUART + (c + 1) * BANK],
                                 start=True, stop=True)
                    ins.then_inc(sem("z_ready"), 1)
                u = unit(Q, j, 1)
                if u:
                    k = u[2] % ROT
                    pe.wait_ge(sem("sqz_ready"), count(u))
                    for c in range(2):
                        ins = add(z_bank(k, c), kap_l[0:ROWS, bass.ts(u[1], P)],
                                  kap_r[0:ROWS, u[0] * QUART + c * BANK:u[0] * QUART + (c + 1) * BANK])
                    ins.then_inc(sem("zk_ready"), 1)
                u = unit(Q, j, 4)
                if u:
                    k = u[2] % ROT
                    pe.wait_ge(sem("ystaged"), count(u))
                    pe.wait_ge(sem("wgt_ready"), count(u))
                    if isinstance(u[1], int) and u[1] == 0:
                        if u[0] > 0:
                            pe.wait_ge(sem("quarter_out"), u[0])
                        clear(0, 2)
                    for c in range(2):
                        ins = add(PS[0:D + 1, c * BANK:(c + 1) * BANK], ystage[:, k, :], wgt[:, k, c * BANK:(c + 1) * BANK])
                    ins.then_inc(sem("agg2_done"), 1)
            walk2(pe, step2)
            pe.wait_ge(sem("quarter_out"), 4)
            for t in range(T):
                ins = mm(PS[:, agg2_col(t):agg2_col(t) + D + 1], TB[0:D + 1, t * P:(t + 1) * P], ident[0:D + 1, 0:D + 1],
                         start=True, stop=True)
            ins.then_inc(sem("agg2_nodes"), 1)
            pe.wait_ge(sem("tan_ready"), 1)
            flip(cen, 0).then_inc(sem("tanT_ready"), 1)
            copied_out("tanT_out")
            linear(wbd["w2"][:, :], 4 * BANK).then_inc(sem("lin_w2"), 1)

            pe.wait_ge(sem("feats_ready_l3"), 1)
            flip(H, 0).then_inc(sem("h3T_ready"), 1)
            copied_out("h3T_out")
            linear(wbd["w3"][:, :], 4 * BANK).then_inc(sem("lin_w3"), 1)
            pe.wait_ge(sem("parts3_ready"), 1)

            def counts(k, u, lhsT):
                for c in range(2):
                    ins = add(PS[:, (2 * u + c) * BANK:(2 * u + c + 1) * BANK], lhsT,
                              mask[:, k, u * UNIT + c * BANK:u * UNIT + (c + 1) * BANK])
                return ins

            def gather3(h, k, u):
                b = 4 + 2 * h + u
                for part in range(3):
                    for c in range(2):
                        ins = add(PS[D * c:D * c + D, b * BANK:(b + 1) * BANK], sstage[:, k, part * D:(part + 1) * D],
                                  pw[:, k, u * UNIT + c * BANK:u * UNIT + (c + 1) * BANK])
                return ins

            def step3(h, s, k, first):
                for u in range(2):
                    if not first:
                        pe.wait_ge(sem("pw_ready"), s * 2 + (u - 1))
                        counts((k - 1) % 4, u, tri_rest[:, :])
                    pe.wait_ge(sem("mask_ready"), s + 1)
                    counts(k, u, tri_above[:, :]).then_inc(sem("counts_ready"), 1)
                    if not first:
                        pe.wait_ge(sem("staged3"), s)
                        gather3(h, (k - 1) % 4, u).then_inc(sem("agg3_done"), 1)

            for h in range(2):
                if h:
                    pe.wait_ge(sem("pw_ready"), 2 * T * h)
                clear(0, 4)
                clear(4 + 2 * h, 6 + 2 * h)
                for k in range(4):
                    step3(h, h * T + k, k, k == 0)
                with pe.Fori(1, T // 4) as it:
                    for k in range(4):
                        step3(h, it * 4 + (h * T + k), k, False)
                for u in range(2):
                    pe.wait_ge(sem("pw_ready"), 2 * T * (h + 1) - 1 + u)
                    pe.wait_ge(sem("staged3"), T * (h + 1))
                    gather3(h, 3, u).then_inc(sem("agg3_done"), 1)
            copied_out("sums_out3")
            to_nodes(ident[:, :], TA, 0).then_inc(sem("agg3_nodes"), 1)

        @block.scalar
        def _(act):
            def one(name, out_ap, in_ap, func, wait, **kw):
                act.wait_ge(sem(wait[0]), wait[1])
                nc.scalar.activation(out_ap, in_ap, func, **kw).then_inc(sem(name), 1)

            def norm(L):
                one(f"ln{L}_sq", sqr, cen, ACT.Square, (f"ln{L}_centred", 1))
                one(f"ln{L}_sd", st[2][:, :], st[1][:, :], ACT.Sqrt, (f"ln{L}_var", 1))

            def copy_out(name, dst, src, ready):
                one(f"{name}_a", dst, src, ACT.Copy, ready)

            one("scales_ready", esc[:, :], scal[:, 0:3], ACT.Exp, ("biases_loaded", 16 * 7))
            norm(0)
            copy_out("sums_out0", TA[:, 0:UNIT], PS[:, 0:UNIT], ("agg0_done", 2 * T))
            norm(1)
            copy_out("hT_out", TA[:, 0:UNIT], PS[:, 0:UNIT], ("hT_ready", 1))

            def lorentz(tag, hb):
                act.wait_ge(sem(f"{tag}_biased"), 1)
                nc.scalar.activation(sqr[:, :, 0:D - 1], hb[:, :, 1:D], ACT.Square).then_inc(sem(f"{tag}_sq"), 1)
                nc.scalar.activation(st[0][:, :], hb[:, :, 0], ACT.Sigmoid).then_inc(sem(f"{tag}_sig"), 1)
                one(f"{tag}_root", st[4][:, :], st[3][:, :], ACT.Sqrt, (f"{tag}_ratio", 1))
            lorentz("h", HBq)
            copy_out("hlT_out", TA[:, 0:UNIT], PS[:, 0:UNIT], ("hlT_ready", 1))
            lorentz("q", HBq)
            act.wait_ge(sem("q_done"), 1)
            lorentz("k", HBk)
            for n, dst in enumerate((q_hh, q_ll, k_hl)):
                src = banks(0 if n % 2 else 4, 4 if n % 2 else 8).bitcast(F16)
                copy_out("pair_out", dst[:, 0:HALF], src[:, 0:HALF], ("pair_ready", n + 1))

            act.wait_ge(sem("att_scale_ready"), 1)

            def sigm(u, n, first):
                act.wait_ge(sem("scores_ready"), n + 1)
                if not first:
                    act.wait_ge(sem("prob_ready"), n - 1)
                b = 4 + 2 * (u % 2)
                nc.scalar.activation(att[:, u % 2, :], PS[:, b * BANK:(b + 2) * BANK], ACT.Sigmoid,
                                     bias=att_sc[:, 2:3], scale=att_sc[:, 1:2]).then_inc(sem("att_ready"), 1)
            for u in range(4):
                sigm(u, u, u < 2)
            with act.Fori(1, T) as it:
                for u in range(4):
                    sigm(u, it * 4 + u, False)
            copy_out("sums_out1", TA[:, 0:UNIT], PS[:, 0:UNIT], ("agg1_done", 4 * T))
            one("sup_sq", sqr, banks(4, 8).rearrange("p (t c) -> p t c", t=T), ACT.Square, ("support_ready", 1))
            one("sup_root", st[2][:, :], st[1][:, :], ACT.Sqrt, ("sup_inner", 1))
            norm(2)

            one("y_sq", sqr, Y[:, :, 0:D], ACT.Square, ("feats2_ready", 1))
            copy_out("zl_out", TA[0:ROWS, 0:HALF], PS[0:ROWS, 0:HALF], ("zl_flipped", 1))
            copy_out("zr_out", TB[0:ROWS, 0:HALF], PS[0:ROWS, 0:HALF], ("zr_flipped", 1))
            act.wait_ge(sem("zr_flipped"), 2)
            act.wait_ge(sem("zl_out_a"), 1)
            one("kap_rows_ready", kap_l[0:ROWS, :], TA[0:ROWS, :], ACT.Copy, ("zl_out_v", 1))
            one("kap_rows_ready", kap_r[0:ROWS, :], TA[0:ROWS, :], ACT.Copy, ("zl_out_v", 1), scale=kmask[0:ROWS, 0:1])

            def step2(Q, j):
                u = unit(Q, j, 3)
                if u:
                    k = u[2] % ROT
                    act.wait_ge(sem("sum_ready"), count(u))
                    nc.scalar.activation(sum_[:, k, :], sum_[:, k, :], ACT.Ln, scale=st[5][:, u1(u)])\
                      .then_inc(sem("tau_ready"), 1)
                u = unit(Q, j, 1)
                if u:
                    k = u[2] % ROT
                    act.wait_ge(sem("rest_ready"), count(u))
                    if prior(u, ROT) is not None:
                        act.wait_ge(sem("rad_ready"), prior(u, ROT))
                        act.wait_ge(sem("root_ready"), prior(u, ROT))
                    nc.scalar.activation(rin[:, k, :], sqz[:, k, :], ACT.Ln).then_inc(sem("lnr_ready"), 1)
                u = unit(Q, j, 0)
                if u:
                    k = u[2] % ROT
                    act.wait_ge(sem("z_ready"), count(u))
                    if prior(u, ROT) is not None:
                        act.wait_ge(sem("root_ready"), prior(u, ROT))
                    nc.scalar.activation(sqz[:, k, :], PS[:, (2 + 2 * k) * BANK:(4 + 2 * k) * BANK], ACT.Square)\
                      .then_inc(sem("sqz_ready"), 1)
                u = unit(Q, j, 1)
                if u:
                    k = u[2] % ROT
                    act.wait_ge(sem("lnr_ready"), count(u))
                    nc.scalar.activation(rin[:, k, :], rin[:, k, :], ACT.Exp, scale=-0.5).then_inc(sem("rin_ready"), 1)
                u = unit(Q, j, 5)
                if u and isinstance(u[1], int) and u[1] == T - 1:
                    act.wait_ge(sem("agg2_done"), count(u))
                    nc.scalar.activation(TB[0:D + 1, u[0] * QUART:(u[0] + 1) * QUART], PS[0:D + 1, 0:QUART], ACT.Copy)\
                      .then_inc(sem("quarter_out"), 1)
            nc.scalar.preload_act_table_set("natural_log_exp_and_others")
            act.wait_ge(sem("stats2_ready"), 1)
            walk2(act, step2)
            copy_out("tanT_out", TA[:, 0:UNIT], PS[:, 0:UNIT], ("tanT_ready", 1))
            one("v_sq", sqr, cen, ACT.Square, ("v_ready", 1))
            one("v_root", st[2][:, :], st[1][:, :], ACT.Sqrt, ("v_norm2", 1))
            one("v_tanh", st[4][:, :], st[3][:, :], ACT.Tanh, ("v_norm", 1))
            norm(3)

            copy_out("h3T_out", TA[:, 0:UNIT], PS[:, 0:UNIT], ("h3T_ready", 1))

            def power(h, s, k, u, first):
                act.wait_ge(sem("counts_ready"), s * 2 + (u + 1))
                if not first:
                    act.wait_ge(sem("agg3_done"), s * 2 + (u - 7))
                nc.scalar.activation(pw[:, k, u * UNIT:(u + 1) * UNIT].bitcast(I16), PS[:, u * UNIT:(u + 1) * UNIT], ACT.Relu)\
                  .then_inc(sem("pw_ready"), 1)
            for h in range(2):
                for k in range(4):
                    for u in range(2):
                        power(h, h * T + k, k, u, h == 0)
                with act.Fori(1, T // 4) as it:
                    for k in range(4):
                        for u in range(2):
                            power(h, it * 4 + (h * T + k), k, u, False)
            copy_out("sums_out3", TA[:, 0:UNIT], PS[:, 4 * BANK:6 * BANK], ("agg3_done", 4 * T))

        @block.vector
        def _(dve):
            V = nc.vector
            chain = [0]

            def link(ins):
                chain[0] += 1
                ins.then_inc(sem("dve_chain"), 1)
                dve.wait_ge(sem("dve_chain"), chain[0])

            def rsqrt(v, root):
                link(V.reciprocal(root, root))
                link(V.tensor_tensor(st[9][:, :], root, root, ALU.mult))
                link(V.tensor_tensor(st[9][:, :], st[9][:, :], v, ALU.mult))
                link(V.tensor_scalar(st[9][:, :], st[9][:, :], -0.5, 1.5, ALU.mult, ALU.add))
                link(V.tensor_tensor(root, root, st[9][:, :], ALU.mult))

            def norm(L, done, dst=H[:, :, :]):
                link(V.reduce_sum(st[0][:, :], X[:, :, :], AX.X))
                link(V.tensor_scalar(st[0][:, :], st[0][:, :], -1.0 / D, None, ALU.mult))
                V.tensor_tensor(cen, X[:, :, :], bcast_t(st[0][:, :]), ALU.add).then_inc(sem(f"ln{L}_centred"), 1)
                if L == 1:
                    dve.wait_ge(sem("deg_summed"), 1)
                    V.tensor_scalar(deg[:, :], PS[:, 0:T], 1e-8, None, ALU.max).then_inc(sem("deg_out"), 1)
                dve.wait_ge(sem(f"ln{L}_sq"), 1)
                link(V.reduce_sum(st[1][:, :], sqr, AX.X))
                V.tensor_scalar(st[1][:, :], st[1][:, :], 1.0 / D, EPS, ALU.mult, ALU.add).then_inc(sem(f"ln{L}_var"), 1)
                dve.wait_ge(sem(f"ln{L}_sd"), 1)
                rsqrt(st[1][:, :], st[2][:, :])
                V.scalar_tensor_tensor(dst, cen, 0.0, bcast_t(st[2][:, :]), ALU.max, ALU.mult)\
                 .then_inc(sem(done), 1)

            def copy_out(name, dst, src, ready):
                dve.wait_ge(sem(ready[0]), ready[1])
                V.tensor_copy(dst, src).then_inc(sem(f"{name}_v"), 1)

            link(V.memset(TB[:, :], 0.0))
            dve.wait_ge(sem("x_loaded"), 16)
            norm(0, "feats0_ready", H[:, :, :])
            def add_deg(s, loaded, before):
                dve.wait_ge(sem(f"adj0_loaded{s}"), loaded)
                if before is not None:
                    dve.wait_ge(sem("deg_added"), before)
                half = s % 2
                V.tensor_tensor(TB[:, half * HALF:(half + 1) * HALF], TB[:, half * HALF:(half + 1) * HALF], ring[:, s, :], ALU.add)\
                 .then_inc(sem("deg_added"), 1)
            for s in range(RING):
                add_deg(s, 16, s - 1 if s >= 2 else None)
            with dve.Fori(1, 2 * T // RING) as it:
                for s in range(RING):
                    add_deg(s, it * 16 + 16, it * RING + (s - 1))
            copy_out("sums_out0", TA[:, UNIT:2 * UNIT], PS[:, UNIT:2 * UNIT], ("agg0_done", 2 * T))
            dve.wait_ge(sem("biases_loaded"), 16 * 7)
            dve.wait_ge(sem("z0_ready"), 1)
            z_hi = banks(4, 8).rearrange("p (t c) -> p t c", t=T)
            z_lo = banks(0, 4).rearrange("p (t c) -> p t c", t=T)
            link(V.tensor_tensor(cen, z_hi, bcast_c(bias["l0"][:, :]), ALU.add))
            link(V.scalar_tensor_tensor(X[:, :, :], cen, 0.0, X[:, :, :], ALU.max, ALU.add))

            norm(1, "feats_ready_l1")
            copy_out("hT_out", TA[:, UNIT:2 * UNIT], PS[:, UNIT:2 * UNIT], ("hT_ready", 1))
            dve.wait_ge(sem("scales_ready"), 1)

            def lorentz(tag, z, b, hb, dst, scale, time_sign, done):
                link_name = f"{tag}_biased"
                V.tensor_tensor(hb, z, bcast_c(b), ALU.add).then_inc(sem(link_name), 1)
                dve.wait_ge(sem(f"{tag}_sig"), 1)
                link(V.tensor_scalar(st[5][:, :], st[0][:, :], scale, 1.1, ALU.mult, ALU.add))
                dve.wait_ge(sem(f"{tag}_sq"), 1)
                link(V.reduce_sum(st[1][:, :], sqr[:, :, 0:D - 1], AX.X))
                link(V.tensor_scalar(st[1][:, :], st[1][:, :], 1e-8, None, ALU.max))
                link(V.reciprocal(st[1][:, :], st[1][:, :]))
                link(V.tensor_tensor(st[2][:, :], st[5][:, :], st[5][:, :], ALU.mult))
                V.scalar_tensor_tensor(st[3][:, :], st[2][:, :], -1.0, st[1][:, :], ALU.add, ALU.mult)\
                 .then_inc(sem(f"{tag}_ratio"), 1)
                dve.wait_ge(sem(f"{tag}_root"), 1)
                link(V.reciprocal(st[6][:, :], st[4][:, :]))
                link(V.tensor_tensor(st[6][:, :], st[6][:, :], st[3][:, :], ALU.mult))
                link(V.tensor_tensor(st[6][:, :], st[6][:, :], st[4][:, :], ALU.add))
                V.scalar_tensor_tensor(dst, hb, 0.5, bcast_t(st[6][:, :]), ALU.mult, ALU.mult).then_inc(sem(f"{tag}_space"), 1)
                dve.wait_ge(sem(f"{tag}_space"), 1)
                link(V.tensor_scalar(dst[:, :, 0], st[5][:, :], time_sign, None, ALU.mult))

            dve.wait_ge(sem("lin_h"), 1)
            lorentz("h", z_hi, bias["l1"][:, :], HBq, HL, esc[:, 0:1], 1.0, None)
            V.tensor_copy(st[7][:, :], st[5][:, :]).then_inc(sem("feats1_ready"), 1)
            copy_out("hlT_out", TA[:, UNIT:2 * UNIT], PS[:, UNIT:2 * UNIT], ("hlT_ready", 1))

            def parts(src, dst, a, b, c, name, twice=1):
                wide = src.unsqueeze(2).broadcast_to([P, T, twice, D])
                link(V.tensor_copy(dst[:, :, a:a + twice, :], wide))
                link(V.tensor_tensor(src, src, dst[:, :, a, :], ALU.subtract))
                link(V.tensor_copy(dst[:, :, b:b + twice, :], wide))
                V.tensor_tensor(dst[:, :, c, :], src, dst[:, :, b, :], ALU.subtract).then_inc(sem(name), 1)

            link(V.tensor_scalar(top[:, :], esc[:, :], 1.1, 1.0 / HALVES_TOP, ALU.add, ALU.mult))
            link(V.reciprocal(inv_top[:, :], top[:, :]))

            def halves(src, dst, twice, scale):
                link(V.tensor_scalar(src, src, scale, None, ALU.mult))
                wide = src.unsqueeze(2).broadcast_to([P, T, twice, D])
                link(V.tensor_copy(dst[:, :, 0:twice, :], wide))
                V.tensor_tensor(dst[:, :, twice:2 * twice, :], wide, dst[:, :, 0:twice, :], ALU.subtract)\
                 .then_inc(sem("halves_ready"), 1)

            dve.wait_ge(sem("lin_q"), 1)
            lorentz("q", z_hi, bias["q"][:, :], HBq, HBq, esc[:, 1:2], -1.0, None)
            V.tensor_copy(st[7][:, :], st[5][:, :]).then_inc(sem("q_done"), 1)
            dve.wait_ge(sem("lin_k"), 1)
            lorentz("k", z_lo, bias["k"][:, :], HBk, HBk, esc[:, 2:3], 1.0, None)
            halves(HBq, Q4, 2, inv_top[:, 1:2])
            halves(HBk, K2, 1, inv_top[:, 2:3])
            link(V.reciprocal(att_sc[:, 0:1], scal[:, 4:5]))
            link(V.tensor_scalar(att_sc[:, 0:1], att_sc[:, 0:1], 2.0, None, ALU.mult))
            link(V.tensor_scalar(att_sc[:, 1:2], att_sc[:, 0:1], top[:, 1:2], top[:, 2:3], ALU.mult, ALU.mult))
            V.tensor_scalar(att_sc[:, 2:3], att_sc[:, 0:1], scal[:, 3:4], None, ALU.add).then_inc(sem("att_scale_ready"), 1)
            for n, dst in enumerate((q_hh, q_ll, k_hl)):
                src = banks(0 if n % 2 else 4, 4 if n % 2 else 8).bitcast(F16)
                copy_out("pair_out", dst[:, HALF:N], src[:, HALF:N], ("pair_ready", n + 1))

            def product(u, n, s, loaded, first):
                dve.wait_ge(sem("att_ready"), n + 1)
                dve.wait_ge(sem(f"adj1_loaded{s}"), loaded)
                if not first:
                    dve.wait_ge(sem("agg1_done"), n - 3)
                V.tensor_tensor(prob[:, u, :], att[:, u % 2, :], ring[:, s, (u % 2) * UNIT:(u % 2 + 1) * UNIT], ALU.mult)\
                 .then_inc(sem("prob_ready"), 1)

            def turn1(it, loaded, peeled):
                for k in range(2):
                    for u in range(4):
                        product(u, it * 8 + (4 * k + u), 2 * k + u // 2, loaded, peeled and k == 0)
            turn1(0, 16, True)
            with dve.Fori(1, T // 2) as it:
                turn1(it, it * 16 + 16, False)
            copy_out("sums_out1", TA[:, UNIT:2 * UNIT], PS[:, UNIT:2 * UNIT], ("agg1_done", 4 * T))
            dve.wait_ge(sem("sup_sq"), 1)
            link(V.reduce_sum(st[0][:, :], sqr[:, :, 1:D], AX.X))
            link(V.tensor_tensor(st[1][:, :], st[0][:, :], sqr[:, :, 0], ALU.subtract))
            link(V.scalar_tensor_tensor(st[2][:, :], st[1][:, :], -1.0, st[1][:, :], ALU.mult, ALU.max))
            V.tensor_scalar(st[1][:, :], st[2][:, :], 1e-8, None, ALU.max).then_inc(sem("sup_inner"), 1)
            dve.wait_ge(sem("sup_root"), 1)
            rsqrt(st[1][:, :], st[2][:, :])
            link(V.tensor_tensor(cen, z_hi, bcast_t(st[2][:, :]), ALU.mult))
            link(V.tensor_tensor(X[:, :, :], X[:, :, :], cen, ALU.add))

            norm(2, "feats2_ready", Y[:, :, 0:D])
            dve.wait_ge(sem("y_sq"), 1)
            ysq, ball, iball, sgn, nball2 = (st[k][:, :] for k in (3, 4, 5, 6, 7))
            link(V.reduce_sum(ysq, sqr, AX.X))
            link(V.tensor_scalar(Y[:, :, D], ysq, 1.0, None, ALU.add))
            link(V.tensor_scalar(ball, ysq, -1.0, 1.0, ALU.mult, ALU.add))
            link(V.tensor_scalar(sgn, ball, 0.0, 2.0, ALU.is_ge, ALU.mult))
            link(V.tensor_scalar(sgn, sgn, -1.0, None, ALU.add))
            link(V.memset(Y[:, :, D + 1], 1.0))
            V.tensor_copy(Y[:, :, D + 2], sgn).then_inc(sem("zl_nodes_ready"), 1)
            link(V.scalar_tensor_tensor(iball, ball, -1.0, ball, ALU.mult, ALU.max))
            link(V.tensor_scalar(iball, iball, BALL_FLOOR, None, ALU.max))
            link(V.tensor_tensor(nball2, iball, iball, ALU.mult))
            link(V.tensor_scalar(nball2, nball2, -1.0, None, ALU.mult))
            V.reciprocal(iball, iball).then_inc(sem("stats2_ready"), 1)
            dve.wait_ge(sem("stats2_ready"), 1)
            link(V.scalar_tensor_tensor(zi[:, :, 0:D], Y[:, :, 0:D], -4.0, bcast_t(iball), ALU.mult, ALU.mult))
            link(V.tensor_tensor(zi[:, :, D], Y[:, :, D], iball, ALU.mult))
            V.memset(zi[:, :, D + 1:ROWS], 0.0).then_inc(sem("zr_nodes_ready"), 1)
            copy_out("zl_out", TA[0:ROWS, HALF:N], PS[0:ROWS, HALF:N], ("zl_flipped", 2))
            copy_out("zr_out", TB[0:ROWS, HALF:N], PS[0:ROWS, HALF:N], ("zr_flipped", 2))

            def step2(Q, j):
                u = unit(Q, j, 0)
                if u:
                    k = u[2] % ROT
                    dve.wait_ge(sem("sqz_ready"), count(u))
                    V.tensor_scalar(sqz[:, k, :], sqz[:, k, :], st[7][:, u1(u)], ROOT_FLOOR, ALU.add, ALU.max)\
                     .then_inc(sem("rest_ready"), 1)
                u = unit(Q, j, 1)
                if u:
                    k = u[2] % ROT
                    dve.wait_ge(sem("rin_ready"), count(u))
                    if prior(u, ROT) is not None:
                        dve.wait_ge(sem("wgt_ready"), prior(u, ROT))
                    V.tensor_tensor(sum_[:, k, :], sqz[:, k, :], rin[:, k, :], ALU.mult).then_inc(sem("root_ready"), 1)
                u = unit(Q, j, 3)
                if u:
                    k = u[2] % ROT
                    dve.wait_ge(sem("tau_ready"), count(u))
                    dve.wait_ge(sem("rad_ready"), count(u))
                    if prior(u, ROT) is not None:
                        dve.wait_ge(sem("agg2_done"), prior(u, ROT))
                    V.scalar_tensor_tensor(wgt[:, k, :], sum_[:, k, :], TAU_MAX, rad[:, k, :], ALU.min, ALU.mult)\
                     .then_inc(sem("wgt_ready"), 1)
                u = unit(Q, j, 1)
                if u:
                    k = u[2] % ROT
                    dve.wait_ge(sem("root_ready"), count(u))
                    dve.wait_ge(sem("zk_ready"), count(u))
                    V.tensor_tensor(sum_[:, k, :], sum_[:, k, :], PS[:, (2 + 2 * k) * BANK:(4 + 2 * k) * BANK], ALU.add)\
                     .then_inc(sem("sum_ready"), 1)
            walk2(dve, step2)

            dve.wait_ge(sem("agg2_nodes"), 1)
            G = work[:, 0:T * (D + 1)].rearrange("p (t c) -> p t c", t=T)
            for b in range(5):
                n = min(7, T - 7 * b)
                V.tensor_copy(G[:, 7 * b:7 * b + n, :],
                              PS[:, b * BANK:b * BANK + n * (D + 1)].rearrange("p (t c) -> p t c", t=n))\
                 .then_inc(sem("agg2_copied"), 1)
            dve.wait_ge(sem("agg2_copied"), 5)
            link(V.tensor_tensor(sqr, G[:, :, 0:D], Y[:, :, 0:D], ALU.mult))
            link(V.reduce_sum(st[0][:, :], sqr, AX.X))
            link(V.scalar_tensor_tensor(st[0][:, :], st[0][:, :], 2.0, G[:, :, D], ALU.mult, ALU.subtract))
            link(V.reciprocal(st[1][:, :], deg[:, :]))
            link(V.tensor_tensor(st[1][:, :], st[1][:, :], iball, ALU.mult))
            link(V.tensor_scalar(st[2][:, :], ball, MIN_NORM, None, ALU.max))
            link(V.tensor_tensor(st[1][:, :], st[1][:, :], st[2][:, :], ALU.mult))
            link(V.tensor_tensor(st[0][:, :], st[0][:, :], st[1][:, :], ALU.mult))
            link(V.tensor_tensor(st[1][:, :], st[1][:, :], ball, ALU.mult))
            link(V.tensor_tensor(sqr, Y[:, :, 0:D], bcast_t(st[0][:, :]), ALU.mult))
            link(V.tensor_tensor(cen, G[:, :, 0:D], bcast_t(st[1][:, :]), ALU.mult))
            V.tensor_tensor(cen, cen, sqr, ALU.add).then_inc(sem("tan_ready"), 1)
            copy_out("tanT_out", TA[:, UNIT:2 * UNIT], PS[:, UNIT:2 * UNIT], ("tanT_ready", 1))
            dve.wait_ge(sem("lin_w2"), 1)
            V.tensor_tensor(cen, z_hi, bcast_c(bias["w2"][:, :]), ALU.add).then_inc(sem("v_ready"), 1)
            dve.wait_ge(sem("v_sq"), 1)
            link(V.reduce_sum(st[0][:, :], sqr, AX.X))
            V.tensor_scalar(st[1][:, :], st[0][:, :], NORM2_FLOOR, None, ALU.max).then_inc(sem("v_norm2"), 1)
            dve.wait_ge(sem("v_root"), 1)
            rsqrt(st[1][:, :], st[2][:, :])
            V.tensor_tensor(st[3][:, :], st[1][:, :], st[2][:, :], ALU.mult).then_inc(sem("v_norm"), 1)
            dve.wait_ge(sem("v_tanh"), 1)
            link(V.tensor_tensor(st[2][:, :], st[2][:, :], st[4][:, :], ALU.mult))
            link(V.tensor_tensor(cen, cen, bcast_t(st[2][:, :]), ALU.mult))
            link(V.tensor_tensor(X[:, :, :], X[:, :, :], cen, ALU.add))

            norm(3, "feats_ready_l3")
            copy_out("h3T_out", TA[:, UNIT:2 * UNIT], PS[:, UNIT:2 * UNIT], ("h3T_ready", 1))
            dve.wait_ge(sem("lin_w3"), 1)
            link(V.tensor_scalar(cen, z_hi, W_SCALE, None, ALU.mult))
            parts(cen, S3, 0, 1, 2, "parts3_ready")
            link(V.tensor_tensor(X[:, :, :], X[:, :, :], bcast_c(bias["w3"][:, :]), ALU.add))

            def make_mask(s, k, loaded, first):
                dve.wait_ge(sem(f"adj3_loaded{k}"), loaded)
                if not first:
                    dve.wait_ge(sem("agg3_done"), s * 2 - 6)
                V.tensor_scalar(mask[:, k, :], ring[:, k, :], 0.0, None, ALU.not_equal).then_inc(sem("mask_ready"), 1)
            for h in range(2):
                for k in range(4):
                    make_mask(h * T + k, k, 16 * (h * T // 4 + 1), h == 0)
                with dve.Fori(1, T // 4) as it:
                    for k in range(4):
                        make_mask(it * 4 + (h * T + k), k, it * 16 + 16 * (h * T // 4 + 1), False)
            copy_out("sums_out3", TA[:, UNIT:2 * UNIT], PS[:, 6 * BANK:8 * BANK], ("agg3_done", 4 * T))
            dve.wait_ge(sem("agg3_nodes"), 1)
            V.tensor_tensor(X[:, :, :], X[:, :, :], z_lo, ALU.add).then_inc(sem("result_ready"), 1)


ROOT_FLOOR = 1e-12
NORM2_FLOOR = 1e-30


def kernel(**inputs):
    import numpy as _np
    import concourse.bacc as _bacc
    from concourse.bass_utils import run_bass_kernel_spmd as _run

    a = {k: _np.asarray(v) for k, v in inputs.items()}
    scalars = _np.stack([a["L1_gnn_scale"], a["L1_gnn_scale_q"], a["L1_gnn_scale_k"],
                         a["L1_gnn_att_bias"], a["L1_gnn_att_scale"]]).reshape(5)
    given = {
        "x": a["x"], "adj_t": a["adj"].T,
        "w0_t": a["L0_gnn_W"].T, "b0": a["L0_gnn_b"],
        "w1_t": a["L1_gnn_W"].T, "b1": a["L1_gnn_b"],
        "wq_t": a["L1_gnn_Wq"].T, "bq": a["L1_gnn_bq"],
        "wk_t": a["L1_gnn_Wk"].T, "bk": a["L1_gnn_bk"],
        "scalars": scalars,
        "w2": a["L2_gnn_weight"], "b2": a["L2_gnn_bias"],
        "w3": a["L3_gnn_weight"], "b3": a["L3_gnn_bias"],
    }
    nc = _bacc.Bacc("TRN2", target_bir_lowering=False, num_devices=1)
    arrays, args = {}, []
    for name, v in given.items():
        v = _np.ascontiguousarray(v)
        arrays[f"in_{name}"] = v
        args.append(nc.dram_tensor(f"in_{name}", v.shape, mybir.dt.from_np(v.dtype), kind="ExternalInput").ap())
    args.append(nc.dram_tensor("out_x", (N, D), F32, kind="ExternalOutput").ap())
    graph_layers(nc, *args)
    r = _run(nc, [arrays], core_ids=[0])
    return r.results[0]["out_x"]
```

```python
import concourse.bass as bass
from concourse import mybir
from contextlib import ExitStack

F32 = mybir.dt.float32
BF16 = mybir.dt.bfloat16
F16 = mybir.dt.float16
I16 = mybir.dt.int16
ALU = mybir.AluOpType
ACT = mybir.ActivationFunctionType
AX = mybir.AxisListType

N = 4096
D = 64
P = 128
T = N // P
BANK = 512
EPS = 1e-5
UNIT = 2 * BANK
HALF = N // 2
RING = 4
RING0 = 8
G = 2
TG = T // G
SLOT = 2048

CLIP = 1.0 - 1e-5
TAU_MAX = 12.206062
MIN_NORM = 1e-15
BALL_FLOOR = 1e-6
KAPPA = 2.0 ** 39
ROWS = D + 3
QUART = N // 4
ROT = 3
RING2 = 6

HALVES_TOP = 1024.0

MAX_NEIGH = 100
BF_STEP = 128.0
BF_BASE = MAX_NEIGH * BF_STEP
W_SCALE = 2.0 ** (127 - MAX_NEIGH)


def graph_layers(nc, x, adj_t, w0_t, b0, w1_t, b1, wq_t, bq, wk_t, bk, scalars, w2, b2, w3, b3, out):
    ctx = ExitStack()
    with ctx:
        def sb(name, shape, dt=F32):
            return ctx.enter_context(nc.sbuf_tensor(name, shape, dt))

        named = {}

        def sem(name):
            if name not in named:
                named[name] = ctx.enter_context(nc.semaphore(name))
            return named[name]

        ring = sb("ring", [P, RING, HALF])
        ring2 = ring[:, :, :].rearrange("p r (u n) -> p (r u) n", u=2)
        X = sb("X", [P, T, D])
        H = sb("H", [P, T, D])
        Y = sb("Y", [P, T, ROWS])
        TA = sb("TA", [P, N])
        TB = sb("TB", [P, N])
        work = sb("work", [P, 12 * SLOT])
        PS = ctx.enter_context(nc.psum_tensor("PS", [P, 8 * BANK], F32))

        def slot(k, n=1):
            return work[:, k * SLOT:(k + n) * SLOT]

        def nodes(ap):
            return ap.rearrange("p (t c) -> p t c", t=T)

        ident = sb("ident", [P, P])
        identh = sb("identh", [P, P], F16)
        wbd = {k: sb(f"wbd_{k}", [P, P]) for k in ("l0", "l1", "q", "k", "w2", "w3")}
        BIASES = ("l0", "l1", "q", "k", "w2", "w3")
        bias = sb("bias", [P, 6, D])
        brem = sb("brem", [P, 6, D])
        bcut = [sb(f"bcut{k}", [P, 6, D], BF16) for k in range(3)]
        brow = sb("brow", [P, 6, D], BF16)
        bones = sb("bones", [P, P], BF16)
        scal = sb("scal", [P, 5])
        esc = sb("esc", [P, 3])
        att_sc = sb("att_sc", [P, 3])
        half_top = sb("half_top", [P, 3])
        top, inv_top = sb("top", [P, 3]), sb("inv_top", [P, 3])
        deg = sb("deg", [P, T])
        zeros = sb("zeros", [P, BANK], BF16)
        ones = sb("ones", [P, 1])
        st = [sb(f"st{k}", [P, T]) for k in range(10)]
        ystage = sb("ystage", [P, 4, D + 1])
        zstage = sb("zstage", [P, ROT, P])
        sstage = sb("sstage", [P, 4, 3 * D], BF16)
        kmask = sb("kmask", [P, 1])
        tri_above = sb("tri_above", [P, P], BF16)
        tri_rest = sb("tri_rest", [P, P], BF16)

        tm = {k: sb(f"time_{k}", [P, T]) for k in ("h", "q", "k")}
        cen = nodes(slot(10))
        sqr = nodes(slot(11))

        def grp(ap, g):
            return ap[:, g * TG:(g + 1) * TG]

        def over_c(v, g):
            return grp(v, g).unsqueeze(2).broadcast_to([P, TG, D])

        def banks(a, b):
            return PS[:, a * BANK:b * BANK]

        def z_of(first, g):
            return banks(first + 2 * g, first + 2 * g + 2).rearrange("p (t c) -> p t c", t=TG)

        q_hh, q_ll, k_hl = (slot(k).bitcast(F16) for k in range(3))
        HL = nodes(slot(5))
        HBq, HBk = nodes(slot(6)), nodes(slot(7))
        Q2 = slot(8).bitcast(F16).rearrange("p (t s c) -> p t s c", t=T, s=2)
        K2 = slot(9).bitcast(F16).rearrange("p (t s c) -> p t s c", t=T, s=2)
        att = slot(6).rearrange("p (k n) -> p k n", k=2)
        prob = slot(7, 2).rearrange("p (k n) -> p k n", k=4)
        def trio(first):
            return work[:, first * UNIT:(first + ROT) * UNIT].rearrange("p (k n) -> p k n", k=ROT)
        sqz, rin, sum_, rad, wgt = (trio(ROT * k) for k in range(5))
        kap_l = work[:, 15 * UNIT:17 * UNIT].bitcast(BF16)
        kap_r = work[:, 17 * UNIT:19 * UNIT].bitcast(BF16)
        zi = work[:, 0:T * ROWS].rearrange("p (t c) -> p t c", t=T)
        Gn = work[:, 0:T * (D + 1)].rearrange("p (t c) -> p t c", t=T)
        mask = slot(0, 2).bitcast(BF16).rearrange("p (k n) -> p k n", k=4)
        pw = slot(2, 2).bitcast(BF16).rearrange("p (k n) -> p k n", k=4)
        S3 = work[:, 4 * SLOT:4 * SLOT + 3 * SLOT // 2].bitcast(BF16).rearrange("p (t s c) -> p t s c", t=T, s=3)

        adj_tiles = adj_t.rearrange("(t p) n -> t p n", p=P)
        x_nodes = x.rearrange("(t p) c -> p t c", p=P)
        out_nodes = out.rearrange("(t p) c -> p t c", p=P)

        def unit(Q, j, back):
            if isinstance(j, tuple):
                it, k = j
                n0 = Q * T + k - back
                return (Q, it * RING2 + (k - back), n0 % RING2, it + n0 // RING2)
            n = Q * T + j - back
            return (n // T, n % T, n % RING2, n // RING2) if 0 <= n < 4 * T else None

        def walk2(eng, step):
            for Q in range(4):
                for j in range(RING2):
                    step(Q, j)
                with eng.Fori(1, T // RING2) as it:
                    for k in range(RING2):
                        step(Q, (it, k))
                for j in range(T // RING2 * RING2, T):
                    step(Q, j)
            for j in range(DRAIN):
                step(4, j)

        DRAIN = 6

        def count(u):
            return u[0] * T + u[1] + 1

        def prior(u, rot):
            return None if isinstance(u[1], int) and count(u) <= rot else count(u) - rot

        def loads2(u):
            return u[3] * 16 + 16

        def agg2_col(t):
            g, t = t // TG, t % TG
            return (2 + 3 * g + t // 7) * BANK + (t % 7) * (D + 1)

        def ring0(k):
            return ring[:, k, :] if k < RING else slot(k - RING)

        def u1(u):
            return slice(u[1], u[1] + 1) if isinstance(u[1], int) else bass.ts(u[1], 1)

        LOADS0 = 16 * (2 * T // RING0)
        LOADS1 = LOADS0 + 16 * (2 * T // RING)

        block = ctx.enter_context(nc.Block())

        @block.sync
        def _(sp):
            for g in range(G):
                sp.dma_start(grp(X, g), grp(x_nodes, g)).then_inc(sem(f"x_loaded{g}"), 16)

            def tile(s, turn=RING):
                if isinstance(s, int):
                    return adj_tiles[s // 2, :, (s % 2) * HALF:(s % 2 + 1) * HALF]
                it, k = s
                return adj_tiles[it * (turn // 2) + k // 2, :, (k % 2) * HALF:(k % 2 + 1) * HALF]

            def load(k, src):
                sp.dma_start(ring[:, k, :], src).then_inc(sem(f"adj_loaded{k}"), 16)

            for k in range(RING0):
                sp.dma_start(ring0(k), tile(k)).then_inc(sem(f"adj_loaded{k}"), 16)
                if k == 1:
                    for n, bsrc in enumerate((b0, b1, bq, bk, b2, b3)):
                        sp.dma_start(bias[:, n, :], bsrc.partition_broadcast(P)).then_inc(sem("biases_loaded"), 16)
                    sp.dma_start(scal[:, :], scalars.partition_broadcast(P)).then_inc(sem("biases_loaded"), 16)
            for wname, wsrc in (("l0", w0_t), ("l1", w1_t), ("q", wq_t), ("k", wk_t), ("w2", w2), ("w3", w3)):
                sp.wait_ge(sem("wbd_zeroed"), 6)
                for r in range(2):
                    sp.dma_start(wbd[wname][r * D:(r + 1) * D, r * D:(r + 1) * D], wsrc).then_inc(sem("weights_loaded"), 16)
            with sp.Fori(1, 2 * T // RING0) as it:
                for k in range(RING0):
                    sp.wait_ge(sem("agg0_done"), it * RING0 + (k - RING0 + 1))
                    sp.wait_ge(sem("deg_added"), it * RING0 + (k - RING0 + 1))
                    sp.dma_start(ring0(k), tile((it, k), RING0)).then_inc(sem(f"adj_loaded{k}"), 16)
            for k in range(RING):
                sp.wait_ge(sem("agg0_done"), 2 * T - RING0 + k + 1)
                sp.wait_ge(sem("deg_added"), 2 * T - RING0 + k + 1)
                load(k, tile(k))
            with sp.Fori(1, 2 * T // RING) as it:
                for k in range(RING):
                    sp.wait_ge(sem("prob_ready"), (it * RING + (k - RING + 1)) * 2)
                    load(k, tile((it, k)))
            sp.wait_ge(sem("prob_ready"), 4 * T)

            def load2(Q, j):
                u = unit(Q, j, 0)
                if u is None:
                    return
                if prior(u, RING2) is not None:
                    sp.wait_ge(sem("rad_ready"), prior(u, RING2))
                sp.dma_start(ring2[:, u[2], :], adj_tiles[u[1], :, Q * QUART:(Q + 1) * QUART])\
                  .then_inc(sem(f"adj2_loaded{u[2]}"), 16)
            walk2(sp, load2)
            sp.wait_ge(sem("rad_ready"), 4 * T)

            def load3(h, jt, k):
                sp.dma_start(ring[:, k, :], adj_tiles[jt, :, h * HALF:(h + 1) * HALF])\
                  .then_inc(sem(f"adj_loaded{k}"), 16)
            for h in range(2):
                for k in range(RING):
                    if h:
                        sp.wait_ge(sem("mask_ready"), h * T + k - RING + 1)
                    load3(h, T - 1 - k, k)
                with sp.Fori(1, T // RING) as it:
                    for k in range(RING):
                        jt = it * (-RING) + (T - 1 - k)
                        sp.wait_ge(sem("mask_ready"), it * RING + (h * T + k - RING + 1))
                        load3(h, jt, k)
            for g in range(G):
                sp.wait_ge(sem("result_ready"), g + 1)
                sp.dma_start(grp(out_nodes, g), grp(X, g)).then_inc(sem("stored"), 16)
            sp.wait_ge(sem("stored"), 16 * G)

        @block.gpsimd
        def _(pool):
            chain = [0]

            def link(ins):
                chain[0] += 1
                ins.then_inc(sem("pool_chain"), 1)
                pool.wait_ge(sem("pool_chain"), chain[0])

            for w in wbd.values():
                nc.gpsimd.memset(w[:, :], 0.0).then_inc(sem("wbd_zeroed"), 1)
            nc.gpsimd.memset(zeros[:, :], 0.0).then_inc(sem("consts_ready"), 1)
            nc.gpsimd.memset(ones[:, :], 1.0).then_inc(sem("consts_ready"), 1)
            nc.gpsimd.memset(bones[:, :], 1.0).then_inc(sem("consts_ready"), 1)
            link(nc.gpsimd.memset(ident[:, :], 0.0))
            link(nc.gpsimd.affine_select(out=ident[:, :], in_=ident[:, :], compare_op=ALU.not_equal, fill=1.0,
                                         base=0, pattern=[[-1, P]], channel_multiplier=1))
            nc.gpsimd.tensor_copy(identh[:, :], ident[:, :]).then_inc(sem("consts_ready"), 1)
            link(nc.gpsimd.memset(kmask[:, :], 0.0))
            link(nc.gpsimd.affine_select(out=kmask[:, :], in_=kmask[:, :], compare_op=ALU.not_equal, fill=KAPPA,
                                         base=-(D + 1), pattern=[[0, 1]], channel_multiplier=1))
            nc.gpsimd.affine_select(out=kmask[:, :], in_=kmask[:, :], compare_op=ALU.not_equal, fill=-KAPPA,
                                    base=-(D + 2), pattern=[[0, 1]], channel_multiplier=1)\
              .then_inc(sem("consts_ready"), 1)
            link(nc.gpsimd.memset(tri_above[:, :], -BF_STEP))
            link(nc.gpsimd.affine_select(out=tri_above[:, :], in_=tri_above[:, :], compare_op=ALU.is_ge, fill=0.0,
                                         base=0, pattern=[[-1, P]], channel_multiplier=1))
            nc.gpsimd.affine_select(out=tri_above[:, :], in_=tri_above[:, :], compare_op=ALU.not_equal, fill=BF_BASE,
                                    base=0, pattern=[[-1, P]], channel_multiplier=1).then_inc(sem("consts_ready"), 1)
            link(nc.gpsimd.memset(tri_rest[:, :], -BF_STEP))
            link(nc.gpsimd.affine_select(out=tri_rest[:, :], in_=tri_rest[:, :], compare_op=ALU.is_ge, fill=0.0,
                                         base=0, pattern=[[1, P]], channel_multiplier=-1))
            nc.gpsimd.affine_select(out=tri_rest[:, :], in_=tri_rest[:, :], compare_op=ALU.not_equal,
                                    fill=-BF_STEP - BF_BASE, base=0, pattern=[[-1, P]], channel_multiplier=1)\
              .then_inc(sem("consts_ready"), 1)

            for layer, feats in ((0, H), (1, HL)):
                pool.wait_ge(sem(f"feats{layer}_ready"), 1)
                if layer:
                    pool.wait_ge(sem("agg0_done"), 2 * T)
                for k in range(2):
                    nc.gpsimd.tensor_copy(ystage[:, k, 0:D], feats[:, k, 0:D]).then_inc(sem(f"staged{layer}"), 1)
                for first, last in ((1, TG // 2), (TG // 2, T // 2)):
                  if first > 1:
                    pool.wait_ge(sem(f"feats{layer}_ready"), G)
                  with pool.Fori(first, last) as it:
                    for k in range(2):
                        if layer == 0:
                            pool.wait_ge(sem("agg0_done"), it * 4 + (2 * k - 2))
                        else:
                            pool.wait_ge(sem("agg1_done"), it * 8 + (4 * k - 4))
                        nc.gpsimd.tensor_copy(ystage[:, k, 0:D], feats[:, it * 2 + k, 0:D])\
                          .then_inc(sem(f"staged{layer}"), 1)

            pool.wait_ge(sem("zl_out_a"), 1)
            pool.wait_ge(sem("zl_out_v"), 1)
            pool.wait_ge(sem("agg1_done"), 4 * T)

            def step2(Q, j):
                for u in ([unit(0, 0, 0)] if (Q, j) == (0, 0) else []) + [unit(Q, j, -1)]:
                    if u is None:
                        continue
                    if prior(u, ROT) is not None:
                        pool.wait_ge(sem("z_ready"), prior(u, ROT))
                    nc.gpsimd.tensor_copy(zstage[0:ROWS, u[2] % ROT, :], TA[0:ROWS, bass.ts(u[1], P)])\
                      .then_inc(sem("zstaged"), 1)
                u = unit(Q, j, 2)
                if u:
                    k = u[2] % ROT
                    pool.wait_ge(sem("rin_ready"), count(u))
                    pool.wait_ge(sem(f"adj2_loaded{u[2]}"), loads2(u))
                    if prior(u, ROT) is not None:
                        pool.wait_ge(sem("wgt_ready"), prior(u, ROT))
                    nc.gpsimd.tensor_tensor(rad[:, k, :], rin[:, k, :], ring2[:, u[2], :], ALU.mult)\
                      .then_inc(sem("rad_ready"), 1)
                    if prior(u, ROT) is not None:
                        pool.wait_ge(sem("agg2_done"), prior(u, ROT))
                    nc.gpsimd.tensor_copy(ystage[:, k, :], Y[:, u[1], 0:D + 1]).then_inc(sem("ystaged"), 1)
            walk2(pool, step2)

            for g in range(G):
                pool.wait_ge(sem("ln_centred"), 4 * G)
                pool.wait_ge(sem("biases_loaded"), 16 * 7)
                nc.gpsimd.tensor_tensor(grp(X, g), grp(X, g), bias[:, 5:6, :].broadcast_to([P, TG, D]), ALU.add)\
                  .then_inc(sem("bias3_added"), 1)
            pool.wait_ge(sem("parts3_ready"), G)
            for h in range(2):
                for k in range(4):
                    if h:
                        pool.wait_ge(sem("agg3_done"), 2 * (h * T + k - 4 + 1))
                    nc.gpsimd.tensor_copy(sstage[:, k, :].rearrange("p (s c) -> p s c", s=3), S3[:, T - 1 - k, :, :])\
                      .then_inc(sem("staged3"), 1)
                with pool.Fori(1, T // 4) as it:
                    for k in range(4):
                        jt = it * (-4) + (T - 1 - k)
                        pool.wait_ge(sem("agg3_done"), it * 8 + 2 * (h * T + k - 4 + 1))
                        nc.gpsimd.tensor_copy(sstage[:, k, :].rearrange("p (s c) -> p s c", s=3), S3[:, jt, :, :]).then_inc(sem("staged3"), 1)

        @block.tensor
        def _(pe):
            mm = nc.tensor.matmul

            def clear(first, last, signal=None):
                for b in range(first, last):
                    ins = mm(PS[:, b * BANK:(b + 1) * BANK], zeros[:, 0:P], zeros[:, :], start=True, stop=True)
                return ins

            def add(out_ap, lhsT, rhs):
                return mm(out_ap, lhsT, rhs, start=False, stop=True, skip_group_check=True)

            def to_nodes(rhs, g, dst, b=None):
                for a in (2 * g, 2 * g + 1):
                    if b is not None:
                        bias_rows(b, dst + a)
                    for q in range(4):
                        o = banks(dst + a, dst + a + 1).rearrange("p (r b c) -> p b r c", r=2, b=4)
                        ins = mm(o[:, q, :, :], TA[:, a * BANK + q * P:a * BANK + (q + 1) * P], rhs,
                                 start=b is None, stop=True, skip_group_check=True)
                return ins

            def bias_rows(b, bank):
                return mm(banks(bank, bank + 1).rearrange("p (t c) -> p t c", c=D), bones[0:96, :],
                          brow[0:96, b:b + 1, :].broadcast_to([96, BANK // D, D]), start=True, stop=True)

            def flip(src, g, dst):
                for u in range(g * TG // 2, (g + 1) * TG // 2):
                    ins = nc.tensor.transpose(PS[:, dst * BANK + u * P:dst * BANK + (u + 1) * P],
                                              src[:, 2 * u:2 * u + 2, :], ident[:, :])
                return ins

            def linear(w, b, g, dst):
                for a in (2 * g, 2 * g + 1):
                    if b is not None:
                        bias_rows(b, dst + a)
                    for u in range(4 * a, 4 * a + 4):
                        ins = mm(PS[:, dst * BANK + u * P:dst * BANK + (u + 1) * P], TA[:, u * P:(u + 1) * P], w,
                                 start=b is None, stop=True, skip_group_check=True)
                return ins

            def copied_out(name, n=1):
                pe.wait_ge(sem(f"{name}_a"), n)
                pe.wait_ge(sem(f"{name}_v"), n)

            pe.wait_ge(sem("consts_ready"), 7)
            clear(0, 4)

            def tile0(k, loaded, staged):
                pe.wait_ge(sem("staged0"), staged)
                for half in range(2):
                    s = 2 * k + half
                    pe.wait_ge(sem(f"adj_loaded{s}"), loaded)
                    for c in range(4):
                        cc = 4 * half + c
                        ins = add(PS[D * (cc % 2):D * (cc % 2) + D, (cc // 2) * BANK:(cc // 2 + 1) * BANK],
                                  ystage[:, k % 2, 0:D], ring0(s)[:, c * BANK:(c + 1) * BANK])
                    ins.then_inc(sem("agg0_done"), 1)
            with pe.Fori(0, 2 * T // RING0) as it:
                for k in range(RING0 // 2):
                    tile0(k, it * 16 + 16, it * (RING0 // 2) + (k + 1))
            pe.wait_ge(sem("weights_loaded"), 16 * 12)
            pe.wait_ge(sem("brow_ready"), 3)
            pe.wait_ge(sem("sums_out0_a"), 1)
            to_nodes(wbd["l0"][:, :], 0, 4, 0).then_inc(sem("z0_ready"), 1)
            pe.wait_ge(sem("sums_out0_v"), 1)
            to_nodes(wbd["l0"][:, :], 1, 4, 0).then_inc(sem("z0_ready"), 1)
            pe.wait_ge(sem("deg_added"), 2 * T)
            for t in range(T):
                ins = mm(PS[:, t:t + 1], TB[:, t * P:(t + 1) * P], ones[:, :], start=True, stop=True)
            ins.then_inc(sem("deg_summed"), 1)

            pe.wait_ge(sem("deg_out"), 1)
            for g in range(G):
                pe.wait_ge(sem("feats_ready_l1"), g + 1)
                flip(H, g, 0).then_inc(sem("hT_ready"), 1)
                pe.wait_ge(sem("hT_out"), g + 1)
                linear(wbd["l1"][:, :], 1, g, 4).then_inc(sem("lin_h"), 1)
            for g in range(G):
                pe.wait_ge(sem("feats1_ready"), g + 1)
                flip(HL, g, 0).then_inc(sem("hlT_ready"), 1)
                pe.wait_ge(sem("hlT_out"), g + 1)
                linear(wbd["q"][:, :], 2, g, 4).then_inc(sem("lin_q"), 1)
                linear(wbd["k"][:, :], 3, g, 0).then_inc(sem("lin_k"), 1)

            def fold(src, half, g, dst):
                o = banks(dst, dst + 2).bitcast(F16)
                for t in range(TG):
                    for r in range(2):
                        ins = nc.tensor.transpose(o[r * D:(r + 1) * D, t * P:(t + 1) * P], src[:, g * TG + t, half, :],
                                                  identh[:, :])
                return ins

            for g in range(G):
                pe.wait_ge(sem("q_high"), g + 1)
                pe.wait_ge(sem("q_low"), g + 1)
                fold(Q2, 0, g, 4 + 2 * g).then_inc(sem("qhh_ready"), 1)
                pe.wait_ge(sem("k_high"), g + 1)
                pe.wait_ge(sem("k_low"), g + 1)
                o = banks(2 * g, 2 * g + 2).bitcast(F16)
                for t in range(TG):
                    ins = nc.tensor.transpose(o[:, t * P:(t + 1) * P], K2[:, g * TG + t, :, :], identh[:, :])
                ins.then_inc(sem("khl_ready"), 1)
                pe.wait_ge(sem("qhh_out"), g + 1)
                fold(Q2, 1, g, 4 + 2 * g).then_inc(sem("qll_ready"), 1)
            pe.wait_ge(sem("khl_out"), G)
            pe.wait_ge(sem("qll_out"), G)
            clear(0, 4)

            def scores(k, u, n, first, jt):
                b = 4 + 2 * (u % 2)
                if not first:
                    pe.wait_ge(sem("att_ready"), n - 1)
                for c in range(2):
                    i0 = u * UNIT + c * BANK
                    o = PS[:, (b + c) * BANK:(b + c + 1) * BANK]
                    mm(o, k_hl[:, bass.ts(jt, P)], q_hh[:, i0:i0 + BANK], start=True, stop=False)
                    ins = mm(o, k_hl[:, bass.ts(jt, P)], q_ll[:, i0:i0 + BANK], start=False, stop=True)
                ins.then_inc(sem("scores_ready"), 1)

            def gather1(k, u, n):
                pe.wait_ge(sem("prob_ready"), n + 1)
                for c in range(2):
                    ins = add(PS[D * c:D * c + D, u * BANK:(u + 1) * BANK], ystage[:, k, 0:D],
                              prob[:, u, c * BANK:(c + 1) * BANK])
                ins.then_inc(sem("agg1_done"), 1)

            def turn1(it, peeled):
                for k in range(2):
                    jt = it * 2 + k
                    pe.wait_ge(sem("staged1"), it * 2 + (k + 1))
                    for u in range(4):
                        n = it * 8 + (4 * k + u)
                        scores(k, u, n, peeled and k == 0 and u < 2, jt)
                        if not (peeled and k == 0 and u < 2):
                            back = 4 * k + u - 2
                            gather1((back // 4) % 2, back % 4, it * 8 + back)
            turn1(0, True)
            with pe.Fori(1, T // 2) as it:
                turn1(it, False)
            for u in (2, 3):
                gather1(1, u, 4 * (T - 1) + u)
            pe.wait_ge(sem("sums_out1_a"), 1)
            to_nodes(ident[:, :], 0, 4).then_inc(sem("support_ready"), 1)
            pe.wait_ge(sem("sums_out1_v"), 1)
            to_nodes(ident[:, :], 1, 4).then_inc(sem("support_ready"), 1)

            def flip_rows(src, g):
                for t in range(g * TG, (g + 1) * TG):
                    ins = nc.tensor.transpose(PS[0:ROWS, t * P:(t + 1) * P], src[:, t, :], ident[:, :])
                return ins
            pe.wait_ge(sem("support_used"), G)
            for g in range(G):
                pe.wait_ge(sem("zl_nodes_ready"), g + 1)
                flip_rows(Y, g).then_inc(sem("zl_flipped"), 1)
            for g in range(G):
                pe.wait_ge(sem("zr_nodes_ready"), g + 1)
                pe.wait_ge(sem("zl_out_v" if g else "zl_out_a"), 1)
                flip_rows(zi, g).then_inc(sem("zr_flipped"), 1)
            copied_out("zr_out")
            pe.wait_ge(sem("kap_rows_ready"), 2 * G)

            def z_bank(k, c):
                return PS[:, (2 + 2 * k + c) * BANK:(3 + 2 * k + c) * BANK]

            def step2(Q, j):
                u = unit(Q, j, 0)
                if u:
                    k = u[2] % ROT
                    pe.wait_ge(sem("zstaged"), count(u))
                    if prior(u, ROT) is not None:
                        pe.wait_ge(sem("sum_ready"), prior(u, ROT))
                    for c in range(2):
                        ins = mm(z_bank(k, c), zstage[0:ROWS, k, :], TB[0:ROWS, Q * QUART + c * BANK:Q * QUART + (c + 1) * BANK],
                                 start=True, stop=True)
                    ins.then_inc(sem("z_ready"), 1)
                u = unit(Q, j, 1)
                if u:
                    k = u[2] % ROT
                    pe.wait_ge(sem("sqz_ready"), count(u))
                    for c in range(2):
                        ins = add(z_bank(k, c), kap_l[0:ROWS, bass.ts(u[1], P)],
                                  kap_r[0:ROWS, u[0] * QUART + c * BANK:u[0] * QUART + (c + 1) * BANK])
                    ins.then_inc(sem("zk_ready"), 1)
                u = unit(Q, j, 4)
                if u:
                    k = u[2] % ROT
                    pe.wait_ge(sem("ystaged"), count(u))
                    pe.wait_ge(sem("wgt_ready"), count(u))
                    if isinstance(u[1], int) and u[1] == 0:
                        if u[0] > 0:
                            pe.wait_ge(sem("quarter_out"), u[0])
                        clear(0, 2)
                    for c in range(2):
                        ins = add(PS[0:D + 1, c * BANK:(c + 1) * BANK], ystage[:, k, :], wgt[:, k, c * BANK:(c + 1) * BANK])
                    ins.then_inc(sem("agg2_done"), 1)
            walk2(pe, step2)
            for g in range(G):
                pe.wait_ge(sem("quarter_out"), 2 * g + 2)
                for t in range(g * TG, (g + 1) * TG):
                    ins = mm(PS[:, agg2_col(t):agg2_col(t) + D + 1], TB[0:D + 1, t * P:(t + 1) * P], ident[0:D + 1, 0:D + 1],
                             start=True, stop=True)
                ins.then_inc(sem("agg2_nodes"), 1)
            for g in range(G):
                pe.wait_ge(sem("tan_ready"), g + 1)
                if g == 0:
                    pe.wait_ge(sem("agg2_copied"), 3 * G)
                flip(cen, g, 0).then_inc(sem("tanT_ready"), 1)
                pe.wait_ge(sem("tanT_out"), g + 1)
                linear(wbd["w2"][:, :], 4, g, 4).then_inc(sem("lin_w2"), 1)

            for g in range(G):
                pe.wait_ge(sem("feats_ready_l3"), g + 1)
                flip(H, g, 0).then_inc(sem("h3T_ready"), 1)
                pe.wait_ge(sem("h3T_out"), g + 1)
                linear(wbd["w3"][:, :], None, g, 4).then_inc(sem("lin_w3"), 1)
            pe.wait_ge(sem("parts3_ready"), G)

            def counts(k, u, lhsT):
                for c in range(2):
                    ins = add(PS[:, (2 * u + c) * BANK:(2 * u + c + 1) * BANK], lhsT,
                              mask[:, k, u * UNIT + c * BANK:u * UNIT + (c + 1) * BANK])
                return ins

            def gather3(h, k, u):
                b = 4 + 2 * h + u
                for part in range(3):
                    for c in range(2):
                        ins = add(PS[D * c:D * c + D, b * BANK:(b + 1) * BANK], sstage[:, k, part * D:(part + 1) * D],
                                  pw[:, k, u * UNIT + c * BANK:u * UNIT + (c + 1) * BANK])
                return ins

            def step3(h, s, k, first):
                for u in range(2):
                    if not first:
                        pe.wait_ge(sem("pw_ready"), s * 2 + (u - 1))
                        counts((k - 1) % 4, u, tri_rest[:, :])
                    pe.wait_ge(sem("mask_ready"), s + 1)
                    counts(k, u, tri_above[:, :]).then_inc(sem("counts_ready"), 1)
                    if not first:
                        pe.wait_ge(sem("staged3"), s)
                        gather3(h, (k - 1) % 4, u).then_inc(sem("agg3_done"), 1)

            for h in range(2):
                if h:
                    pe.wait_ge(sem("pw_ready"), 2 * T * h)
                clear(0, 4)
                clear(4 + 2 * h, 6 + 2 * h)
                for k in range(4):
                    step3(h, h * T + k, k, k == 0)
                with pe.Fori(1, T // 4) as it:
                    for k in range(4):
                        step3(h, it * 4 + (h * T + k), k, False)
                for u in range(2):
                    pe.wait_ge(sem("pw_ready"), 2 * T * (h + 1) - 1 + u)
                    pe.wait_ge(sem("staged3"), T * (h + 1))
                    gather3(h, 3, u).then_inc(sem("agg3_done"), 1)
            pe.wait_ge(sem("sums_out3_a"), 1)
            to_nodes(ident[:, :], 0, 0).then_inc(sem("agg3_nodes"), 1)
            pe.wait_ge(sem("sums_out3_v"), 1)
            to_nodes(ident[:, :], 1, 0).then_inc(sem("agg3_nodes"), 1)

        @block.scalar
        def _(act):
            def one(name, out_ap, in_ap, func, wait, **kw):
                act.wait_ge(sem(wait[0]), wait[1])
                nc.scalar.activation(out_ap, in_ap, func, **kw).then_inc(sem(name), 1)

            def norm(L):
                for g in range(G):
                    one("ln_sq", grp(sqr, g), grp(cen, g), ACT.Square, ("ln_centred", L * G + g + 1))
                for g in range(G):
                    one("ln_sd", grp(st[2], g), grp(st[1], g), ACT.Sqrt, ("ln_var", L * G + g + 1))

            def flipped_out(name, g, ready):
                one(name, TA[:, g * UNIT:(g + 1) * UNIT], PS[:, g * UNIT:(g + 1) * UNIT], ACT.Copy, (ready, g + 1))

            norm(0)
            one("scales_ready", esc[:, :], scal[:, 0:3], ACT.Exp, ("biases_loaded", 16 * 7))
            one("sums_out0_a", TA[:, 0:UNIT], PS[:, 0:UNIT], ACT.Copy, ("agg0_done", 2 * T))
            norm(1)
            for g in range(G):
                flipped_out("hT_out", g, "hT_ready")

            def lorentz_squares(tag, first, g):
                act.wait_ge(sem(f"lin_{tag}"), g + 1)
                z = z_of(first, g)
                if tag == "k":
                    act.wait_ge(sem("q_summed"), g + 1)
                nc.scalar.activation(grp(sqr, g)[:, :, 0:D - 1], z[:, :, 1:D], ACT.Square).then_inc(sem(f"{tag}_sq"), 1)
                nc.scalar.activation(grp(tm[tag], g), z[:, :, 0], ACT.Sigmoid).then_inc(sem(f"{tag}_sig"), 1)

            def lorentz_root(tag, g):
                one(f"{tag}_root", grp(st[4], g), grp(st[3], g), ACT.Sqrt, (f"{tag}_ratio", g + 1))
            for g in range(G):
                lorentz_squares("h", 4, g)
            for g in range(G):
                lorentz_root("h", g)
            for g in range(G):
                flipped_out("hlT_out", g, "hlT_ready")
            for g in range(G):
                lorentz_squares("q", 4, g)
            for g in range(G):
                lorentz_squares("k", 0, g)
            for g in range(G):
                lorentz_root("q", g)
            for tag, src, dst in (("q", HBq, Q2), ("k", HBk, K2)):
                for g in range(G):
                    one(f"{tag}_high", grp(dst, g)[:, :, 0, :], grp(src, g), ACT.Copy, (f"{tag}_point", g + 1))
                if tag == "q":
                    for g in range(G):
                        lorentz_root("k", g)

            def folded_out(name, dst, g, bank, ready):
                one(name, dst[:, g * HALF:(g + 1) * HALF], banks(bank, bank + 2).bitcast(F16), ACT.Copy, (ready, g + 1))
            for g in range(G):
                folded_out("qhh_out", q_hh, g, 4 + 2 * g, "qhh_ready")
                folded_out("khl_out", k_hl, g, 2 * g, "khl_ready")

            act.wait_ge(sem("att_scale_ready"), 1)

            def sigm(u, n, first):
                act.wait_ge(sem("scores_ready"), n + 1)
                if not first:
                    act.wait_ge(sem("prob_ready"), n - 1)
                b = 4 + 2 * (u % 2)
                nc.scalar.activation(att[:, u % 2, :], PS[:, b * BANK:(b + 2) * BANK], ACT.Sigmoid,
                                     bias=att_sc[:, 2:3], scale=att_sc[:, 1:2]).then_inc(sem("att_ready"), 1)
            for u in range(4):
                sigm(u, u, u < 2)
            with act.Fori(1, T) as it:
                for u in range(4):
                    sigm(u, it * 4 + u, False)
            one("sums_out1_a", TA[:, 0:UNIT], PS[:, 0:UNIT], ACT.Copy, ("agg1_done", 4 * T))
            for g in range(G):
                one("sup_sq", grp(sqr, g), z_of(4, g), ACT.Square, ("support_ready", g + 1))
            for g in range(G):
                one("sup_root", grp(st[2], g), grp(st[1], g), ACT.Sqrt, ("sup_inner", g + 1))
            norm(2)

            for g in range(G):
                one("y_sq", grp(sqr, g), grp(Y, g)[:, :, 0:D], ACT.Square, ("feats2_ready", g + 1))
            nc.scalar.preload_act_table_set("natural_log_exp_and_others")
            one("zl_out_a", TA[0:ROWS, 0:HALF], PS[0:ROWS, 0:HALF], ACT.Copy, ("zl_flipped", 1))
            one("zr_out_a", TB[0:ROWS, 0:HALF], PS[0:ROWS, 0:HALF], ACT.Copy, ("zr_flipped", 1))

            def step2(Q, j):
                u = unit(Q, j, 3)
                if u:
                    k = u[2] % ROT
                    act.wait_ge(sem("sum_ready"), count(u))
                    nc.scalar.activation(sum_[:, k, :], sum_[:, k, :], ACT.Ln, scale=st[5][:, u1(u)])\
                      .then_inc(sem("tau_ready"), 1)
                u = unit(Q, j, 1)
                if u:
                    k = u[2] % ROT
                    act.wait_ge(sem("rest_ready"), count(u))
                    if prior(u, ROT) is not None:
                        act.wait_ge(sem("rad_ready"), prior(u, ROT))
                        act.wait_ge(sem("root_ready"), prior(u, ROT))
                    nc.scalar.activation(rin[:, k, :], sqz[:, k, :], ACT.Ln).then_inc(sem("lnr_ready"), 1)
                u = unit(Q, j, 0)
                if u:
                    k = u[2] % ROT
                    act.wait_ge(sem("z_ready"), count(u))
                    if prior(u, ROT) is not None:
                        act.wait_ge(sem("root_ready"), prior(u, ROT))
                    nc.scalar.activation(sqz[:, k, :], PS[:, (2 + 2 * k) * BANK:(4 + 2 * k) * BANK], ACT.Square)\
                      .then_inc(sem("sqz_ready"), 1)
                u = unit(Q, j, 1)
                if u:
                    k = u[2] % ROT
                    act.wait_ge(sem("lnr_ready"), count(u))
                    nc.scalar.activation(rin[:, k, :], rin[:, k, :], ACT.Exp, scale=-0.5).then_inc(sem("rin_ready"), 1)
                u = unit(Q, j, 5)
                if u and isinstance(u[1], int) and u[1] == T - 1:
                    act.wait_ge(sem("agg2_done"), count(u))
                    nc.scalar.activation(TB[0:D + 1, u[0] * QUART:(u[0] + 1) * QUART], PS[0:D + 1, 0:QUART], ACT.Copy)\
                      .then_inc(sem("quarter_out"), 1)
            act.wait_ge(sem("stats2_ready"), G)
            walk2(act, step2)
            for g in range(G):
                for b in range(3):
                    n = min(7, TG - 7 * b)
                    t = g * TG + 7 * b
                    one("agg2_copied", Gn[:, t:t + n, :],
                        PS[:, agg2_col(t):agg2_col(t) + n * (D + 1)].rearrange("p (t c) -> p t c", t=n),
                        ACT.Copy, ("agg2_nodes", g + 1))
            for g in range(G):
                flipped_out("tanT_out", g, "tanT_ready")
            for g in range(G):
                one("v_sq", grp(sqr, g), z_of(4, g), ACT.Square, ("lin_w2", g + 1))
            for g in range(G):
                one("v_root", grp(st[2], g), grp(st[1], g), ACT.Sqrt, ("v_norm2", g + 1))
            for g in range(G):
                one("v_tanh", grp(st[4], g), grp(st[3], g), ACT.Tanh, ("v_norm", g + 1))
            norm(3)

            for g in range(G):
                flipped_out("h3T_out", g, "h3T_ready")
            for g in range(G):
                one("part_a", grp(S3, g)[:, :, 0, :], z_of(4, g), ACT.Copy, ("lin_w3", g + 1), scale=W_SCALE)
            for g in range(G):
                one("part_b", grp(S3, g)[:, :, 1, :], grp(cen, g), ACT.Copy, ("rest_a", g + 1))

            def power(h, s, k, u, first):
                act.wait_ge(sem("counts_ready"), s * 2 + (u + 1))
                if not first:
                    act.wait_ge(sem("agg3_done"), s * 2 + (u - 7))
                nc.scalar.activation(pw[:, k, u * UNIT:(u + 1) * UNIT].bitcast(I16), PS[:, u * UNIT:(u + 1) * UNIT], ACT.Relu)\
                  .then_inc(sem("pw_ready"), 1)
            for h in range(2):
                for k in range(4):
                    for u in range(2):
                        power(h, h * T + k, k, u, h == 0)
                with act.Fori(1, T // 4) as it:
                    for k in range(4):
                        for u in range(2):
                            power(h, it * 4 + (h * T + k), k, u, False)
            one("sums_out3_a", TA[:, 0:UNIT], PS[:, 4 * BANK:6 * BANK], ACT.Copy, ("agg3_done", 4 * T))

        @block.vector
        def _(dve):
            V = nc.vector
            chain = [0]

            def link(ins):
                chain[0] += 1
                ins.then_inc(sem("dve_chain"), 1)
                dve.wait_ge(sem("dve_chain"), chain[0])

            last = [0] * G

            def hold(g):
                dve.wait_ge(sem("dve_chain"), last[g])

            def chained(g, ins):
                chain[0] += 1
                last[g] = chain[0]
                ins.then_inc(sem("dve_chain"), 1)

            def rsqrt(name, v, root, before=0):
                for g in range(G):
                    dve.wait_ge(sem(name), before + g + 1)
                    chained(g, V.reciprocal(grp(root, g), grp(root, g)))
                for g in range(G):
                    hold(g)
                    chained(g, V.tensor_tensor(grp(st[9], g), grp(root, g), grp(root, g), ALU.mult))
                for g in range(G):
                    hold(g)
                    chained(g, V.tensor_tensor(grp(st[9], g), grp(st[9], g), grp(v, g), ALU.mult))
                for g in range(G):
                    hold(g)
                    chained(g, V.tensor_scalar(grp(st[9], g), grp(st[9], g), -0.5, 1.5, ALU.mult, ALU.add))
                for g in range(G):
                    hold(g)
                    chained(g, V.tensor_tensor(grp(root, g), grp(root, g), grp(st[9], g), ALU.mult))

            def norm(L, done, dst=H):
                for g in range(G):
                    if L == 0:
                        dve.wait_ge(sem(f"x_loaded{g}"), 16)
                    hold(g)
                    chained(g, V.reduce_sum(grp(st[0], g), grp(X, g), AX.X))
                for g in range(G):
                    hold(g)
                    chained(g, V.tensor_scalar(grp(st[0], g), grp(st[0], g), -1.0 / D, None, ALU.mult))
                for g in range(G):
                    hold(g)
                    V.tensor_tensor(grp(cen, g), grp(X, g), over_c(st[0], g), ALU.add).then_inc(sem("ln_centred"), 1)
                if L == 1:
                    dve.wait_ge(sem("deg_summed"), 1)
                    V.tensor_scalar(deg[:, :], PS[:, 0:T], 1e-8, None, ALU.max).then_inc(sem("deg_out"), 1)
                for g in range(G):
                    dve.wait_ge(sem("ln_sq"), L * G + g + 1)
                    chained(g, V.reduce_sum(grp(st[1], g), grp(sqr, g), AX.X))
                for g in range(G):
                    hold(g)
                    V.tensor_scalar(grp(st[1], g), grp(st[1], g), 1.0 / D, EPS, ALU.mult, ALU.add)\
                     .then_inc(sem("ln_var"), 1)
                rsqrt("ln_sd", st[1], st[2], L * G)
                for g in range(G):
                    hold(g)
                    V.scalar_tensor_tensor(grp(dst, g)[:, :, 0:D], grp(cen, g), 0.0, over_c(st[2], g), ALU.max, ALU.mult)\
                     .then_inc(sem(done), 1)

            def copy_out(name, dst, src, ready):
                dve.wait_ge(sem(ready[0]), ready[1])
                V.tensor_copy(dst, src).then_inc(sem(name), 1)

            norm(0, "feats0_ready")
            link(V.memset(TB[:, :], 0.0))
            def add_deg(s, loaded, before):
                dve.wait_ge(sem(f"adj_loaded{s}"), loaded)
                if before is not None:
                    dve.wait_ge(sem("deg_added"), before)
                half = s % 2
                V.tensor_tensor(TB[:, half * HALF:(half + 1) * HALF], TB[:, half * HALF:(half + 1) * HALF], ring0(s), ALU.add)\
                 .then_inc(sem("deg_added"), 1)
            for s in range(RING0):
                add_deg(s, 16, s - 1 if s >= 2 else None)
            with dve.Fori(1, 2 * T // RING0) as it:
                for s in range(RING0):
                    add_deg(s, it * 16 + 16, it * RING0 + (s - 1))
            dve.wait_ge(sem("biases_loaded"), 16 * 7)
            link(V.memset(brow[:, :, :], 0.0))
            link(V.tensor_copy(bcut[0][:, :, :], bias[:, :, :]))
            link(V.tensor_tensor(brem[:, :, :], bias[:, :, :], bcut[0][:, :, :], ALU.subtract))
            link(V.tensor_copy(bcut[1][:, :, :], brem[:, :, :]))
            link(V.tensor_tensor(bcut[2][:, :, :], brem[:, :, :], bcut[1][:, :, :], ALU.subtract))
            for k in range(3):
                V.tensor_copy(brow[32 * k:32 * k + 1, :, :], bcut[k][32 * k:32 * k + 1, :, :]).then_inc(sem("brow_ready"), 1)
            dve.wait_ge(sem("scales_ready"), 1)
            link(V.tensor_scalar(top[:, :], esc[:, :], 1.1, 1.0 / HALVES_TOP, ALU.add, ALU.mult))
            link(V.reciprocal(inv_top[:, :], top[:, :]))
            link(V.tensor_scalar(half_top[:, :], inv_top[:, :], 0.5, None, ALU.mult))
            copy_out("sums_out0_v", TA[:, UNIT:2 * UNIT], PS[:, UNIT:2 * UNIT], ("agg0_done", 2 * T))
            for g in range(G):
                dve.wait_ge(sem("z0_ready"), g + 1)
                chained(g, V.scalar_tensor_tensor(grp(X, g), z_of(4, g), 0.0, grp(X, g), ALU.max, ALU.add))

            norm(1, "feats_ready_l1")

            def lorentz_ratio(tag, scale, ssum, ssq):
                for g in range(G):
                    dve.wait_ge(sem(f"{tag}_sq"), g + 1)
                    V.reduce_sum(grp(ssum, g), grp(sqr, g)[:, :, 0:D - 1], AX.X).then_inc(sem(f"{tag}_summed"), 1)
                for g in range(G):
                    dve.wait_ge(sem(f"{tag}_sig"), g + 1)
                    chained(g, V.tensor_scalar(grp(tm[tag], g), grp(tm[tag], g), scale, 1.1, ALU.mult, ALU.add))
                for g in range(G):
                    dve.wait_ge(sem(f"{tag}_summed"), g + 1)
                    chained(g, V.tensor_scalar(grp(ssum, g), grp(ssum, g), 1e-8, None, ALU.max))
                for g in range(G):
                    hold(g)
                    chained(g, V.reciprocal(grp(ssum, g), grp(ssum, g)))
                for g in range(G):
                    chained(g, V.tensor_tensor(grp(ssq, g), grp(tm[tag], g), grp(tm[tag], g), ALU.mult))
                for g in range(G):
                    hold(g)
                    V.scalar_tensor_tensor(grp(st[3], g), grp(ssq, g), -1.0, grp(ssum, g), ALU.add, ALU.mult)\
                     .then_inc(sem(f"{tag}_ratio"), 1)

            def lorentz_point(tag, first, dst, half, time_factor, done):
                for g in range(G):
                    dve.wait_ge(sem(f"{tag}_root"), g + 1)
                    chained(g, V.reciprocal(grp(st[6], g), grp(st[4], g)))
                for g in range(G):
                    hold(g)
                    chained(g, V.tensor_tensor(grp(st[6], g), grp(st[6], g), grp(st[3], g), ALU.mult))
                for g in range(G):
                    hold(g)
                    chained(g, V.tensor_tensor(grp(st[6], g), grp(st[6], g), grp(st[4], g), ALU.add))
                for g in range(G):
                    hold(g)
                    chained(g, V.scalar_tensor_tensor(grp(dst, g), z_of(first, g), half, over_c(st[6], g), ALU.mult, ALU.mult))
                for g in range(G):
                    hold(g)
                    if time_factor is None:
                        V.tensor_copy(grp(dst, g)[:, :, 0], grp(tm[tag], g)).then_inc(sem(done), 1)
                    else:
                        V.tensor_scalar(grp(dst, g)[:, :, 0], grp(tm[tag], g), *time_factor).then_inc(sem(done), 1)

            lorentz_ratio("h", esc[:, 0:1], st[1], st[2])
            lorentz_point("h", 4, HL, 0.5, None, "feats1_ready")
            lorentz_ratio("q", esc[:, 1:2], st[1], st[2])
            lorentz_point("q", 4, HBq, half_top[:, 1:2], (inv_top[:, 1:2], -1.0, ALU.mult, ALU.mult), "q_point")
            lorentz_ratio("k", esc[:, 2:3], st[7], st[8])

            def low(tag, src, dst):
                for g in range(G):
                    dve.wait_ge(sem(f"{tag}_high"), g + 1)
                    V.tensor_tensor(grp(dst, g)[:, :, 1, :], grp(src, g), grp(dst, g)[:, :, 0, :], ALU.subtract)\
                     .then_inc(sem(f"{tag}_low"), 1)
            low("q", HBq, Q2)
            lorentz_point("k", 0, HBk, half_top[:, 2:3], (inv_top[:, 2:3], None, ALU.mult), "k_point")
            low("k", HBk, K2)
            link(V.reciprocal(att_sc[:, 0:1], scal[:, 4:5]))
            link(V.tensor_scalar(att_sc[:, 0:1], att_sc[:, 0:1], 2.0, None, ALU.mult))
            link(V.tensor_scalar(att_sc[:, 1:2], att_sc[:, 0:1], top[:, 1:2], top[:, 2:3], ALU.mult, ALU.mult))
            V.tensor_scalar(att_sc[:, 2:3], att_sc[:, 0:1], scal[:, 3:4], None, ALU.add).then_inc(sem("att_scale_ready"), 1)
            for g in range(G):
                copy_out("qll_out", q_ll[:, g * HALF:(g + 1) * HALF], banks(4 + 2 * g, 6 + 2 * g).bitcast(F16),
                         ("qll_ready", g + 1))

            def product(u, n, s, loaded, first):
                dve.wait_ge(sem("att_ready"), n + 1)
                dve.wait_ge(sem(f"adj_loaded{s}"), loaded)
                if not first:
                    dve.wait_ge(sem("agg1_done"), n - 3)
                V.tensor_tensor(prob[:, u, :], att[:, u % 2, :], ring[:, s, (u % 2) * UNIT:(u % 2 + 1) * UNIT], ALU.mult)\
                 .then_inc(sem("prob_ready"), 1)

            def turn1(it, loaded, peeled):
                for k in range(2):
                    for u in range(4):
                        product(u, it * 8 + (4 * k + u), 2 * k + u // 2, loaded, peeled and k == 0)
            turn1(0, LOADS0 + 16, True)
            with dve.Fori(1, T // 2) as it:
                turn1(it, it * 16 + (LOADS0 + 16), False)
            copy_out("sums_out1_v", TA[:, UNIT:2 * UNIT], PS[:, UNIT:2 * UNIT], ("agg1_done", 4 * T))
            for g in range(G):
                dve.wait_ge(sem("sup_sq"), g + 1)
                chained(g, V.reduce_sum(grp(st[0], g), grp(sqr, g)[:, :, 1:D], AX.X))
            for g in range(G):
                hold(g)
                chained(g, V.tensor_tensor(grp(st[1], g), grp(st[0], g), grp(sqr, g)[:, :, 0], ALU.subtract))
            for g in range(G):
                hold(g)
                chained(g, V.scalar_tensor_tensor(grp(st[2], g), grp(st[1], g), -1.0, grp(st[1], g), ALU.mult, ALU.max))
            for g in range(G):
                hold(g)
                V.tensor_scalar(grp(st[1], g), grp(st[2], g), 1e-8, None, ALU.max).then_inc(sem("sup_inner"), 1)
            rsqrt("sup_root", st[1], st[2])
            for g in range(G):
                hold(g)
                V.tensor_tensor(grp(cen, g), z_of(4, g), over_c(st[2], g), ALU.mult).then_inc(sem("support_used"), 1)
            for g in range(G):
                dve.wait_ge(sem("support_used"), g + 1)
                chained(g, V.tensor_tensor(grp(X, g), grp(X, g), grp(cen, g), ALU.add))

            norm(2, "feats2_ready", Y)
            ysq, ball, iball, sgn, nball2 = (st[k] for k in (3, 4, 5, 6, 7))
            V.memset(zi[:, :, D + 1:ROWS], 0.0).then_inc(sem("zi_zeroed"), 1)
            V.memset(Y[:, :, D + 1], 1.0).then_inc(sem("y_ones"), 1)
            for g in range(G):
                dve.wait_ge(sem("y_sq"), g + 1)
                chained(g, V.reduce_sum(grp(ysq, g), grp(sqr, g), AX.X))
            for g in range(G):
                hold(g)
                chained(g, V.tensor_scalar(grp(ball, g), grp(ysq, g), -1.0, 1.0, ALU.mult, ALU.add))
            for g in range(G):
                hold(g)
                chained(g, V.tensor_scalar(grp(sgn, g), grp(ball, g), 0.0, 2.0, ALU.is_ge, ALU.mult))
            for g in range(G):
                hold(g)
                chained(g, V.tensor_scalar(grp(sgn, g), grp(sgn, g), -1.0, None, ALU.add))
            for g in range(G):
                V.tensor_scalar(grp(Y, g)[:, :, D], grp(ysq, g), 1.0, None, ALU.add).then_inc(sem("y_one_plus"), 1)
            for g in range(G):
                hold(g)
                dve.wait_ge(sem("y_one_plus"), g + 1)
                dve.wait_ge(sem("y_ones"), 1)
                V.tensor_copy(grp(Y, g)[:, :, D + 2], grp(sgn, g)).then_inc(sem("zl_nodes_ready"), 1)
            for g in range(G):
                chained(g, V.scalar_tensor_tensor(grp(iball, g), grp(ball, g), -1.0, grp(ball, g), ALU.mult, ALU.max))
            for g in range(G):
                hold(g)
                chained(g, V.tensor_scalar(grp(iball, g), grp(iball, g), BALL_FLOOR, None, ALU.max))
            for g in range(G):
                hold(g)
                chained(g, V.scalar_tensor_tensor(grp(nball2, g), grp(iball, g), -1.0, grp(iball, g), ALU.mult, ALU.mult))
            for g in range(G):
                hold(g)
                V.reciprocal(grp(iball, g), grp(iball, g)).then_inc(sem("stats2_ready"), 1)
            for g in range(G):
                dve.wait_ge(sem("stats2_ready"), g + 1)
                chained(g, V.scalar_tensor_tensor(grp(zi, g)[:, :, 0:D], grp(Y, g)[:, :, 0:D], -4.0, over_c(iball, g),
                                                  ALU.mult, ALU.mult))
                hold(g)
                dve.wait_ge(sem("zi_zeroed"), 1)
                V.tensor_tensor(grp(zi, g)[:, :, D], grp(Y, g)[:, :, D], grp(iball, g), ALU.mult)\
                 .then_inc(sem("zr_nodes_ready"), 1)
            copy_out("zl_out_v", TA[0:ROWS, HALF:N], PS[0:ROWS, HALF:N], ("zl_flipped", 2))
            for g in range(G):
                cols = slice(g * HALF, (g + 1) * HALF)
                dve.wait_ge(sem("zl_out_v" if g else "zl_out_a"), 1)
                V.tensor_copy(kap_l[0:ROWS, cols], TA[0:ROWS, cols]).then_inc(sem("kap_rows_ready"), 1)
                V.tensor_scalar(kap_r[0:ROWS, cols], TA[0:ROWS, cols], kmask[0:ROWS, 0:1], None, ALU.mult)\
                 .then_inc(sem("kap_rows_ready"), 1)
            copy_out("zr_out_v", TB[0:ROWS, HALF:N], PS[0:ROWS, HALF:N], ("zr_flipped", 2))

            def step2(Q, j):
                u = unit(Q, j, 0)
                if u:
                    k = u[2] % ROT
                    dve.wait_ge(sem("sqz_ready"), count(u))
                    V.tensor_scalar(sqz[:, k, :], sqz[:, k, :], st[7][:, u1(u)], ROOT_FLOOR, ALU.add, ALU.max)\
                     .then_inc(sem("rest_ready"), 1)
                u = unit(Q, j, 1)
                if u:
                    k = u[2] % ROT
                    dve.wait_ge(sem("rin_ready"), count(u))
                    if prior(u, ROT) is not None:
                        dve.wait_ge(sem("wgt_ready"), prior(u, ROT))
                    V.tensor_tensor(sum_[:, k, :], sqz[:, k, :], rin[:, k, :], ALU.mult).then_inc(sem("root_ready"), 1)
                u = unit(Q, j, 3)
                if u:
                    k = u[2] % ROT
                    dve.wait_ge(sem("tau_ready"), count(u))
                    dve.wait_ge(sem("rad_ready"), count(u))
                    if prior(u, ROT) is not None:
                        dve.wait_ge(sem("agg2_done"), prior(u, ROT))
                    V.scalar_tensor_tensor(wgt[:, k, :], sum_[:, k, :], TAU_MAX, rad[:, k, :], ALU.min, ALU.mult)\
                     .then_inc(sem("wgt_ready"), 1)
                u = unit(Q, j, 1)
                if u:
                    k = u[2] % ROT
                    dve.wait_ge(sem("root_ready"), count(u))
                    dve.wait_ge(sem("zk_ready"), count(u))
                    V.tensor_tensor(sum_[:, k, :], sum_[:, k, :], PS[:, (2 + 2 * k) * BANK:(4 + 2 * k) * BANK], ALU.add)\
                     .then_inc(sem("sum_ready"), 1)
            walk2(dve, step2)

            for g in range(G):
                dve.wait_ge(sem("agg2_copied"), 3 * g + 3)
                chained(g, V.tensor_tensor(grp(sqr, g), grp(Gn, g)[:, :, 0:D], grp(Y, g)[:, :, 0:D], ALU.mult))
            for g in range(G):
                hold(g)
                chained(g, V.reduce_sum(grp(st[0], g), grp(sqr, g), AX.X))
            for g in range(G):
                hold(g)
                chained(g, V.scalar_tensor_tensor(grp(st[0], g), grp(st[0], g), 2.0, grp(Gn, g)[:, :, D],
                                                  ALU.mult, ALU.subtract))
            link(V.reciprocal(st[1][:, :], deg[:, :]))
            link(V.tensor_tensor(st[1][:, :], st[1][:, :], iball[:, :], ALU.mult))
            link(V.tensor_scalar(st[2][:, :], ball[:, :], MIN_NORM, None, ALU.max))
            link(V.tensor_tensor(st[1][:, :], st[1][:, :], st[2][:, :], ALU.mult))
            link(V.tensor_tensor(st[0][:, :], st[0][:, :], st[1][:, :], ALU.mult))
            link(V.tensor_tensor(st[1][:, :], st[1][:, :], ball[:, :], ALU.mult))
            for g in range(G):
                chained(g, V.tensor_tensor(grp(sqr, g), grp(Y, g)[:, :, 0:D], over_c(st[0], g), ALU.mult))
            for g in range(G):
                V.tensor_tensor(grp(cen, g), grp(Gn, g)[:, :, 0:D], over_c(st[1], g), ALU.mult).then_inc(sem("ball_part"), 1)
            for g in range(G):
                hold(g)
                dve.wait_ge(sem("ball_part"), g + 1)
                V.tensor_tensor(grp(cen, g), grp(cen, g), grp(sqr, g), ALU.add).then_inc(sem("tan_ready"), 1)
            for g in range(G):
                dve.wait_ge(sem("v_sq"), g + 1)
                chained(g, V.reduce_sum(grp(st[0], g), grp(sqr, g), AX.X))
            for g in range(G):
                hold(g)
                V.tensor_scalar(grp(st[1], g), grp(st[0], g), NORM2_FLOOR, None, ALU.max).then_inc(sem("v_norm2"), 1)
            rsqrt("v_root", st[1], st[2])
            for g in range(G):
                hold(g)
                V.tensor_tensor(grp(st[3], g), grp(st[1], g), grp(st[2], g), ALU.mult).then_inc(sem("v_norm"), 1)
            for g in range(G):
                dve.wait_ge(sem("v_tanh"), g + 1)
                chained(g, V.tensor_tensor(grp(st[2], g), grp(st[2], g), grp(st[4], g), ALU.mult))
            for g in range(G):
                hold(g)
                chained(g, V.tensor_tensor(grp(cen, g), z_of(4, g), over_c(st[2], g), ALU.mult))
            for g in range(G):
                hold(g)
                chained(g, V.tensor_tensor(grp(X, g), grp(X, g), grp(cen, g), ALU.add))

            norm(3, "feats_ready_l3")
            for g in range(G):
                dve.wait_ge(sem("part_a"), g + 1)
                V.scalar_tensor_tensor(grp(cen, g), z_of(4, g), W_SCALE, grp(S3, g)[:, :, 0, :], ALU.mult, ALU.subtract)\
                 .then_inc(sem("rest_a"), 1)
            for g in range(G):
                dve.wait_ge(sem("part_b"), g + 1)
                V.tensor_tensor(grp(S3, g)[:, :, 2, :], grp(cen, g), grp(S3, g)[:, :, 1, :], ALU.subtract)\
                 .then_inc(sem("parts3_ready"), 1)

            def make_mask(s, k, loaded, first):
                dve.wait_ge(sem(f"adj_loaded{k}"), loaded)
                if not first:
                    dve.wait_ge(sem("agg3_done"), s * 2 - 6)
                V.tensor_scalar(mask[:, k, :], ring[:, k, :], 0.0, None, ALU.not_equal).then_inc(sem("mask_ready"), 1)
            for h in range(2):
                for k in range(4):
                    make_mask(h * T + k, k, LOADS1 + 16 * (h * T // 4 + 1), h == 0)
                with dve.Fori(1, T // 4) as it:
                    for k in range(4):
                        make_mask(it * 4 + (h * T + k), k, it * 16 + (LOADS1 + 16 * (h * T // 4 + 1)), False)
            copy_out("sums_out3_v", TA[:, UNIT:2 * UNIT], PS[:, 6 * BANK:8 * BANK], ("agg3_done", 4 * T))
            for g in range(G):
                dve.wait_ge(sem("agg3_nodes"), g + 1)
                dve.wait_ge(sem("bias3_added"), g + 1)
                V.tensor_tensor(grp(X, g), grp(X, g), z_of(0, g), ALU.add).then_inc(sem("result_ready"), 1)


ROOT_FLOOR = 1e-12
NORM2_FLOOR = 1e-30


def kernel(**inputs):
    import numpy as _np
    import concourse.bacc as _bacc
    from concourse.bass_utils import run_bass_kernel_spmd as _run

    a = {k: _np.asarray(v) for k, v in inputs.items()}
    scalars = _np.stack([a["L1_gnn_scale"], a["L1_gnn_scale_q"], a["L1_gnn_scale_k"],
                         a["L1_gnn_att_bias"], a["L1_gnn_att_scale"]]).reshape(5)
    given = {
        "x": a["x"], "adj_t": a["adj"].T,
        "w0_t": a["L0_gnn_W"].T, "b0": a["L0_gnn_b"],
        "w1_t": a["L1_gnn_W"].T, "b1": a["L1_gnn_b"],
        "wq_t": a["L1_gnn_Wq"].T, "bq": a["L1_gnn_bq"],
        "wk_t": a["L1_gnn_Wk"].T, "bk": a["L1_gnn_bk"],
        "scalars": scalars,
        "w2": a["L2_gnn_weight"], "b2": a["L2_gnn_bias"],
        "w3": a["L3_gnn_weight"], "b3": a["L3_gnn_bias"],
    }
    nc = _bacc.Bacc("TRN2", target_bir_lowering=False, num_devices=1)
    arrays, args = {}, []
    for name, v in given.items():
        v = _np.ascontiguousarray(v)
        arrays[f"in_{name}"] = v
        args.append(nc.dram_tensor(f"in_{name}", v.shape, mybir.dt.from_np(v.dtype), kind="ExternalInput").ap())
    args.append(nc.dram_tensor("out_x", (N, D), F32, kind="ExternalOutput").ap())
    graph_layers(nc, *args)
    r = _run(nc, [arrays], core_ids=[0])
    return r.results[0]["out_x"]
```

```python
import concourse.bass as bass
from concourse import mybir
from contextlib import ExitStack

F32 = mybir.dt.float32
BF16 = mybir.dt.bfloat16
F16 = mybir.dt.float16
U8 = mybir.dt.uint8
I16 = mybir.dt.int16
ALU = mybir.AluOpType
ACT = mybir.ActivationFunctionType
AX = mybir.AxisListType

N = 4096
D = 64
P = 128
T = N // P
BANK = 512
EPS = 1e-5
UNIT = 2 * BANK
HALF = N // 2
RING = 4
RING0 = 8
G = 2
TG = T // G
MADE = 8
CODES = 8
SLOT = 2048

CLIP = 1.0 - 1e-5
TAU_MAX = 12.206062
MIN_NORM = 1e-15
BALL_FLOOR = 1e-6
KAPPA = 2.0 ** 39
ROWS = D + 3
QUART = N // 4
ROT = 3
ROOT_V = 832
RING2 = 6

HALVES_TOP = 1024.0

MAX_NEIGH = 100
BF_STEP = 128.0
W_SCALE = 2.0 ** (127 - MAX_NEIGH)


def graph_layers(nc, x, adj_t, codes, w0_t, b0, w1_t, b1, wq_t, bq, wk_t, bk, scalars, w2, b2, w3, b3, out):
    ctx = ExitStack()
    with ctx:
        def sb(name, shape, dt=F32):
            return ctx.enter_context(nc.sbuf_tensor(name, shape, dt))

        named = {}

        def sem(name):
            if name not in named:
                named[name] = ctx.enter_context(nc.semaphore(name))
            return named[name]

        ring = sb("ring", [P, RING, HALF])
        ring2 = ring[:, :, :].rearrange("p r (u n) -> p (r u) n", u=2)
        X = sb("X", [P, T, D])
        H = sb("H", [P, T, D])
        Y = sb("Y", [P, T, ROWS])
        TA = sb("TA", [P, N])
        TB = sb("TB", [P, N])
        work = sb("work", [P, 12 * SLOT])
        PS = ctx.enter_context(nc.psum_tensor("PS", [P, 8 * BANK], F32))

        def slot(k, n=1):
            return work[:, k * SLOT:(k + n) * SLOT]

        def nodes(ap):
            return ap.rearrange("p (t c) -> p t c", t=T)

        ident = sb("ident", [P, P])
        identh = sb("identh", [P, P], F16)
        WEIGHTS = ("l0", "l1", "q", "k", "w2", "w3")
        wbd = {k: sb(f"wbd_{k}", [P, P]) for k in WEIGHTS}
        bias = sb("bias", [P, 6, D])
        brem = sb("brem", [P, 6, D])
        bcut = [sb(f"bcut{k}", [P, 6, D], BF16) for k in range(3)]
        brow = sb("brow", [P, 6, D], BF16)
        bones = sb("bones", [P, P], BF16)
        scal = sb("scal", [P, 5])
        esc = sb("esc", [P, 3])
        att_sc = sb("att_sc", [P, 3])
        half_top = sb("half_top", [P, 3])
        top, inv_top = sb("top", [P, 3]), sb("inv_top", [P, 3])
        deg = sb("deg", [P, T])
        ones = sb("ones", [P, 1])
        st = [sb(f"st{k}", [P, T]) for k in range(10)]
        ystage = sb("ystage", [P, 4, D + 1])
        zstage = sb("zstage", [P, ROT, P])
        sstage = sb("sstage", [P, 4, 3 * D], BF16)
        kmask = sb("kmask", [P, 1])
        tri_above = sb("tri_above", [P, P], BF16)
        tri_rest = sb("tri_rest", [P, P], BF16)

        tm = {k: sb(f"time_{k}", [P, T]) for k in ("h", "q", "k")}
        agg_v, agg_y = sb("agg_v", [P, T]), sb("agg_y", [P, T])
        cen = nodes(slot(10))
        sqr = nodes(slot(11))

        def grp(ap, g):
            return ap[:, g * TG:(g + 1) * TG]

        def over_c(v, g):
            return grp(v, g).unsqueeze(2).broadcast_to([P, TG, D])

        def banks(a, b):
            return PS[:, a * BANK:b * BANK]

        def z_of(first, g):
            return banks(first + 2 * g, first + 2 * g + 2).rearrange("p (t c) -> p t c", t=TG)

        q_hh, q_ll, k_hl = (slot(k).bitcast(F16) for k in range(3))
        HL = nodes(slot(5))
        HBq, HBk = nodes(slot(6)), nodes(slot(7))
        Q2 = slot(8).bitcast(F16).rearrange("p (t s c) -> p t s c", t=T, s=2)
        K2 = slot(9).bitcast(F16).rearrange("p (t s c) -> p t s c", t=T, s=2)
        att = slot(6).rearrange("p (k n) -> p k n", k=2)
        prob = slot(7, 2).rearrange("p (k n) -> p k n", k=4)
        def trio(first):
            return work[:, first * UNIT:(first + ROT) * UNIT].rearrange("p (k n) -> p k n", k=ROT)
        sqz, rin, sum_, rad, wgt = (trio(ROT * k) for k in range(5))
        kap_l = work[:, 15 * UNIT:17 * UNIT].bitcast(BF16)
        kap_r = work[:, 17 * UNIT:19 * UNIT].bitcast(BF16)
        zi = work[:, 0:T * ROWS].rearrange("p (t c) -> p t c", t=T)
        Gn = work[:, 0:T * (D + 1)].rearrange("p (t c) -> p t c", t=T)
        mask = slot(4, 2).bitcast(BF16).rearrange("p (k n) -> p k n", k=4)
        made = slot(6, 2).bitcast(U8).rearrange("p (k n) -> p k n", k=MADE)
        code = ring[:, 0:2, :].rearrange("p r n -> p (r n)").bitcast(U8).rearrange("p (k n) -> p k n", k=CODES)
        pw = slot(2, 2).bitcast(BF16).rearrange("p (k n) -> p k n", k=4)
        S3 = work[:, 4 * SLOT:4 * SLOT + 3 * SLOT // 2].bitcast(BF16).rearrange("p (t s c) -> p t s c", t=T, s=3)

        adj_tiles = adj_t.rearrange("(t p) n -> t p n", p=P)
        code_tiles = codes.rearrange("(t p) n -> t p n", p=P)
        x_nodes = x.rearrange("(t p) c -> p t c", p=P)
        out_nodes = out.rearrange("(t p) c -> p t c", p=P)

        def unit(Q, j, back):
            if isinstance(j, tuple):
                it, k = j
                n0 = Q * T + k - back
                return (Q, it * RING2 + (k - back), n0 % RING2, it + n0 // RING2)
            n = Q * T + j - back
            return (n // T, n % T, n % RING2, n // RING2) if 0 <= n < 4 * T else None

        def walk2(eng, step):
            for Q in range(4):
                for j in range(RING2):
                    step(Q, j)
                with eng.Fori(1, T // RING2) as it:
                    for k in range(RING2):
                        step(Q, (it, k))
                for j in range(T // RING2 * RING2, T):
                    step(Q, j)
            for j in range(DRAIN):
                step(4, j)

        DRAIN = 6

        def count(u):
            return u[0] * T + u[1] + 1

        def prior(u, rot):
            return None if isinstance(u[1], int) and count(u) <= rot else count(u) - rot

        def loads2(u):
            return u[3] * 16 + 16

        def agg2_col(t):
            g, t = t // TG, t % TG
            return (2 + 3 * g + t // 7) * BANK + (t % 7) * (D + 1)

        def ring0(k):
            return ring[:, k, :] if k < RING else slot(k - RING)

        def u1(u):
            return slice(u[1], u[1] + 1) if isinstance(u[1], int) else bass.ts(u[1], 1)

        BEFORE = {"h": 0, "q": G, "k": 2 * G}

        LOADS0 = 16 * (2 * T // RING0)
        LOADS1 = LOADS0 + 16 * (2 * T // RING)


        def LOADS2(k):
            return LOADS1 if k < RING else LOADS0

        block = ctx.enter_context(nc.Block())

        @block.sync
        def _(sp):
            for g in range(G):
                sp.dma_start(grp(X, g), grp(x_nodes, g)).then_inc(sem(f"x_loaded{g}"), 16)

            def tile0(h, jt):
                return adj_tiles[jt, :, h * HALF:(h + 1) * HALF]

            def tile(s):
                if isinstance(s, int):
                    return adj_tiles[s // 2, :, (s % 2) * HALF:(s % 2 + 1) * HALF]
                it, k = s
                return adj_tiles[it * (RING // 2) + k // 2, :, (k % 2) * HALF:(k % 2 + 1) * HALF]

            def load(k, src):
                sp.dma_start(ring[:, k, :], src).then_inc(sem(f"adj_loaded{k}"), 16)

            for k in range(RING0):
                sp.dma_start(ring0(k), tile0(0, T - 1 - k)).then_inc(sem(f"adj_loaded{k}"), 16)
                if k == 1:
                    for n, bsrc in enumerate((b0, b1, bq, bk, b2, b3)):
                        sp.dma_start(bias[:, n, :], bsrc.partition_broadcast(P)).then_inc(sem("biases_loaded"), 16)
                    sp.dma_start(scal[:, :], scalars.partition_broadcast(P)).then_inc(sem("biases_loaded"), 16)
            for wname, wsrc in (("l0", w0_t), ("l1", w1_t), ("q", wq_t), ("k", wk_t), ("w2", w2), ("w3", w3)):
                sp.wait_ge(sem("wbd_zeroed"), 6)
                for r in range(2):
                    sp.dma_start(wbd[wname][r * D:(r + 1) * D, r * D:(r + 1) * D], wsrc).then_inc(sem("weights_loaded"), 16)
            def free0(s):
                sp.wait_ge(sem("agg0_done"), s)
                sp.wait_ge(sem("deg_added"), s)
            for h in range(2):
                if h:
                    for k in range(RING0):
                        free0(h * T + k - RING0 + 1)
                        sp.dma_start(ring0(k), tile0(h, T - 1 - k)).then_inc(sem(f"adj_loaded{k}"), 16)
                with sp.Fori(1, T // RING0) as it:
                    for k in range(RING0):
                        jt = it * (-RING0) + (T - 1 - k)
                        free0(it * RING0 + (h * T + k - RING0 + 1))
                        sp.dma_start(ring0(k), tile0(h, jt)).then_inc(sem(f"adj_loaded{k}"), 16)
            for k in range(RING):
                sp.wait_ge(sem("agg0_done"), 2 * T - RING0 + k + 1)
                sp.wait_ge(sem("deg_added"), 2 * T - RING0 + k + 1)
                load(k, tile(k))
            with sp.Fori(1, 2 * T // RING) as it:
                for k in range(RING):
                    sp.wait_ge(sem("prob_ready"), (it * RING + (k - RING + 1)) * 2)
                    load(k, tile((it, k)))
            sp.wait_ge(sem("prob_ready"), 4 * T)

            def load2(Q, j):
                u = unit(Q, j, 0)
                if u is None:
                    return
                if prior(u, RING2) is not None:
                    sp.wait_ge(sem("rad_ready"), prior(u, RING2))
                sp.dma_start(ring2[:, u[2], :], adj_tiles[u[1], :, Q * QUART:(Q + 1) * QUART])\
                  .then_inc(sem(f"adj2_loaded{u[2]}"), 16)
            walk2(sp, load2)
            sp.wait_ge(sem("rad_ready"), 4 * T)
            for k in range(MADE):
                sp.wait_ge(sem(f"codes_stored{k}"), 2 * T // MADE * 16)

            def store(g):
                sp.wait_ge(sem("result_ready"), g + 1)
                sp.dma_start(grp(out_nodes, g), grp(X, g)).then_inc(sem("stored"), 16)

            def load3(h, at, k):
                sp.dma_start(code[:, k, :], code_tiles[at, :, h * HALF:(h + 1) * HALF])\
                  .then_inc(sem(f"adj_loaded{k}"), 16)
            for h in range(2):
                for k in range(CODES):
                    if h:
                        sp.wait_ge(sem("pw_ready_a"), h * T + k - CODES + 1)
                        sp.wait_ge(sem("pw_ready_v"), h * T + k - CODES + 1)
                    load3(h, T - 1 - k, k)
                if h:
                    store(0)
                with sp.Fori(1, T // CODES) as it:
                    for k in range(CODES):
                        at = it * (-CODES) + (T - 1 - k)
                        sp.wait_ge(sem("pw_ready_a"), it * CODES + (h * T + k - CODES + 1))
                        sp.wait_ge(sem("pw_ready_v"), it * CODES + (h * T + k - CODES + 1))
                        load3(h, at, k)
            store(1)
            sp.wait_ge(sem("stored"), 16 * G)

        @block.gpsimd
        def _(pool):
            chain = [0]

            def link(ins):
                chain[0] += 1
                ins.then_inc(sem("pool_chain"), 1)
                pool.wait_ge(sem("pool_chain"), chain[0])

            for w in wbd.values():
                nc.gpsimd.memset(w[:, :], 0.0).then_inc(sem("wbd_zeroed"), 1)
            nc.gpsimd.memset(ones[:, :], 1.0).then_inc(sem("consts_ready"), 1)
            nc.gpsimd.memset(bones[:, :], 1.0).then_inc(sem("consts_ready"), 1)
            link(nc.gpsimd.memset(ident[:, :], 0.0))
            link(nc.gpsimd.affine_select(out=ident[:, :], in_=ident[:, :], compare_op=ALU.not_equal, fill=1.0,
                                         base=0, pattern=[[-1, P]], channel_multiplier=1))
            nc.gpsimd.tensor_copy(identh[:, :], ident[:, :]).then_inc(sem("consts_ready"), 1)
            link(nc.gpsimd.memset(kmask[:, :], 0.0))
            link(nc.gpsimd.affine_select(out=kmask[:, :], in_=kmask[:, :], compare_op=ALU.not_equal, fill=KAPPA,
                                         base=-(D + 1), pattern=[[0, 1]], channel_multiplier=1))
            nc.gpsimd.affine_select(out=kmask[:, :], in_=kmask[:, :], compare_op=ALU.not_equal, fill=-KAPPA,
                                    base=-(D + 2), pattern=[[0, 1]], channel_multiplier=1)\
              .then_inc(sem("consts_ready"), 1)
            link(nc.gpsimd.memset(tri_above[:, :], -1.0))
            link(nc.gpsimd.affine_select(out=tri_above[:, :], in_=tri_above[:, :], compare_op=ALU.is_ge, fill=0.0,
                                         base=0, pattern=[[-1, P]], channel_multiplier=1))
            nc.gpsimd.affine_select(out=tri_above[:, :], in_=tri_above[:, :], compare_op=ALU.not_equal, fill=float(MAX_NEIGH),
                                    base=0, pattern=[[-1, P]], channel_multiplier=1).then_inc(sem("consts_ready"), 1)
            link(nc.gpsimd.memset(tri_rest[:, :], -1.0))
            link(nc.gpsimd.affine_select(out=tri_rest[:, :], in_=tri_rest[:, :], compare_op=ALU.is_ge, fill=0.0,
                                         base=0, pattern=[[1, P]], channel_multiplier=-1))
            nc.gpsimd.affine_select(out=tri_rest[:, :], in_=tri_rest[:, :], compare_op=ALU.not_equal,
                                    fill=-1.0 - MAX_NEIGH, base=0, pattern=[[-1, P]], channel_multiplier=1)\
              .then_inc(sem("consts_ready"), 1)

            nc.gpsimd.memset(TB[:, :], 0.0).then_inc(sem("consts_ready"), 1)
            for h in range(2):
                pool.wait_ge(sem("feats0_ready"), G)
                for k in range(2):
                    if h:
                        pool.wait_ge(sem("agg0_done"), h * T + k - 1)
                    nc.gpsimd.tensor_copy(ystage[:, k, 0:D], H[:, T - 1 - k, :]).then_inc(sem("staged0"), 1)
                if h == 0:
                    pool.wait_ge(sem("biases_loaded"), 16 * 7)
                    link(nc.gpsimd.memset(brow[:, :, :], 0.0))
                    link(nc.gpsimd.tensor_copy(bcut[0][:, :, :], bias[:, :, :]))
                    link(nc.gpsimd.tensor_tensor(brem[:, :, :], bias[:, :, :], bcut[0][:, :, :], ALU.subtract))
                    link(nc.gpsimd.tensor_copy(bcut[1][:, :, :], brem[:, :, :]))
                    link(nc.gpsimd.tensor_tensor(bcut[2][:, :, :], brem[:, :, :], bcut[1][:, :, :], ALU.subtract))
                    for k in range(3):
                        nc.gpsimd.tensor_copy(brow[32 * k:32 * k + 1, :, :], bcut[k][32 * k:32 * k + 1, :, :])\
                          .then_inc(sem("brow_ready"), 1)
                        pool.wait_ge(sem("brow_ready"), k + 1)
                with pool.Fori(1, T // 2) as it:
                    for k in range(2):
                        jt = it * (-2) + (T - 1 - k)
                        pool.wait_ge(sem("agg0_done"), it * 2 + (h * T + k - 1))
                        nc.gpsimd.tensor_copy(ystage[:, k, 0:D], H[:, jt, :]).then_inc(sem("staged0"), 1)
            pool.wait_ge(sem("feats1_ready"), 1)
            pool.wait_ge(sem("agg0_done"), 2 * T)
            for k in range(2):
                nc.gpsimd.tensor_copy(ystage[:, k, 0:D], HL[:, k, :]).then_inc(sem("staged1"), 1)
            pool.wait_ge(sem("feats1_ready"), G)
            for g in range(G):
                pool.wait_ge(sem("q_high"), g + 1)
                nc.gpsimd.tensor_tensor(grp(Q2, g)[:, :, 1, :], grp(HBq, g), grp(Q2, g)[:, :, 0, :], ALU.subtract)\
                  .then_inc(sem("q_low"), 1)
            with pool.Fori(1, T // 2) as it:
                for k in range(2):
                    pool.wait_ge(sem("agg1_done"), it * 8 + (4 * k - 4))
                    nc.gpsimd.tensor_copy(ystage[:, k, 0:D], HL[:, it * 2 + k, :]).then_inc(sem("staged1"), 1)

            def add_x1(name):
                pool.wait_ge(sem(name), 2)
                nc.gpsimd.tensor_tensor(grp(X, 1), grp(X, 1), grp(cen, 1), ALU.add).then_inc(sem("x1_added"), 1)
            add_x1("support_used")

            pool.wait_ge(sem("zl_out_a"), 1)
            pool.wait_ge(sem("zl_out_v"), 1)
            pool.wait_ge(sem("agg1_done"), 4 * T)

            def step2(Q, j):
                for u in ([unit(0, 0, 0)] if (Q, j) == (0, 0) else []) + [unit(Q, j, -1)]:
                    if u is None:
                        continue
                    if prior(u, ROT) is not None:
                        pool.wait_ge(sem("z_ready"), prior(u, ROT))
                    nc.gpsimd.tensor_copy(zstage[0:ROWS, u[2] % ROT, :], TA[0:ROWS, bass.ts(u[1], P)])\
                      .then_inc(sem("zstaged"), 1)
                u = unit(Q, j, 1)
                if u:
                    k = u[2] % ROT
                    pool.wait_ge(sem("rin_ready"), count(u))
                    if prior(u, ROT) is not None:
                        pool.wait_ge(sem("wgt_ready"), prior(u, ROT))
                    nc.gpsimd.tensor_tensor(sum_[:, k, ROOT_V:], sqz[:, k, ROOT_V:], rin[:, k, ROOT_V:], ALU.mult)\
                      .then_inc(sem("root_ready_p"), 1)
                u = unit(Q, j, 2)
                if u:
                    k = u[2] % ROT
                    pool.wait_ge(sem("rin_ready"), count(u))
                    pool.wait_ge(sem(f"adj2_loaded{u[2]}"), loads2(u))
                    if prior(u, ROT) is not None:
                        pool.wait_ge(sem("wgt_ready"), prior(u, ROT))
                    nc.gpsimd.tensor_tensor(rad[:, k, :], rin[:, k, :], ring2[:, u[2], :], ALU.mult)\
                      .then_inc(sem("rad_ready"), 1)
                    if prior(u, ROT) is not None:
                        pool.wait_ge(sem("agg2_done"), prior(u, ROT))
                    nc.gpsimd.tensor_copy(ystage[:, k, :], Y[:, u[1], 0:D + 1]).then_inc(sem("ystaged"), 1)
            walk2(pool, step2)

            pool.wait_ge(sem("agg_coef"), 1)
            for g in range(G):
                pool.wait_ge(sem("agg2_copied"), 3 * g + 3)
                nc.gpsimd.tensor_tensor(grp(cen, g), grp(Gn, g)[:, :, 0:D], over_c(agg_v, g), ALU.mult)\
                  .then_inc(sem("ball_part"), 1)
            add_x1("v_used")

            for g in range(G):
                pool.wait_ge(sem("ln_centred"), 4 * G)
                pool.wait_ge(sem("biases_loaded"), 16 * 7)
                nc.gpsimd.tensor_tensor(grp(X, g), grp(X, g), bias[:, 5:6, :].broadcast_to([P, TG, D]), ALU.add)\
                  .then_inc(sem("bias3_added"), 1)
            pool.wait_ge(sem("parts3_ready"), 1)
            for h in range(2):
                for k in range(4):
                    if h:
                        pool.wait_ge(sem("agg3_done"), h * T + k - 4 + 1)
                    nc.gpsimd.tensor_copy(sstage[:, k, :].rearrange("p (s c) -> p s c", s=3), S3[:, k, :, :])\
                      .then_inc(sem("staged3"), 1)
                pool.wait_ge(sem("parts3_ready"), G)
                with pool.Fori(1, T // 4) as it:
                    for k in range(4):
                        pool.wait_ge(sem("agg3_done"), it * 4 + (h * T + k - 4 + 1))
                        nc.gpsimd.tensor_copy(sstage[:, k, :].rearrange("p (s c) -> p s c", s=3), S3[:, it * 4 + k, :, :])\
                          .then_inc(sem("staged3"), 1)

        @block.tensor
        def _(pe):
            mm = nc.tensor.matmul

            def add(out_ap, lhsT, rhs, starts=False):
                return mm(out_ap, lhsT, rhs, start=starts, stop=True, skip_group_check=True)

            def to_nodes(rhs, g, dst, b=None):
                for a in (2 * g, 2 * g + 1):
                    if b is not None:
                        bias_rows(b, dst + a)
                    for q in range(4):
                        o = banks(dst + a, dst + a + 1).rearrange("p (r b c) -> p b r c", r=2, b=4)
                        ins = mm(o[:, q, :, :], TA[:, a * BANK + q * P:a * BANK + (q + 1) * P], rhs,
                                 start=b is None, stop=True, skip_group_check=True)
                return ins

            def bias_rows(b, bank):
                return mm(banks(bank, bank + 1).rearrange("p (t c) -> p t c", c=D), bones[0:96, :],
                          brow[0:96, b:b + 1, :].broadcast_to([96, BANK // D, D]), start=True, stop=True)

            def flip(src, g, dst):
                for u in range(g * TG // 2, (g + 1) * TG // 2):
                    ins = nc.tensor.transpose(PS[:, dst * BANK + u * P:dst * BANK + (u + 1) * P],
                                              src[:, 2 * u:2 * u + 2, :], ident[:, :])
                return ins

            def linear(w, b, g, dst):
                for a in (2 * g, 2 * g + 1):
                    if b is not None:
                        bias_rows(b, dst + a)
                    for u in range(4 * a, 4 * a + 4):
                        ins = mm(PS[:, dst * BANK + u * P:dst * BANK + (u + 1) * P], TA[:, u * P:(u + 1) * P], w,
                                 start=b is None, stop=True, skip_group_check=True)
                return ins

            pe.wait_ge(sem("consts_ready"), 6)
            def tile0(h, s, k, loaded, first):
                pe.wait_ge(sem("staged0"), s + 1)
                pe.wait_ge(sem(f"adj_loaded{k}"), loaded)
                for c in range(4):
                    ins = add(PS[D * (c % 2):D * (c % 2) + D, (2 * h + c // 2) * BANK:(2 * h + c // 2 + 1) * BANK],
                              ystage[:, k % 2, 0:D], ring0(k)[:, c * BANK:(c + 1) * BANK], first)
                ins.then_inc(sem("agg0_done"), 1)
                for u in range(2):
                    if not first:
                        pe.wait_ge(sem("codes_made"), s * 2 + (u - 1))
                        counts((k - 1) % 4, u, tri_rest[:, :])
                    if u == 0:
                        pe.wait_ge(sem("mask_ready"), s + 1)
                    counts(k % 4, u, tri_above[:, :], first).then_inc(sem("counts_ready"), 1)

            def counts(k, u, lhsT, starts=False):
                for c in range(2):
                    ins = add(PS[:, (4 + 2 * u + c) * BANK:(5 + 2 * u + c) * BANK], lhsT,
                              mask[:, k, u * UNIT + c * BANK:u * UNIT + (c + 1) * BANK], starts)
                return ins

            for h in range(2):
                if h:
                    pe.wait_ge(sem("codes_made"), 2 * T * h)
                for k in range(RING0):
                    tile0(h, h * T + k, k, (h * T // RING0 + 1) * 16, k == 0)
                    if h and k == 5:
                        pe.wait_ge(sem("weights_loaded"), 16 * 12)
                        pe.wait_ge(sem("brow_ready"), 3)
                        pe.wait_ge(sem("sums_out0_a"), 1)
                        to_nodes(wbd["l0"][:, :], 0, 0, 0).then_inc(sem("z0_ready"), 1)
                with pe.Fori(1, T // RING0) as it:
                    for k in range(RING0):
                        tile0(h, it * RING0 + (h * T + k), k, it * 16 + (h * T // RING0 + 1) * 16, False)
            pe.wait_ge(sem("sums_out0_v"), 1)
            to_nodes(wbd["l0"][:, :], 1, 0, 0).then_inc(sem("z0_ready"), 1)
            pe.wait_ge(sem("codes_made"), 4 * T)
            pe.wait_ge(sem("deg_added"), 2 * T)
            for t in range(T):
                ins = mm(PS[:, 7 * BANK + t:7 * BANK + t + 1], TB[:, t * P:(t + 1) * P], ones[:, :], start=True, stop=True)
            ins.then_inc(sem("deg_summed"), 1)

            for g in range(G):
                pe.wait_ge(sem("feats_ready_l1"), g + 1)
                flip(H, g, 0).then_inc(sem("flipped"), 1)
            pe.wait_ge(sem("deg_out"), 1)
            for g in range(G):
                pe.wait_ge(sem("flip_out"), g + 1)
                linear(wbd["l1"][:, :], 1, g, 4).then_inc(sem("lin_h"), 1)
            for g in range(G):
                pe.wait_ge(sem("feats1_ready"), g + 1)
                flip(HL, g, 0).then_inc(sem("flipped"), 1)
            for g in range(G):
                pe.wait_ge(sem("flip_out"), G + g + 1)
                linear(wbd["q"][:, :], 2, g, 4).then_inc(sem("lin_q"), 1)
            for g in range(G):
                linear(wbd["k"][:, :], 3, g, 0).then_inc(sem("lin_k"), 1)

            def fold(src, half, g, dst):
                o = banks(dst, dst + 2).bitcast(F16)
                for t in range(TG):
                    for r in range(2):
                        ins = nc.tensor.transpose(o[r * D:(r + 1) * D, t * P:(t + 1) * P], src[:, g * TG + t, half, :],
                                                  identh[:, :])
                return ins

            for g in range(G):
                pe.wait_ge(sem("q_high"), g + 1)
                fold(Q2, 0, g, 4 + 2 * g).then_inc(sem("qhh_ready"), 1)
            for g in range(G):
                pe.wait_ge(sem("q_low"), g + 1)
                pe.wait_ge(sem("qhh_out"), g + 1)
                fold(Q2, 1, g, 4 + 2 * g).then_inc(sem("qll_ready"), 1)
            for g in range(G):
                pe.wait_ge(sem("k_high"), g + 1)
                pe.wait_ge(sem("k_low"), g + 1)
                o = banks(2 * g, 2 * g + 2).bitcast(F16)
                for t in range(TG):
                    ins = nc.tensor.transpose(o[:, t * P:(t + 1) * P], K2[:, g * TG + t, :, :], identh[:, :])
                ins.then_inc(sem("khl_ready"), 1)
            pe.wait_ge(sem("khl_out_a"), 1)
            pe.wait_ge(sem("khl_out_v"), 1)
            pe.wait_ge(sem("qll_out"), G)

            def scores(k, u, n, first, jt):
                b = 4 + 2 * (u % 2)
                if not first:
                    pe.wait_ge(sem("att_ready"), n - 1)
                for c in range(2):
                    i0 = u * UNIT + c * BANK
                    o = PS[:, (b + c) * BANK:(b + c + 1) * BANK]
                    mm(o, k_hl[:, bass.ts(jt, P)], q_hh[:, i0:i0 + BANK], start=True, stop=False)
                    ins = mm(o, k_hl[:, bass.ts(jt, P)], q_ll[:, i0:i0 + BANK], start=False, stop=True)
                ins.then_inc(sem("scores_ready"), 1)

            def gather1(k, u, n, starts=False):
                pe.wait_ge(sem("prob_ready"), n + 1)
                for c in range(2):
                    ins = add(PS[D * c:D * c + D, u * BANK:(u + 1) * BANK], ystage[:, k, 0:D],
                              prob[:, u, c * BANK:(c + 1) * BANK], starts)
                ins.then_inc(sem("agg1_done"), 1)

            def turn1(it, peeled):
                for k in range(2):
                    jt = it * 2 + k
                    pe.wait_ge(sem("staged1"), it * 2 + (k + 1))
                    for u in range(4):
                        n = it * 8 + (4 * k + u)
                        scores(k, u, n, peeled and k == 0 and u < 2, jt)
                        if not (peeled and k == 0 and u < 2):
                            back = 4 * k + u - 2
                            gather1((back // 4) % 2, back % 4, it * 8 + back, peeled and back < 4)
            turn1(0, True)
            with pe.Fori(1, T // 2) as it:
                turn1(it, False)
            for u in (2, 3):
                gather1(1, u, 4 * (T - 1) + u)
            pe.wait_ge(sem("sums_out1_a"), 1)
            to_nodes(ident[:, :], 0, 4).then_inc(sem("support_ready"), 1)
            pe.wait_ge(sem("sums_out1_v"), 1)
            to_nodes(ident[:, :], 1, 4).then_inc(sem("support_ready"), 1)

            def flip_rows(src, g):
                for t in range(g * TG, (g + 1) * TG):
                    ins = nc.tensor.transpose(PS[0:ROWS, t * P:(t + 1) * P], src[:, t, :], ident[:, :])
                return ins
            pe.wait_ge(sem("support_used"), G)
            for g in range(G):
                pe.wait_ge(sem("zl_nodes_ready"), g + 1)
                flip_rows(Y, g).then_inc(sem("zl_flipped"), 1)
            for g in range(G):
                pe.wait_ge(sem("zr_nodes_ready"), g + 1)
                pe.wait_ge(sem("zl_out_v" if g else "zl_out_a"), 1)
                flip_rows(zi, g).then_inc(sem("zr_flipped"), 1)

            def z_bank(k, c):
                return PS[:, (2 + 2 * k + c) * BANK:(3 + 2 * k + c) * BANK]

            def step2(Q, j):
                u = unit(Q, j, 0)
                if (Q, j) == (0, 0):
                    pe.wait_ge(sem("zr_out_a"), 1)
                if (Q, j) == (0, 1):
                    pe.wait_ge(sem("zr_out_v"), 1)
                if u:
                    k = u[2] % ROT
                    pe.wait_ge(sem("zstaged"), count(u))
                    if prior(u, ROT) is not None:
                        pe.wait_ge(sem("sum_ready"), prior(u, ROT))
                    for c in range(2):
                        ins = mm(z_bank(k, c), zstage[0:ROWS, k, :], TB[0:ROWS, Q * QUART + c * BANK:Q * QUART + (c + 1) * BANK],
                                 start=True, stop=True)
                    ins.then_inc(sem("z_ready"), 1)
                if (Q, j) == (0, 1):
                    pe.wait_ge(sem("kap_ready_a"), 2)
                if (Q, j) == (0, 2):
                    pe.wait_ge(sem("kap_ready_v"), 2)
                u = unit(Q, j, 1)
                if u:
                    k = u[2] % ROT
                    pe.wait_ge(sem("sqz_ready"), count(u))
                    for c in range(2):
                        ins = add(z_bank(k, c), kap_l[0:ROWS, bass.ts(u[1], P)],
                                  kap_r[0:ROWS, u[0] * QUART + c * BANK:u[0] * QUART + (c + 1) * BANK])
                    ins.then_inc(sem("zk_ready"), 1)
                u = unit(Q, j, 4)
                if (Q, j) == (4, 2):
                    pe.wait_ge(sem("sum_ready"), 4 * T)
                    pe.wait_ge(sem("quarter_out"), 3)
                    nodes2(0, TG)
                    nodes2(TG, TG + 7)
                if u:
                    k = u[2] % ROT
                    pe.wait_ge(sem("ystaged"), count(u))
                    pe.wait_ge(sem("wgt_ready"), count(u))
                    starts = isinstance(u[1], int) and u[1] == 0
                    if starts and u[0] > 0:
                        pe.wait_ge(sem("quarter_out"), u[0])
                    for c in range(2):
                        ins = add(PS[0:D + 1, c * BANK:(c + 1) * BANK], ystage[:, k, :], wgt[:, k, c * BANK:(c + 1) * BANK],
                                  starts)
                    ins.then_inc(sem("agg2_done"), 1)
            def nodes2(first, end):
                for t in range(first, end):
                    ins = mm(PS[:, agg2_col(t):agg2_col(t) + D + 1], TB[0:D + 1, t * P:(t + 1) * P], ident[0:D + 1, 0:D + 1],
                             start=True, stop=True)
                ins.then_inc(sem("agg2_nodes"), 1)

            walk2(pe, step2)
            pe.wait_ge(sem("quarter_out"), 4)
            nodes2(TG + 7, T)
            for g in range(G):
                pe.wait_ge(sem("tan_ready"), g + 1)
                if g == 0:
                    pe.wait_ge(sem("agg2_copied"), 3 * G)
                flip(cen, g, 0).then_inc(sem("flipped"), 1)
                pe.wait_ge(sem("flip_out"), 2 * G + g + 1)
                linear(wbd["w2"][:, :], 4, g, 4).then_inc(sem("lin_w2"), 1)

            for g in range(G):
                pe.wait_ge(sem("feats_ready_l3"), g + 1)
                flip(H, g, 0).then_inc(sem("flipped"), 1)
            for g in range(G):
                pe.wait_ge(sem("flip_out"), 3 * G + g + 1)
                linear(wbd["w3"][:, :], None, g, 4).then_inc(sem("lin_w3"), 1)
            pe.wait_ge(sem("parts3_ready"), G)

            def step3(h, s, k, first=False):
                pe.wait_ge(sem("staged3"), s + 1)
                for u in range(2):
                    pe.wait_ge(sem("pw_ready_v" if u else "pw_ready_a"), s + 1)
                    b = 4 + 2 * h + u
                    for part in range(3):
                        for c in range(2):
                            ins = add(PS[D * c:D * c + D, b * BANK:(b + 1) * BANK], sstage[:, k, part * D:(part + 1) * D],
                                      pw[:, k, u * UNIT + c * BANK:u * UNIT + (c + 1) * BANK], first and part == 0)
                ins.then_inc(sem("agg3_done"), 1)

            for h in range(2):
                for k in range(4):
                    step3(h, h * T + k, k, k == 0)
                if h:
                    pe.wait_ge(sem("sums_out3_a"), 1)
                    to_nodes(ident[:, :], 0, 0).then_inc(sem("agg3_nodes"), 1)
                with pe.Fori(1, T // 4) as it:
                    for k in range(4):
                        step3(h, it * 4 + (h * T + k), k)
            pe.wait_ge(sem("sums_out3_v"), 1)
            to_nodes(ident[:, :], 1, 0).then_inc(sem("agg3_nodes"), 1)

        @block.scalar
        def _(act):
            def one(name, out_ap, in_ap, func, wait, **kw):
                act.wait_ge(sem(wait[0]), wait[1])
                nc.scalar.activation(out_ap, in_ap, func, **kw).then_inc(sem(name), 1)

            chain = [0]

            def power_of(name, dst, src, exponent, wait, before=0, groups=range(G)):
                for g in groups:
                    act.wait_ge(sem(wait), before + g + 1)
                    nc.scalar.activation(grp(dst, g), grp(src, g), ACT.Ln).then_inc(sem("act_chain"), 1)
                for g in groups:
                    chain[0] += 1
                    act.wait_ge(sem("act_chain"), chain[0])
                    nc.scalar.activation(grp(dst, g), grp(dst, g), ACT.Exp, scale=exponent).then_inc(sem(name), 1)

            def norm(L, groups=range(G)):
                for g in groups:
                    one("ln_sq", grp(sqr, g), grp(cen, g), ACT.Square, ("ln_centred", L * G + g + 1))
                power_of("ln_sd", st[2], st[1], -0.5, "ln_var", L * G, groups)

            nc.scalar.preload_act_table_set("natural_log_exp_and_others")

            def flipped_out(n, g):
                one("flip_out", TA[:, g * UNIT:(g + 1) * UNIT], PS[:, g * UNIT:(g + 1) * UNIT], ACT.Copy, ("flipped", n * G + g + 1))

            norm(0)
            one("scales_ready", esc[:, :], scal[:, 0:3], ACT.Exp, ("biases_loaded", 16 * 7))

            def make_code(h, s, k, at, stored):
                for u in range(2):
                    act.wait_ge(sem("counts_ready"), s * 2 + (u + 1))
                    if u == 0 and stored is not None:
                        act.wait_ge(sem(f"codes_stored{k}"), stored)
                    nc.scalar.activation(made[:, k, u * UNIT:(u + 1) * UNIT], PS[:, (4 + 2 * u) * BANK:(6 + 2 * u) * BANK],
                                         ACT.Relu).then_inc(sem("codes_made"), 1)
                act.wait_ge(sem("codes_made"), s * 2 + 2)
                act.dma_start(code_tiles[at, :, h * HALF:(h + 1) * HALF], made[:, k, :]).then_inc(sem(f"codes_stored{k}"), 16)
            for h in range(2):
                for k in range(MADE):
                    make_code(h, h * T + k, k, k, h * T // MADE * 16 if h else None)
                    if h and k == 3:
                        one("sums_out0_a", TA[:, 0:UNIT], PS[:, 0:UNIT], ACT.Copy, ("agg0_done", T))
                with act.Fori(1, T // MADE) as it:
                    for k in range(MADE):
                        make_code(h, it * MADE + (h * T + k), k, it * MADE + k, it * 16 + h * T // MADE * 16)
            norm(1)
            for g in range(G):
                flipped_out(0, g)

            def lorentz_squares(tag, first, g):
                act.wait_ge(sem(f"lin_{tag}"), g + 1)
                z = z_of(first, g)
                if tag == "k":
                    act.wait_ge(sem("point_summed"), G + g + 1)
                nc.scalar.activation(grp(sqr, g)[:, :, 0:D - 1], z[:, :, 1:D], ACT.Square).then_inc(sem("point_sq"), 1)
                nc.scalar.activation(grp(tm[tag], g), z[:, :, 0], ACT.Exp, scale=-1.0).then_inc(sem("point_exp"), 1)

            def lorentz_root(tag):
                power_of("point_root", st[4], st[3], 0.5, "point_ratio", BEFORE[tag])
            for g in range(G):
                lorentz_squares("h", 4, g)
            lorentz_root("h")
            for g in range(G):
                flipped_out(1, g)
            for g in range(G):
                lorentz_squares("q", 4, g)
            lorentz_squares("k", 0, 0)
            lorentz_root("q")
            lorentz_squares("k", 0, 1)
            def folded_out(name, dst, g, bank, ready):
                one(name, dst[:, g * HALF:(g + 1) * HALF], banks(bank, bank + 2).bitcast(F16), ACT.Copy, (ready, g + 1))
            for tag, src, dst in (("q", HBq, Q2), ("k", HBk, K2)):
                for g in range(G):
                    one(f"{tag}_high", grp(dst, g)[:, :, 0, :], grp(src, g), ACT.Copy, (f"{tag}_point", g + 1))
                if tag == "q":
                    lorentz_root("k")
                    for g in range(G):
                        folded_out("qhh_out", q_hh, g, 4 + 2 * g, "qhh_ready")

            folded_out("khl_out_a", k_hl, 0, 0, "khl_ready")

            act.wait_ge(sem("att_scale_ready"), 1)

            def sigm(u, n, first):
                act.wait_ge(sem("scores_ready"), n + 1)
                if not first:
                    act.wait_ge(sem("prob_ready"), n - 1)
                b = 4 + 2 * (u % 2)
                nc.scalar.activation(att[:, u % 2, :], PS[:, b * BANK:(b + 2) * BANK], ACT.Sigmoid,
                                     bias=att_sc[:, 2:3], scale=att_sc[:, 1:2]).then_inc(sem("att_ready"), 1)
            for u in range(4):
                sigm(u, u, u < 2)
            with act.Fori(1, T) as it:
                for u in range(4):
                    sigm(u, it * 4 + u, False)
            one("sums_out1_a", TA[:, 0:UNIT], PS[:, 0:UNIT], ACT.Copy, ("agg1_done", 4 * T - 2))
            for g in range(G):
                one("sup_sq", grp(sqr, g), z_of(4, g), ACT.Square, ("support_ready", g + 1))
            nc.scalar.preload_act_table_set("natural_log_exp_and_others")
            power_of("sup_root", st[2], st[1], -0.5, "sup_inner")
            norm(2)

            for g in range(G):
                one("y_sq", grp(sqr, g), grp(Y, g)[:, :, 0:D], ACT.Square, ("feats2_ready", g + 1))
            one("zl_out_a", TA[0:ROWS, 0:HALF], PS[0:ROWS, 0:HALF], ACT.Copy, ("zl_flipped", 1))
            one("kap_ready_a", kap_l[0:ROWS, 0:HALF], TA[0:ROWS, 0:HALF], ACT.Copy, ("zl_out_a", 1))
            one("zr_out_a", TB[0:ROWS, 0:HALF], PS[0:ROWS, 0:HALF], ACT.Copy, ("zr_flipped", 1))

            def step2(Q, j):
                u = unit(Q, j, 3)
                if u:
                    k = u[2] % ROT
                    act.wait_ge(sem("sum_ready"), count(u))
                    nc.scalar.activation(sum_[:, k, :], sum_[:, k, :], ACT.Ln, scale=st[5][:, u1(u)])\
                      .then_inc(sem("tau_ready"), 1)
                if (Q, j) == (4, 4):
                    for b in range(3):
                        nodes2_out(0, b)
                    nodes2_out(1, 0)
                u = unit(Q, j, 5)
                if u and isinstance(u[1], int) and u[1] == T - 1:
                    act.wait_ge(sem("agg2_done"), count(u))
                    nc.scalar.activation(TB[0:D + 1, u[0] * QUART:(u[0] + 1) * QUART], PS[0:D + 1, 0:QUART], ACT.Copy)\
                      .then_inc(sem("quarter_out"), 1)
                u = unit(Q, j, 1)
                if u:
                    k = u[2] % ROT
                    act.wait_ge(sem("rest_ready"), count(u))
                    if prior(u, ROT) is not None:
                        act.wait_ge(sem("rad_ready"), prior(u, ROT))
                        act.wait_ge(sem("root_ready"), prior(u, ROT))
                    nc.scalar.activation(rin[:, k, :], sqz[:, k, :], ACT.Ln).then_inc(sem("lnr_ready"), 1)
                u = unit(Q, j, 0)
                if u:
                    k = u[2] % ROT
                    act.wait_ge(sem("z_ready"), count(u))
                    if prior(u, ROT) is not None:
                        act.wait_ge(sem("root_ready"), prior(u, ROT))
                        act.wait_ge(sem("root_ready_p"), prior(u, ROT))
                    nc.scalar.activation(sqz[:, k, :], PS[:, (2 + 2 * k) * BANK:(4 + 2 * k) * BANK], ACT.Square)\
                      .then_inc(sem("sqz_ready"), 1)
                u = unit(Q, j, 1)
                if u:
                    k = u[2] % ROT
                    act.wait_ge(sem("lnr_ready"), count(u))
                    nc.scalar.activation(rin[:, k, :], rin[:, k, :], ACT.Exp, scale=-0.5).then_inc(sem("rin_ready"), 1)
            nc.scalar.activation(kap_r[0:ROWS, 0:HALF], TA[0:ROWS, 0:HALF], ACT.Copy, scale=kmask[0:ROWS, 0:1])\
              .then_inc(sem("kap_ready_a"), 1)
            act.wait_ge(sem("stats2_ready"), G)
            def nodes2_out(g, b):
                n = min(7, TG - 7 * b)
                t = g * TG + 7 * b
                one("agg2_copied", Gn[:, t:t + n, :],
                    PS[:, agg2_col(t):agg2_col(t) + n * (D + 1)].rearrange("p (t c) -> p t c", t=n),
                    ACT.Copy, ("agg2_nodes", 1 if g == 0 else 2 if b == 0 else 3))

            walk2(act, step2)
            for b in (1, 2):
                nodes2_out(1, b)
            for g in range(G):
                flipped_out(2, g)
            for g in range(G):
                one("v_sq", grp(sqr, g), z_of(4, g), ACT.Square, ("lin_w2", g + 1))
            power_of("v_root", st[2], st[1], -0.5, "v_norm2")
            for g in range(G):
                one("v_tanh", grp(st[4], g), grp(st[3], g), ACT.Tanh, ("v_norm", g + 1))
            nc.scalar.preload_act_table_set("natural_log_exp_and_others")
            norm(3)

            for g in range(G):
                flipped_out(3, g)
            def power(s, k, slot, loaded, first):
                act.wait_ge(sem(f"adj_loaded{slot}"), loaded)
                if not first:
                    act.wait_ge(sem("agg3_done"), s - 3)
                nc.scalar.activation(pw[:, k, 0:UNIT].bitcast(I16), code[:, slot, 0:UNIT], ACT.Copy, scale=BF_STEP)\
                  .then_inc(sem("pw_ready_a"), 1)
            for k in (0, 1):
                power(k, k, k, LOADS2(k) + 16, True)
            for g in range(G):
                one("part_a", grp(S3, g)[:, :, 0, :], z_of(4, g), ACT.Copy, ("lin_w3", g + 1), scale=W_SCALE)
            for g in range(G):
                one("part_b", grp(S3, g)[:, :, 1, :], grp(cen, g), ACT.Copy, ("rest_a", g + 1))
            for k in (2, 3):
                power(k, k, k, LOADS2(k) + 16, True)

            for h in range(2):
                for k in range(0 if h else 4, CODES):
                    power(h * T + k, k % 4, k, LOADS2(k) + 16 * (h * T // CODES + 1), False)
                    if h and k == 3:
                        one("sums_out3_a", TA[:, 0:UNIT], PS[:, 4 * BANK:6 * BANK], ACT.Copy, ("agg3_done", T))
                with act.Fori(1, T // CODES) as it:
                    for k in range(CODES):
                        power(it * CODES + (h * T + k), k % 4, k, it * 16 + (LOADS2(k) + 16 * (h * T // CODES + 1)), False)

        @block.vector
        def _(dve):
            V = nc.vector
            chain = [0]

            def link(ins):
                chain[0] += 1
                ins.then_inc(sem("dve_chain"), 1)
                dve.wait_ge(sem("dve_chain"), chain[0])

            last = [0] * G

            def hold(g):
                dve.wait_ge(sem("dve_chain"), last[g])

            def chained(g, ins):
                chain[0] += 1
                last[g] = chain[0]
                ins.then_inc(sem("dve_chain"), 1)

            def rsqrt(name, v, root, before=0, groups=range(G)):
                for g in groups:
                    dve.wait_ge(sem(name), before + g + 1)
                    chained(g, V.tensor_tensor(grp(st[9], g), grp(root, g), grp(root, g), ALU.mult))
                for g in groups:
                    hold(g)
                    chained(g, V.tensor_tensor(grp(st[9], g), grp(st[9], g), grp(v, g), ALU.mult))
                for g in groups:
                    hold(g)
                    chained(g, V.tensor_scalar(grp(st[9], g), grp(st[9], g), -0.5, 1.5, ALU.mult, ALU.add))
                for g in groups:
                    hold(g)
                    chained(g, V.tensor_tensor(grp(root, g), grp(root, g), grp(st[9], g), ALU.mult))

            def norm(L, done, dst=H):
                norm_stats(L, range(G))
                for g in range(G):
                    norm_out(g, done, dst)

            def norm_out(g, done, dst=H):
                hold(g)
                V.scalar_tensor_tensor(grp(dst, g)[:, :, 0:D], grp(cen, g), 0.0, over_c(st[2], g), ALU.max, ALU.mult)\
                 .then_inc(sem(done), 1)

            def norm_stats(L, groups):
                for g in groups:
                    if L == 0:
                        dve.wait_ge(sem(f"x_loaded{g}"), 16)
                    if L >= 2 and g == 1:
                        dve.wait_ge(sem("x1_added"), L - 1)
                    else:
                        hold(g)
                    chained(g, V.reduce_sum(grp(st[0], g), grp(X, g), AX.X))
                for g in groups:
                    hold(g)
                    chained(g, V.tensor_scalar(grp(st[0], g), grp(st[0], g), -1.0 / D, None, ALU.mult))
                for g in groups:
                    hold(g)
                    V.tensor_tensor(grp(cen, g), grp(X, g), over_c(st[0], g), ALU.add).then_inc(sem("ln_centred"), 1)
                for g in groups:
                    dve.wait_ge(sem("ln_sq"), L * G + g + 1)
                    chained(g, V.reduce_sum(grp(st[1], g), grp(sqr, g), AX.X))
                for g in groups:
                    hold(g)
                    V.tensor_scalar(grp(st[1], g), grp(st[1], g), 1.0 / D, EPS, ALU.mult, ALU.add)\
                     .then_inc(sem("ln_var"), 1)
                rsqrt("ln_sd", st[1], st[2], L * G, groups)

            def copy_out(name, dst, src, ready):
                dve.wait_ge(sem(ready[0]), ready[1])
                V.tensor_copy(dst, src).then_inc(sem(name), 1)

            norm(0, "feats0_ready")

            def update0(g):
                dve.wait_ge(sem("z0_ready"), g + 1)
                chained(g, V.scalar_tensor_tensor(grp(X, g), z_of(0, g), 0.0, grp(X, g), ALU.max, ALU.add))

            dve.wait_ge(sem("consts_ready"), 7)

            def tile0(h, s, k, loaded, first):
                dve.wait_ge(sem(f"adj_loaded{k}"), loaded)
                if not first:
                    dve.wait_ge(sem("counts_ready"), s * 2 - 4)
                V.tensor_scalar(mask[:, k % 4, :], ring0(k), 0.0, None, ALU.not_equal).then_inc(sem("mask_ready"), 1)
                if not (isinstance(s, int) and s == 0):
                    dve.wait_ge(sem("deg_added"), s)
                V.tensor_tensor(TB[:, h * HALF:(h + 1) * HALF], TB[:, h * HALF:(h + 1) * HALF], ring0(k), ALU.add)\
                 .then_inc(sem("deg_added"), 1)
            for h in range(2):
                for k in range(RING0):
                    tile0(h, h * T + k, k, (h * T // RING0 + 1) * 16, h == 0 and k < 4)
                if h:
                    update0(0)
                    dve.wait_ge(sem("scales_ready"), 1)
                    link(V.tensor_scalar(top[:, :], esc[:, :], 1.1, 1.0 / HALVES_TOP, ALU.add, ALU.mult))
                    link(V.reciprocal(inv_top[:, :], top[:, :]))
                    link(V.tensor_scalar(half_top[:, :], inv_top[:, :], 0.5, None, ALU.mult))
                with dve.Fori(1, T // RING0) as it:
                    for k in range(RING0):
                        tile0(h, it * RING0 + (h * T + k), k, it * 16 + (h * T // RING0 + 1) * 16, False)
            copy_out("sums_out0_v", TA[:, UNIT:2 * UNIT], PS[:, UNIT:2 * UNIT], ("agg0_done", 2 * T))
            update0(1)

            norm_stats(1, range(G))
            dve.wait_ge(sem("staged0"), 2 * T)
            for g in range(G):
                norm_out(g, "feats_ready_l1")
            dve.wait_ge(sem("deg_summed"), 1)
            V.tensor_scalar(deg[:, :], PS[:, 7 * BANK:7 * BANK + T], 1e-8, None, ALU.max).then_inc(sem("deg_out"), 1)

            def lorentz_ratio(tag, scale, ssum, ssq):
                for g in range(G):
                    dve.wait_ge(sem("point_sq"), BEFORE[tag] + g + 1)
                    V.reduce_sum(grp(ssum, g), grp(sqr, g)[:, :, 0:D - 1], AX.X).then_inc(sem("point_summed"), 1)
                for g in range(G):
                    dve.wait_ge(sem("point_exp"), BEFORE[tag] + g + 1)
                    chained(g, V.tensor_scalar(grp(tm[tag], g), grp(tm[tag], g), 1e30, 1.0, ALU.min, ALU.add))
                for g in range(G):
                    hold(g)
                    chained(g, V.reciprocal(grp(tm[tag], g), grp(tm[tag], g)))
                for g in range(G):
                    hold(g)
                    chained(g, V.tensor_scalar(grp(tm[tag], g), grp(tm[tag], g), scale, 1.1, ALU.mult, ALU.add))
                for g in range(G):
                    dve.wait_ge(sem("point_summed"), BEFORE[tag] + g + 1)
                    chained(g, V.tensor_scalar(grp(ssum, g), grp(ssum, g), 1e-8, None, ALU.max))
                for g in range(G):
                    hold(g)
                    chained(g, V.reciprocal(grp(ssum, g), grp(ssum, g)))
                for g in range(G):
                    chained(g, V.tensor_tensor(grp(ssq, g), grp(tm[tag], g), grp(tm[tag], g), ALU.mult))
                for g in range(G):
                    hold(g)
                    V.scalar_tensor_tensor(grp(st[3], g), grp(ssq, g), -1.0, grp(ssum, g), ALU.add, ALU.mult)\
                     .then_inc(sem("point_ratio"), 1)

            def lorentz_point(tag, first, dst, half, time_factor, done):
                for g in range(G):
                    dve.wait_ge(sem("point_root"), BEFORE[tag] + g + 1)
                    chained(g, V.reciprocal(grp(st[6], g), grp(st[4], g)))
                for g in range(G):
                    hold(g)
                    chained(g, V.tensor_tensor(grp(st[6], g), grp(st[6], g), grp(st[3], g), ALU.mult))
                for g in range(G):
                    hold(g)
                    chained(g, V.tensor_tensor(grp(st[6], g), grp(st[6], g), grp(st[4], g), ALU.add))
                for g in range(G):
                    hold(g)
                    chained(g, V.scalar_tensor_tensor(grp(dst, g), z_of(first, g), half, over_c(st[6], g), ALU.mult, ALU.mult))
                for g in range(G):
                    hold(g)
                    if time_factor is None:
                        V.tensor_copy(grp(dst, g)[:, :, 0], grp(tm[tag], g)).then_inc(sem(done), 1)
                    else:
                        V.tensor_scalar(grp(dst, g)[:, :, 0], grp(tm[tag], g), *time_factor).then_inc(sem(done), 1)

            lorentz_ratio("h", esc[:, 0:1], st[1], st[2])
            lorentz_point("h", 4, HL, 0.5, None, "feats1_ready")
            lorentz_ratio("q", esc[:, 1:2], st[1], st[2])
            for k in range(MADE):
                dve.wait_ge(sem(f"codes_stored{k}"), 2 * T // MADE * 16)
            lorentz_point("q", 4, HBq, half_top[:, 1:2], (inv_top[:, 1:2], -1.0, ALU.mult, ALU.mult), "q_point")
            lorentz_ratio("k", esc[:, 2:3], st[7], st[8])

            lorentz_point("k", 0, HBk, half_top[:, 2:3], (inv_top[:, 2:3], None, ALU.mult), "k_point")
            for g in range(G):
                dve.wait_ge(sem("k_high"), g + 1)
                V.tensor_tensor(grp(K2, g)[:, :, 1, :], grp(HBk, g), grp(K2, g)[:, :, 0, :], ALU.subtract)\
                 .then_inc(sem("k_low"), 1)
            link(V.reciprocal(att_sc[:, 0:1], scal[:, 4:5]))
            link(V.tensor_scalar(att_sc[:, 0:1], att_sc[:, 0:1], 2.0, None, ALU.mult))
            link(V.tensor_scalar(att_sc[:, 1:2], att_sc[:, 0:1], top[:, 1:2], top[:, 2:3], ALU.mult, ALU.mult))
            V.tensor_scalar(att_sc[:, 2:3], att_sc[:, 0:1], scal[:, 3:4], None, ALU.add).then_inc(sem("att_scale_ready"), 1)
            for g in range(G):
                copy_out("qll_out", q_ll[:, g * HALF:(g + 1) * HALF], banks(4 + 2 * g, 6 + 2 * g).bitcast(F16),
                         ("qll_ready", g + 1))

            copy_out("khl_out_v", k_hl[:, HALF:N], banks(2, 4).bitcast(F16), ("khl_ready", 2))

            def product(u, n, s, loaded, first):
                dve.wait_ge(sem("att_ready"), n + 1)
                dve.wait_ge(sem(f"adj_loaded{s}"), loaded)
                if not first:
                    dve.wait_ge(sem("agg1_done"), n - 3)
                V.tensor_tensor(prob[:, u, :], att[:, u % 2, :], ring[:, s, (u % 2) * UNIT:(u % 2 + 1) * UNIT], ALU.mult)\
                 .then_inc(sem("prob_ready"), 1)

            def turn1(it, loaded, peeled):
                for k in range(2):
                    for u in range(4):
                        product(u, it * 8 + (4 * k + u), 2 * k + u // 2, loaded, peeled and k == 0)
            turn1(0, LOADS0 + 16, True)
            with dve.Fori(1, T // 2) as it:
                turn1(it, it * 16 + (LOADS0 + 16), False)
            copy_out("sums_out1_v", TA[:, UNIT:2 * UNIT], PS[:, UNIT:2 * UNIT], ("agg1_done", 4 * T))
            for g in range(G):
                dve.wait_ge(sem("sup_sq"), g + 1)
                chained(g, V.reduce_sum(grp(st[0], g), grp(sqr, g)[:, :, 1:D], AX.X))
            for g in range(G):
                hold(g)
                chained(g, V.tensor_tensor(grp(st[1], g), grp(st[0], g), grp(sqr, g)[:, :, 0], ALU.subtract))
            for g in range(G):
                hold(g)
                chained(g, V.scalar_tensor_tensor(grp(st[2], g), grp(st[1], g), -1.0, grp(st[1], g), ALU.mult, ALU.max))
            for g in range(G):
                hold(g)
                V.tensor_scalar(grp(st[1], g), grp(st[2], g), 1e-8, None, ALU.max).then_inc(sem("sup_inner"), 1)
            rsqrt("sup_root", st[1], st[2])
            for g in range(G):
                hold(g)
                V.tensor_tensor(grp(cen, g), z_of(4, g), over_c(st[2], g), ALU.mult).then_inc(sem("support_used"), 1)
            dve.wait_ge(sem("support_used"), 1)
            chained(0, V.tensor_tensor(grp(X, 0), grp(X, 0), grp(cen, 0), ALU.add))

            norm(2, "feats2_ready", Y)
            ysq, ball, iball, sgn, nball2 = (st[k] for k in (3, 4, 5, 6, 7))
            V.memset(zi[:, :, D + 1:ROWS], 0.0).then_inc(sem("zi_zeroed"), 1)
            V.memset(Y[:, :, D + 1], 1.0).then_inc(sem("y_ones"), 1)
            for g in range(G):
                dve.wait_ge(sem("y_sq"), g + 1)
                chained(g, V.reduce_sum(grp(ysq, g), grp(sqr, g), AX.X))
            for g in range(G):
                hold(g)
                chained(g, V.tensor_scalar(grp(ball, g), grp(ysq, g), -1.0, 1.0, ALU.mult, ALU.add))
            for g in range(G):
                hold(g)
                chained(g, V.tensor_scalar(grp(sgn, g), grp(ball, g), 0.0, 2.0, ALU.is_ge, ALU.mult))
            for g in range(G):
                hold(g)
                chained(g, V.tensor_scalar(grp(sgn, g), grp(sgn, g), -1.0, None, ALU.add))
            for g in range(G):
                V.tensor_scalar(grp(Y, g)[:, :, D], grp(ysq, g), 1.0, None, ALU.add).then_inc(sem("y_one_plus"), 1)
            for g in range(G):
                hold(g)
                dve.wait_ge(sem("y_one_plus"), g + 1)
                dve.wait_ge(sem("y_ones"), 1)
                V.tensor_copy(grp(Y, g)[:, :, D + 2], grp(sgn, g)).then_inc(sem("zl_nodes_ready"), 1)
            for g in range(G):
                chained(g, V.scalar_tensor_tensor(grp(iball, g), grp(ball, g), -1.0, grp(ball, g), ALU.mult, ALU.max))
            for g in range(G):
                hold(g)
                chained(g, V.tensor_scalar(grp(iball, g), grp(iball, g), BALL_FLOOR, None, ALU.max))
            for g in range(G):
                hold(g)
                chained(g, V.scalar_tensor_tensor(grp(nball2, g), grp(iball, g), -1.0, grp(iball, g), ALU.mult, ALU.mult))
            for g in range(G):
                hold(g)
                V.reciprocal(grp(iball, g), grp(iball, g)).then_inc(sem("stats2_ready"), 1)
            for g in range(G):
                dve.wait_ge(sem("stats2_ready"), g + 1)
                chained(g, V.scalar_tensor_tensor(grp(zi, g)[:, :, 0:D], grp(Y, g)[:, :, 0:D], -4.0, over_c(iball, g),
                                                  ALU.mult, ALU.mult))
                hold(g)
                dve.wait_ge(sem("zi_zeroed"), 1)
                V.tensor_tensor(grp(zi, g)[:, :, D], grp(Y, g)[:, :, D], grp(iball, g), ALU.mult)\
                 .then_inc(sem("zr_nodes_ready"), 1)
            copy_out("zl_out_v", TA[0:ROWS, HALF:N], PS[0:ROWS, HALF:N], ("zl_flipped", 2))
            dve.wait_ge(sem("zl_out_v"), 1)
            V.tensor_copy(kap_l[0:ROWS, HALF:N], TA[0:ROWS, HALF:N]).then_inc(sem("kap_ready_v"), 1)
            copy_out("zr_out_v", TB[0:ROWS, HALF:N], PS[0:ROWS, HALF:N], ("zr_flipped", 2))
            V.tensor_scalar(kap_r[0:ROWS, HALF:N], TA[0:ROWS, HALF:N], kmask[0:ROWS, 0:1], None, ALU.mult)\
             .then_inc(sem("kap_ready_v"), 1)

            def step2(Q, j):
                u = unit(Q, j, 0)
                if u:
                    k = u[2] % ROT
                    dve.wait_ge(sem("sqz_ready"), count(u))
                    V.tensor_scalar(sqz[:, k, :], sqz[:, k, :], st[7][:, u1(u)], ROOT_FLOOR, ALU.add, ALU.max)\
                     .then_inc(sem("rest_ready"), 1)
                u = unit(Q, j, 1)
                if u:
                    k = u[2] % ROT
                    dve.wait_ge(sem("rin_ready"), count(u))
                    if prior(u, ROT) is not None:
                        dve.wait_ge(sem("wgt_ready"), prior(u, ROT))
                    V.tensor_tensor(sum_[:, k, 0:ROOT_V], sqz[:, k, 0:ROOT_V], rin[:, k, 0:ROOT_V], ALU.mult)\
                     .then_inc(sem("root_ready"), 1)
                u = unit(Q, j, 3)
                if u:
                    k = u[2] % ROT
                    dve.wait_ge(sem("tau_ready"), count(u))
                    dve.wait_ge(sem("rad_ready"), count(u))
                    if prior(u, ROT) is not None:
                        dve.wait_ge(sem("agg2_done"), prior(u, ROT))
                    V.scalar_tensor_tensor(wgt[:, k, :], sum_[:, k, :], TAU_MAX, rad[:, k, :], ALU.min, ALU.mult)\
                     .then_inc(sem("wgt_ready"), 1)
                u = unit(Q, j, 1)
                if u:
                    k = u[2] % ROT
                    dve.wait_ge(sem("root_ready"), count(u))
                    dve.wait_ge(sem("root_ready_p"), count(u))
                    dve.wait_ge(sem("zk_ready"), count(u))
                    V.tensor_tensor(sum_[:, k, :], sum_[:, k, :], PS[:, (2 + 2 * k) * BANK:(4 + 2 * k) * BANK], ALU.add)\
                     .then_inc(sem("sum_ready"), 1)
            walk2(dve, step2)

            link(V.reciprocal(agg_y[:, :], deg[:, :]))
            link(V.tensor_tensor(agg_y[:, :], agg_y[:, :], iball[:, :], ALU.mult))
            link(V.tensor_scalar(agg_v[:, :], ball[:, :], MIN_NORM, None, ALU.max))
            link(V.tensor_tensor(agg_y[:, :], agg_y[:, :], agg_v[:, :], ALU.mult))
            V.tensor_tensor(agg_v[:, :], agg_y[:, :], ball[:, :], ALU.mult).then_inc(sem("agg_coef"), 1)
            for g in range(G):
                dve.wait_ge(sem("agg2_copied"), 3 * g + 3)
                link(V.tensor_tensor(grp(sqr, g), grp(Gn, g)[:, :, 0:D], grp(Y, g)[:, :, 0:D], ALU.mult))
                link(V.reduce_sum(grp(st[0], g), grp(sqr, g), AX.X))
                link(V.scalar_tensor_tensor(grp(st[0], g), grp(st[0], g), 2.0, grp(Gn, g)[:, :, D], ALU.mult, ALU.subtract))
                link(V.tensor_tensor(grp(st[0], g), grp(st[0], g), grp(agg_y, g), ALU.mult))
                link(V.tensor_tensor(grp(sqr, g), grp(Y, g)[:, :, 0:D], over_c(st[0], g), ALU.mult))
                dve.wait_ge(sem("ball_part"), g + 1)
                V.tensor_tensor(grp(cen, g), grp(cen, g), grp(sqr, g), ALU.add).then_inc(sem("tan_ready"), 1)
            for g in range(G):
                dve.wait_ge(sem("v_sq"), g + 1)
                chained(g, V.reduce_sum(grp(st[0], g), grp(sqr, g), AX.X))
            for g in range(G):
                hold(g)
                V.tensor_scalar(grp(st[1], g), grp(st[0], g), NORM2_FLOOR, None, ALU.max).then_inc(sem("v_norm2"), 1)
            rsqrt("v_root", st[1], st[2])
            for g in range(G):
                hold(g)
                V.tensor_tensor(grp(st[3], g), grp(st[1], g), grp(st[2], g), ALU.mult).then_inc(sem("v_norm"), 1)
            for g in range(G):
                dve.wait_ge(sem("v_tanh"), g + 1)
                chained(g, V.tensor_tensor(grp(st[2], g), grp(st[2], g), grp(st[4], g), ALU.mult))
            for g in range(G):
                hold(g)
                V.tensor_tensor(grp(cen, g), z_of(4, g), over_c(st[2], g), ALU.mult).then_inc(sem("v_used"), 1)
            dve.wait_ge(sem("v_used"), 1)
            chained(0, V.tensor_tensor(grp(X, 0), grp(X, 0), grp(cen, 0), ALU.add))

            norm(3, "feats_ready_l3")

            def power(s, k, slot, loaded, first):
                dve.wait_ge(sem(f"adj_loaded{slot}"), loaded)
                if not first:
                    dve.wait_ge(sem("agg3_done"), s - 3)
                V.tensor_scalar(pw[:, k, UNIT:2 * UNIT].bitcast(I16), code[:, slot, UNIT:2 * UNIT], BF_STEP, None, ALU.mult)\
                 .then_inc(sem("pw_ready_v"), 1)
            for k in range(4):
                power(k, k, k, LOADS2(k) + 16, True)
            for g in range(G):
                dve.wait_ge(sem("part_a"), g + 1)
                V.scalar_tensor_tensor(grp(cen, g), z_of(4, g), W_SCALE, grp(S3, g)[:, :, 0, :], ALU.mult, ALU.subtract)\
                 .then_inc(sem("rest_a"), 1)
            for g in range(G):
                dve.wait_ge(sem("part_b"), g + 1)
                V.tensor_tensor(grp(S3, g)[:, :, 2, :], grp(cen, g), grp(S3, g)[:, :, 1, :], ALU.subtract)\
                 .then_inc(sem("parts3_ready"), 1)

            def result(g):
                dve.wait_ge(sem("agg3_nodes"), g + 1)
                dve.wait_ge(sem("bias3_added"), g + 1)
                V.tensor_tensor(grp(X, g), grp(X, g), z_of(0, g), ALU.add).then_inc(sem("result_ready"), 1)

            for h in range(2):
                for k in range(0 if h else 4, CODES):
                    power(h * T + k, k % 4, k, LOADS2(k) + 16 * (h * T // CODES + 1), False)
                if h:
                    result(0)
                with dve.Fori(1, T // CODES) as it:
                    for k in range(CODES):
                        power(it * CODES + (h * T + k), k % 4, k, it * 16 + (LOADS2(k) + 16 * (h * T // CODES + 1)), False)
            copy_out("sums_out3_v", TA[:, UNIT:2 * UNIT], PS[:, 6 * BANK:8 * BANK], ("agg3_done", 2 * T))
            result(1)


ROOT_FLOOR = 1e-12
NORM2_FLOOR = 1e-30


def kernel(**inputs):
    import numpy as _np
    import concourse.bacc as _bacc
    from concourse.bass_utils import run_bass_kernel_spmd as _run

    a = {k: _np.asarray(v) for k, v in inputs.items()}
    scalars = _np.stack([a["L1_gnn_scale"], a["L1_gnn_scale_q"], a["L1_gnn_scale_k"],
                         a["L1_gnn_att_bias"], a["L1_gnn_att_scale"]]).reshape(5)
    given = {
        "x": a["x"], "adj_t": a["adj"].T,
        "w0_t": a["L0_gnn_W"].T, "b0": a["L0_gnn_b"],
        "w1_t": a["L1_gnn_W"].T, "b1": a["L1_gnn_b"],
        "wq_t": a["L1_gnn_Wq"].T, "bq": a["L1_gnn_bq"],
        "wk_t": a["L1_gnn_Wk"].T, "bk": a["L1_gnn_bk"],
        "scalars": scalars,
        "w2": a["L2_gnn_weight"], "b2": a["L2_gnn_bias"],
        "w3": a["L3_gnn_weight"], "b3": a["L3_gnn_bias"],
    }
    nc = _bacc.Bacc("TRN2", target_bir_lowering=False, num_devices=1)
    arrays, args = {}, []
    for name, v in given.items():
        v = _np.ascontiguousarray(v)
        arrays[f"in_{name}"] = v
        args.append(nc.dram_tensor(f"in_{name}", v.shape, mybir.dt.from_np(v.dtype), kind="ExternalInput").ap())
    args.insert(2, nc.dram_tensor("codes", (N, N), U8, kind="Internal").ap())
    args.append(nc.dram_tensor("out_x", (N, D), F32, kind="ExternalOutput").ap())
    graph_layers(nc, *args)
    r = _run(nc, [arrays], core_ids=[0])
    return r.results[0]["out_x"]
```
